# Optimizing a Trainium2 kernel written in Bass

```python
import numpy as np
import jax
import jax.numpy as jnp

def _softmax(x, axis=-1):
    return jax.nn.softmax(x, axis=axis)

def _gelu(x):
    return jax.nn.gelu(x, approximate=True)

def _silu(x):
    return jax.nn.silu(x)

def _sigmoid(x):
    return jax.nn.sigmoid(x)

def _layernorm(x, axis=-1, eps=1e-05):
    m = jnp.mean(x, axis=axis, keepdims=True)
    v = jnp.var(x, axis=axis, keepdims=True)
    return (x - m) / jnp.sqrt(v + eps)

def _scatter_add(tgt, idx, src, axis=0):
    return tgt.at[idx].add(src)

def _segment_sum(src, seg, n):
    return jax.ops.segment_sum(src, seg, n)
kernel_name = 'mk_macaron_d1_jaxref_r8_ae27de'

def setup_inputs(seed: int=0):
    np.random.seed(seed)
    _w = jnp.asarray

    def _L0_attn_setup():
        import math
        import jax, jax.numpy as jnp
        import numpy as np
        NUM_HEADS = 32
        HIDDEN = 512
        HEAD_DIM = HIDDEN // NUM_HEADS
        NEG_INF = -1e+30

        def _alibi_slopes(n: int) -> jnp.ndarray:
            cp2 = 2 ** math.floor(math.log2(n))
            base = 2.0 ** (-2.0 ** (-(math.log2(cp2) - 3)))
            slopes = base ** np.arange(1, cp2 + 1, dtype=np.float64)
            if cp2 != n:
                extra_base = 2.0 ** (-2.0 ** (-(math.log2(2 * cp2) - 3)))
                rem = min(cp2, n - cp2)
                extra = extra_base ** np.arange(1, 1 + 2 * rem, 2, dtype=np.float64)
                slopes = np.concatenate([slopes, extra])
            return jnp.asarray(slopes, dtype=jnp.float32)
        key = jax.random.key(seed)
        k1, k2, k3 = jax.random.split(key, 3)
        B, S = (2, 256)
        hidden_states = jax.random.normal(k1, (B, S, HIDDEN), dtype=jnp.float32)
        Wqkv = jax.random.normal(k2, (HIDDEN, NUM_HEADS * HEAD_DIM + 2 * HEAD_DIM), dtype=jnp.float32) * 0.02
        Wo = jax.random.normal(k3, (HIDDEN, HIDDEN), dtype=jnp.float32) * 0.02
        return {'hidden_states': hidden_states, 'Wqkv': Wqkv, 'Wo': Wo}
    _L0_attn_in = _L0_attn_setup()

    def _L0_ffn_setup():
        import jax, jax.numpy as jnp
        import numpy as np
        DIM = 512
        INTER = 128
        E = 16
        GROUPS = 4
        LIM = 2
        K = 2
        SHARED_INTER = 2 * INTER
        SCALE = 1.0
        key = jax.random.key(seed)
        ks = jax.random.split(key, 16)

        def n(k, shape, s=0.02):
            return jax.random.normal(k, shape, jnp.float32) * s
        return {'x': jax.random.normal(ks[0], (1, 256, DIM), jnp.float32), 'router_w': n(ks[1], (DIM, E)), 'router_b': n(ks[2], (E,)), 'router_bias': n(ks[3], (E,), 1.0), 'ew1': n(ks[4], (E, DIM, INTER)), 'eb1': n(ks[5], (E, INTER)), 'ew2': n(ks[6], (E, DIM, INTER)), 'eb2': n(ks[7], (E, INTER)), 'ew3': n(ks[8], (E, INTER, DIM)), 'eb3': n(ks[9], (E, DIM)), 'sw1': n(ks[10], (DIM, SHARED_INTER)), 'sb1': n(ks[11], (SHARED_INTER,)), 'sw2': n(ks[12], (DIM, SHARED_INTER)), 'sb2': n(ks[13], (SHARED_INTER,)), 'sw3': n(ks[14], (SHARED_INTER, DIM)), 'sb3': n(ks[15], (DIM,))}
    _L0_ffn_in = _L0_ffn_setup()
    _d = {'L0_attn_hidden_states': _L0_attn_in['hidden_states'], 'L0_attn_Wqkv': _L0_attn_in['Wqkv'], 'L0_attn_Wo': _L0_attn_in['Wo'], 'L0_ffn_router_w': _L0_ffn_in['router_w'], 'L0_ffn_router_b': _L0_ffn_in['router_b'], 'L0_ffn_router_bias': _L0_ffn_in['router_bias'], 'L0_ffn_ew1': _L0_ffn_in['ew1'], 'L0_ffn_eb1': _L0_ffn_in['eb1'], 'L0_ffn_ew2': _L0_ffn_in['ew2'], 'L0_ffn_eb2': _L0_ffn_in['eb2'], 'L0_ffn_ew3': _L0_ffn_in['ew3'], 'L0_ffn_eb3': _L0_ffn_in['eb3'], 'L0_ffn_sw1': _L0_ffn_in['sw1'], 'L0_ffn_sb1': _L0_ffn_in['sb1'], 'L0_ffn_sw2': _L0_ffn_in['sw2'], 'L0_ffn_sb2': _L0_ffn_in['sb2'], 'L0_ffn_sw3': _L0_ffn_in['sw3'], 'L0_ffn_sb3': _L0_ffn_in['sb3']}
    _x0 = _d['L0_attn_hidden_states']
    _d['L0_attn_hidden_states'] = jax.random.normal(jax.random.fold_in(jax.random.key(seed), 1), (4, 256, 512), dtype=_x0.dtype)
    del _x0
    return _d

def reference(L0_attn_hidden_states, L0_attn_Wqkv, L0_attn_Wo, L0_ffn_router_w, L0_ffn_router_b, L0_ffn_router_bias, L0_ffn_ew1, L0_ffn_eb1, L0_ffn_ew2, L0_ffn_eb2, L0_ffn_ew3, L0_ffn_eb3, L0_ffn_sw1, L0_ffn_sb1, L0_ffn_sw2, L0_ffn_sb2, L0_ffn_sw3, L0_ffn_sb3):

    def _L0_attn_ref(hidden_states, Wqkv, Wo):
        import math
        import jax, jax.numpy as jnp
        import numpy as np
        NUM_HEADS = 32
        HIDDEN = 512
        HEAD_DIM = HIDDEN // NUM_HEADS
        NEG_INF = -1e+30

        def _alibi_slopes(n: int) -> jnp.ndarray:
            cp2 = 2 ** math.floor(math.log2(n))
            base = 2.0 ** (-2.0 ** (-(math.log2(cp2) - 3)))
            slopes = base ** np.arange(1, cp2 + 1, dtype=np.float64)
            if cp2 != n:
                extra_base = 2.0 ** (-2.0 ** (-(math.log2(2 * cp2) - 3)))
                rem = min(cp2, n - cp2)
                extra = extra_base ** np.arange(1, 1 + 2 * rem, 2, dtype=np.float64)
                slopes = np.concatenate([slopes, extra])
            return jnp.asarray(slopes, dtype=jnp.float32)
        B, S, H = hidden_states.shape
        nH, d = (NUM_HEADS, HEAD_DIM)
        scale = d ** (-0.5)
        qkv = hidden_states @ Wqkv
        q = qkv[..., :nH * d].reshape(B, S, nH, d)
        k = qkv[..., nH * d:nH * d + d]
        v = qkv[..., nH * d + d:]
        scores = jnp.einsum('bqhd,bkd->bhqk', q, k) * scale
        pos_q = jnp.arange(S)[:, None]
        pos_k = jnp.arange(S)[None, :]
        slopes = _alibi_slopes(nH)
        alibi = slopes[:, None, None] * (pos_k - pos_q).astype(jnp.float32)
        causal = pos_k <= pos_q
        scores = jnp.where(causal[None, None], scores + alibi[None], NEG_INF)
        probs = jax.nn.softmax(scores, axis=-1)
        attn = jnp.einsum('bhqk,bkd->bqhd', probs, v).reshape(B, S, H)
        return attn @ Wo

    def _L0_ffn_ref(x, router_w, router_b, router_bias, ew1, eb1, ew2, eb2, ew3, eb3, sw1, sb1, sw2, sb2, sw3, sb3):
        import jax, jax.numpy as jnp
        import numpy as np
        DIM = 512
        INTER = 128
        E = 16
        GROUPS = 4
        LIM = 2
        K = 2
        SHARED_INTER = 2 * INTER
        SCALE = 1.0
        shape = x.shape
        xt = x.reshape(-1, DIM)
        T = xt.shape[0]
        logits = xt @ router_w + router_b
        scores = jax.nn.softmax(logits.astype(jnp.float32), axis=-1) + router_bias
        g = scores.reshape(T, GROUPS, E // GROUPS)
        _, gidx = jax.lax.top_k(g.max(axis=-1), LIM)
        keep = jnp.zeros((T, GROUPS), bool).at[jnp.arange(T)[:, None], gidx].set(True)
        masked = jnp.where(keep[:, :, None], g, -jnp.inf).reshape(T, E)
        _, idx = jax.lax.top_k(masked, K)
        vals = (jnp.take_along_axis(scores, idx, axis=1) * SCALE).astype(x.dtype)
        gate = jnp.zeros((T, E), x.dtype).at[jnp.arange(T)[:, None], idx].add(vals)

        def step(y, p):
            w1, b1, w2, b2, w3, b3, ge = p
            h = jax.nn.silu(xt @ w1 + b1) * (xt @ w2 + b2)
            return (y + ge[:, None] * (h @ w3 + b3), None)
        y, _ = jax.lax.scan(step, jnp.zeros_like(xt), (ew1, eb1, ew2, eb2, ew3, eb3, gate.T))
        z = jax.nn.silu(xt @ sw1 + sb1) * (xt @ sw2 + sb2) @ sw3 + sb3
        return (y + z).reshape(shape)
    x = L0_attn_hidden_states
    x = x + 0.5 * _L0_ffn_ref(_layernorm(x, axis=-1), L0_ffn_router_w, L0_ffn_router_b, L0_ffn_router_bias, L0_ffn_ew1, L0_ffn_eb1, L0_ffn_ew2, L0_ffn_eb2, L0_ffn_ew3, L0_ffn_eb3, L0_ffn_sw1, L0_ffn_sb1, L0_ffn_sw2, L0_ffn_sb2, L0_ffn_sw3, L0_ffn_sb3)
    x = x + _L0_attn_ref(_layernorm(x, axis=-1), L0_attn_Wqkv, L0_attn_Wo)
    x = x + 0.5 * _L0_ffn_ref(_layernorm(x, axis=-1), L0_ffn_router_w, L0_ffn_router_b, L0_ffn_router_bias, L0_ffn_ew1, L0_ffn_eb1, L0_ffn_ew2, L0_ffn_eb2, L0_ffn_ew3, L0_ffn_eb3, L0_ffn_sw1, L0_ffn_sb1, L0_ffn_sw2, L0_ffn_sb2, L0_ffn_sw3, L0_ffn_sb3)
    return x

_drawn_inputs = setup_inputs


def setup_inputs(seed=0):
    import zlib

    import numpy as np

    out = dict(_drawn_inputs(seed))
    spreads = {}
    factors = {'L0_ffn_router_w': 8.0,
     'L0_ffn_router_b': 193.066,
     'L0_ffn_eb1': 8.0,
     'L0_ffn_eb2': 8.0,
     'L0_ffn_sb1': 33.816,
     'L0_ffn_sb2': 32.871,
     'L0_ffn_sb3': 2.842}
    for name, (base, spread) in spreads.items():
        noise = np.random.default_rng([zlib.crc32(name.encode()), seed]).standard_normal(out[name].shape)
        drawn = base * np.exp(spread * noise) if base else spread * noise
        out[name] = jnp.asarray(drawn.astype(out[name].dtype))
    for name, factor in factors.items():
        out[name] = (out[name] * factor).astype(out[name].dtype)
    return out
```

```python
from contextlib import ExitStack

import numpy as np

import concourse.bass as bass
from concourse import mybir
from concourse.alu_op_type import AluOpType as ALU

F32 = mybir.dt.float32
BF16 = mybir.dt.bfloat16
I32 = mybir.dt.int32
U32 = mybir.dt.uint32
ACT = mybir.ActivationFunctionType
AX_X = mybir.AxisListType.X
ds = bass.ds

P = 128
BATCH, SEQ, DIM = 4, 256, 512
TOKENS = BATCH * SEQ
NT = TOKENS // P
KC = DIM // P
E, GROUPS, INTER = 16, 4, 128
SHARED = 256
CHOICES = 2
JOBS = CHOICES * TOKENS // P + E - 1
JP = 32
HEADS, HD = 32, 16
QT = SEQ // P
NEG = -1e30
EPS = 1e-5

QPART = (0, 0, 0, 1, 1, 2)
KPART = (0, 1, 2, 0, 1, 0)
R_ALIBI = len(QPART) * HD
R_MAX = R_ALIBI + 6
ROWS = R_MAX + 3

C_ID, C_IOTA, C_PIDX, C_TILE, C_END = 0, 128, 256, 257, 273
B_UP, B_ONE, B_ID, B_MASK, B_END = 0, 128, 256, 384, 640


def bf16_parts(a):
    parts, rest = [], a.astype(np.float64)
    for _ in range(3):
        bits = rest.astype(np.float32).view(np.uint32)
        bits = (bits + 0x7FFF + ((bits >> 16) & 1)) & np.uint32(0xFFFF0000)
        part = bits.astype(np.uint32).view(np.float32)
        parts.append(part)
        rest = rest - part
    return np.stack(parts)


def shape_constants():
    i = np.arange(P)
    const_f = np.zeros((P, C_END), np.float32)
    const_f[:, C_ID:C_ID + P] = np.eye(P)
    const_f[:, C_IOTA:C_IOTA + P] = i[None, :]
    const_f[:, C_PIDX] = i
    const_f[:, C_TILE:C_TILE + CHOICES * NT] = np.tile(np.arange(NT) * P, CHOICES)[None, :]
    const_b = np.zeros((P, B_END), np.float32)
    const_b[:, B_UP:B_UP + P] = i[:, None] < i[None, :]
    const_b[:, B_ONE:B_ONE + P] = 1.0
    const_b[:, B_ID:B_ID + P] = np.eye(P)
    later = np.where(i[None, :] <= i[:, None], 0.0, NEG)
    const_b[:, B_MASK:B_MASK + 2 * P] = np.concatenate([later, later.T], 1)
    slopes = (2.0 ** (-2.0 ** (-(np.log2(HEADS) - 3)))) ** np.arange(1, HEADS + 1, dtype=np.float64)
    slopes = slopes.astype(np.float32).astype(np.float64)
    pos = np.arange(SEQ, dtype=np.float64)
    rows_q = np.concatenate([
        np.broadcast_to(bf16_parts(slopes)[:, :, None], (3, HEADS, SEQ)),
        bf16_parts(-slopes[:, None] * pos[None, :])]).astype(np.float32)
    rows_k = np.concatenate([np.tile(pos, (3, 1)), np.ones((6, SEQ))]).astype(np.float32)
    return {"const_f": const_f, "const_b": const_b, "rows_q": np.ascontiguousarray(rows_q), "rows_k": rows_k}


def build(nc, x_in, wqkv_in, wo_in, rw_in, rb_in, rbias_in, ew1, eb1, ew2, eb2, ew3, eb3,
          sw1, sb1, sw2, sb2, sw3, sb3, const_f, const_b, rows_q, rows_k, out):
    with ExitStack() as ctx:
        def sb(name, shape, dt=F32):
            return ctx.enter_context(nc.sbuf_tensor(name, shape, dt))

        sems = {}

        def sem(name):
            if name not in sems:
                sems[name] = ctx.enter_context(nc.semaphore(name))
            return sems[name]

        xn_dram = nc.dram_tensor("xn_dram", (TOKENS, DIM), F32).ap()
        y_dram = nc.dram_tensor("y_dram", (JOBS * P, DIM), F32).ap()
        b12_dram = nc.dram_tensor("b12_dram", (3, E + 2, 2 * INTER), BF16).ap()
        q_dram = nc.dram_tensor("q_dram", (2, 3, DIM, SEQ), BF16).ap()
        k_dram = nc.dram_tensor("k_dram", (2, 3, HD, SEQ), BF16).ap()
        m_dram = nc.dram_tensor("m_dram", (2, 3, QT * HEADS, P), BF16).ap()

        x = sb("x", [P, NT, DIM])
        w12 = sb("w12", [P, E, KC, 2 * INTER])
        w3 = sb("w3", [P, E, DIM])
        sw12 = sb("sw12", [P, KC, 2 * SHARED])
        sw3s = sb("sw3s", [P, SHARED // P, DIM])
        wqkv = sb("wqkv", [P, KC, DIM + 2 * HD])
        wo = sb("wo", [P, KC, DIM])
        rw = sb("rw", [P, KC, E])
        cf = sb("cf", [P, C_END])
        cb = sb("cb", [P, B_END], BF16)
        b12x = sb("b12x", [3, (E + 2) * 2 * INTER], BF16)
        eb3x = sb("eb3x", [E + 1, DIM])
        rbc = sb("rbc", [P, 2, E])
        neghalf = sb("neghalf", [P, NT])
        st = sb("st", [P, NT, 6])
        mv = sb("mv", [P, NT, 2])
        varE = sb("varE", [P, NT])
        rstd = sb("rstd", [P, NT])
        ident = cf[:, C_ID:C_ID + P]
        iota = cf[:, C_IOTA:C_IOTA + P]
        upper = cb[:, B_UP:B_UP + P]
        ones = cb[:, B_ONE:B_ONE + P]
        identb = cb[:, B_ID:B_ID + P]
        mask = cb[:, None, B_MASK:B_MASK + P].to_broadcast([P, 2, P])
        mask_t = cb[:, None, B_MASK + P:B_MASK + 2 * P].to_broadcast([P, 2, P])

        WORDS = 13570
        arena = sb("arena", [P, WORDS])
        used = {"ffn": 0, "att": 0}

        def view(kind, shape, dt=F32, at=None):
            n = int(np.prod(shape[1:]))
            words = n if dt != BF16 else (n + 1) // 2
            if at is None:
                at = used[kind]
                used[kind] += words
                assert used[kind] <= WORDS, (kind, used[kind])
            v = arena[0:shape[0], at:at + words]
            if dt != F32:
                v = v.bitcast(dt)
            if len(shape) == 2:
                return v
            names = "abcd"[:len(shape) - 1]
            return v.rearrange(f"p ({' '.join(names)}) -> p {' '.join(names)}",
                               **{c: s for c, s in zip(names, shape[1:])})

        xn = view("ffn", [P, 2, DIM])
        used["att"] = used["ffn"]
        xnT = view("ffn", [P, NT, KC, P])
        xg = view("ffn", [P, 2, DIM])
        xgT = view("ffn", [P, 2, KC, P])
        sg = view("ffn", [P, 2, SHARED])
        hh = view("ffn", [P, 2, SHARED])
        hT = view("ffn", [P, 2, SHARED])
        ysb = view("ffn", [P, 2, DIM])
        yg_at = used["ffn"]
        yg = view("ffn", [P, 2, CHOICES, DIM])
        onehot_p = view("ffn", [P, CHOICES * NT, P], BF16, at=yg_at)
        onehot_j = view("ffn", [P, CHOICES * NT, 2, JP], BF16, at=yg_at + CHOICES * NT * P // 2)
        lg = view("ffn", [P, NT, E])
        sc = view("ffn", [P, NT, E])
        t16 = view("ffn", [P, NT, E])
        red = view("ffn", [P, NT])
        gm8 = view("ffn", [P, NT, 8])
        gtop = view("ffn", [P, NT, 8])
        gidx = view("ffn", [P, NT, 8], U32)
        etop = view("ffn", [P, NT, 8])
        eidx = view("ffn", [P, NT, 8], U32)
        idxf = view("ffn", [P, NT, 2])
        keep = view("ffn", [P, NT, GROUPS])
        keep2 = view("ffn", [P, NT, GROUPS])
        oh = view("ffn", [P, CHOICES, NT, E])
        taken = view("ffn", [P, NT, E], BF16)
        gate = view("ffn", [P, NT, E + 1])
        gateT = view("ffn", [E + 1, 2, P], at=yg_at)
        hv = view("ffn", [P, NT, CHOICES])
        cnt = view("ffn", [P, 4, E])
        cnti = view("ffn", [P, E], I32)
        slot = view("ffn", [P, CHOICES, NT])
        sloti = view("ffn", [P, CHOICES, NT], I32)
        slotu = view("ffn", [P, CHOICES, NT], U32)
        sji = view("ffn", [P, 2, CHOICES * NT], I32)
        sjf = view("ffn", [P, 2, CHOICES * NT])
        listf = view("ffn", [P, JP])
        listu = view("ffn", [P, JP], U32)
        jexf = view("ffn", [1, JP])
        jex = view("ffn", [1, JP], I32)
        jcmp = view("ffn", [1, JP, E], at=yg_at + CHOICES * NT * P // 2 + CHOICES * NT * JP)
        qside = view("att", [P, 2, HEADS, SEQ], BF16)
        kT = view("att", [P, 2, SEQ], BF16)
        xaT_at = used["att"]
        xaT = view("att", [P, KC, SEQ])
        pr_at = used["att"]
        pr = view("att", [P, 2, 3 * 2 * P])
        qp = view("att", [P, 3, KC, SEQ], BF16, at=pr_at)
        qr = view("att", [P, SEQ])
        kp = view("att", [HD, 3, SEQ], BF16)
        kr = qr[0:HD, :]
        vv = view("att", [P, 2, QT, HD + 1])
        rec = view("att", [P, 2, QT, 2])
        m3 = view("att", [P, HEADS, 3])
        nm = view("att", [P, QT, HEADS])
        mr = view("att", [QT * HEADS, P])
        mp = view("att", [QT * HEADS, 3, P], BF16)
        attn = xn
        aT = view("att", [P, KC, P], at=xaT_at)

        ps = ctx.enter_context(nc.psum_tensor("ps", [P, 8, 512], F32))
        PS_GU, PS_HT, PS_Y, PS_XT, PS_MISC = 0, 2, 3, 5, 7
        ps_logit = ps[:, PS_MISC, 0:NT * E].rearrange("p (t e) -> p t e", e=E)
        ps_rank = ps[:, PS_MISC, 128:256].rearrange("p (t e) -> p t e", e=E)
        ps_count = ps[:, PS_MISC, 256:256 + E]
        ps_list = ps[:, PS_MISC, 288:288 + 2 * JP]
        PS_ST, PS_S, PS_O, PS_A = 0, 4, 6, 7

        def bc(ap, shape):
            return ap.to_broadcast(shape)

        b12f = hT[0:E + 2, 0, :]
        b12p = ysb[0:E + 2, 0, 0:3 * INTER].bitcast(BF16).rearrange("p (k f) -> p k f", k=3)

        block = ctx.enter_context(nc.Block())

        def ffn_sp(f):
            for t in range(NT):
                sp_ = nc.sync
                sp_.wait_ge(sem(f"xn{f}"), t + 1)
                sp_.dma_start(xn_dram[t * P:(t + 1) * P, :], xn[:, t % 2, :]).then_inc(sem(f"xn_out{f}_{t % 2}"), 16)
            def store(j, par):
                nc.sync.wait_ge(sem(f"y_sb{f}"), j + 1)
                nc.sync.dma_start(y_dram[ds(j * P, P), :], ysb[:, par, :]).then_inc(sem(f"y_out{f}_{par}"), 16)
            with nc.sync.Fori(0, JOBS // 2) as i:
                store(2 * i, 0)
                store(2 * i + 1, 1)
            store(JOBS - 1, 0)

        def att_sp():
            def q_rows(b):
                p = b % 2
                nc.sync.wait_ge(sem("q_parts"), 3 * KC * (b + 1))
                for k in range(3):
                    nc.sync.dma_start(q_dram[p, k].rearrange("(c p) t -> p c t", p=P), qp[:, k]).then_inc(sem(f"q_out{p}"), 16)
                nc.sync.wait_ge(sem("k_parts"), 3 * (b + 1))
                nc.sync.dma_start(k_dram[p].rearrange("k d t -> d k t"), kp[:]).then_inc(sem(f"q_out{p}"), 16)
                nc.sync.wait_ge(sem(f"q_out{p}"), 64 * (b // 2 + 1))
                if b >= 2:
                    nc.sync.wait_ge(sem("st_done"), HEADS // 2 * (b - 1))
                for r in range(6):
                    nc.sync.dma_start(qside[r * HD:(r + 1) * HD, p],
                                      q_dram[p, QPART[r]].rearrange("(h d) t -> d h t", d=HD)).then_inc(sem(f"q_in{p}"), 16)
                    nc.sync.dma_start(kT[r * HD:(r + 1) * HD, p], k_dram[p, KPART[r]]).then_inc(sem(f"q_in{p}"), 16)

            def m_rows(b):
                p = b % 2
                nc.sync.wait_ge(sem("m_parts"), 3 * (b + 1))
                nc.sync.dma_start(m_dram[p].rearrange("k r q -> r k q"), mp[:]).then_inc(sem(f"m_out{p}"), 16)
                nc.sync.wait_ge(sem(f"m_out{p}"), 16 * (b // 2 + 1))
                for q in range(QT):
                    nc.sync.dma_start(qside[R_MAX:ROWS, p, :, q * P:(q + 1) * P],
                                      m_dram[p, :, q * HEADS:(q + 1) * HEADS, :]).then_inc(sem(f"m_in{p}"), 16)

            q_rows(0)
            q_rows(1)
            m_rows(0)
            for b in range(BATCH):
                if b + 1 < BATCH:
                    m_rows(b + 1)
                if b + 2 < BATCH:
                    q_rows(b + 2)

        @block.sync
        def _(sp):
            sp.dma_start(x[:, 0:NT // 2, :], x_in[0:TOKENS // 2, :].rearrange("(t p) d -> p t d", p=P)).then_inc(sem("x_in0"), 16)
            sp.dma_start(x[:, NT // 2:, :], x_in[TOKENS // 2:, :].rearrange("(t p) d -> p t d", p=P)).then_inc(sem("x_in1"), 16)
            sp.dma_start(cf[:], const_f).then_inc(sem("small_in"), 16)
            sp.dma_start(rw[:], rw_in.rearrange("(c p) e -> p c e", p=P)).then_inc(sem("small_in"), 16)
            sp.dma_start(rbc[:, 0, :], rb_in.partition_broadcast(P)).then_inc(sem("small_in"), 16)
            sp.dma_start(rbc[:, 1, :], rbias_in.partition_broadcast(P)).then_inc(sem("small_in"), 16)
            sp.dma_start(eb3x[0:E, :], eb3).then_inc(sem("small_in"), 16)
            sp.dma_start(eb3x[E:E + 1, :], sb3.rearrange("(a d) -> a d", a=1)).then_inc(sem("small_in"), 16)
            sp.dma_start(b12f[0:E, 0:INTER], eb1).then_inc(sem("bias_in"), 16)
            sp.dma_start(b12f[0:E, INTER:2 * INTER], eb2).then_inc(sem("bias_in"), 16)
            sp.dma_start(b12f[E:E + 1, :], sb1.rearrange("(a d) -> a d", a=1)).then_inc(sem("bias_in"), 16)
            sp.dma_start(b12f[E + 1:E + 2, :], sb2.rearrange("(a d) -> a d", a=1)).then_inc(sem("bias_in"), 16)
            sp.wait_ge(sem("bias_split"), 5)
            sp.dma_start(b12_dram.rearrange("k e f -> e k f"), b12p).then_inc(sem("bias_out"), 16)
            sp.wait_ge(sem("bias_out"), 16)
            sp.dma_start(b12x[:], b12_dram.rearrange("k e f -> k (e f)")).then_inc(sem("bias_rows"), 16)
            ffn_sp(0)
            att_sp()
            ffn_sp(1)
            for t in range(NT):
                sp.wait_ge(sem("final1"), t + 1)
                sp.dma_start(out[t * P:(t + 1) * P, :], x[:, t, :]).then_inc(sem("stored"), 16)
            sp.wait_ge(sem("stored"), 16 * NT)


        def ffn_pool(f):
            pool = nc.gpsimd
            pool.wait_ge(sem(f"var{f}"), 1)
            pool.tensor_tensor(rstd[:], varE[:], neghalf[:], ALU.pow).then_inc(sem(f"rstd{f}"), 1)
            pool.wait_ge(sem(f"list{f}"), 1)
            pool.wait_ge(sem(f"xn_out{f}_0"), 16 * (NT // 2))
            pool.wait_ge(sem(f"xn_out{f}_1"), 16 * (NT // 2))
            for j in range(JOBS):
                if j >= 2:
                    pool.wait_ge(sem(f"xgt{f}"), j - 1)
                pool.indirect_dma_start(xg[:, j % 2, :], None, xn_dram,
                                        bass.IndirectOffsetOnAxis(ap=listu[:, j:j + 1], axis=0)).then_inc(sem(f"xg{f}_{j % 2}"), 16)
            pool.wait_ge(sem(f"y_out{f}_0"), 16 * ((JOBS + 1) // 2))
            pool.wait_ge(sem(f"y_out{f}_1"), 16 * (JOBS // 2))
            for t in range(NT):
                if t >= 2:
                    pool.wait_ge(sem(f"final{f}"), t - 1)
                for c in range(CHOICES):
                    pool.indirect_dma_start(yg[:, t % 2, c, :], None, y_dram,
                                            bass.IndirectOffsetOnAxis(ap=slotu[:, c, t:t + 1], axis=0)).then_inc(sem(f"yg{f}_{t % 2}"), 16)

        def att_pool():
            pool = nc.gpsimd
            pool.wait_ge(sem("final0"), NT)
            for p in range(2):
                pool.dma_start(qside[R_ALIBI:R_MAX, p], rows_q).then_inc(sem("rows_in"), 16)
                pool.dma_start(kT[R_ALIBI:ROWS, p], rows_k).then_inc(sem("rows_in"), 16)
            for b in range(BATCH):
                pool.wait_ge(sem("a_var"), b + 1)
                pool.tensor_tensor(rstd[:, 2 * b:2 * b + 2], varE[:, 2 * b:2 * b + 2], neghalf[:, 0:2], ALU.pow).then_inc(sem("a_rstd"), 1)

        @block.gpsimd
        def _(pool):
            pool.dma_start(cb[:], const_b).then_inc(sem("cb_in"), 16)
            pool.memset(neghalf[:], -0.5).then_inc(sem("neghalf"), 1)
            pool.wait_ge(sem("neghalf"), 1)
            ffn_pool(0)
            att_pool()
            ffn_pool(1)


        def ffn_act(f):
            act = nc.scalar
            for t in range(NT):
                act.wait_ge(sem(f"xt{f}"), t + 1)
                act.copy(xnT[:, t].rearrange("p c q -> p (c q)"), ps[:, PS_XT + t % 2, :]).then_inc(sem(f"xnT{f}"), 1)
            act.wait_ge(sem(f"lg{f}"), 1)
            act.activation(t16[:].rearrange("p t e -> p (t e)"), lg[:].rearrange("p t e -> p (t e)"), ACT.Exp).then_inc(sem(f"rexp{f}"), 1)
            for t in range(NT + 1):
                if t < NT:
                    act.wait_ge(sem(f"s_gu{f}"), t + 1)
                    act.activation(sg[:, t % 2, :], ps[:, PS_GU + t % 2, 0:SHARED], ACT.Silu).then_inc(sem(f"s_silu{f}"), 1)
                if t >= 1:
                    act.wait_ge(sem(f"s_ht{f}"), t)
                    act.copy(hT[:, (t - 1) % 2, :], ps[:, PS_HT, SHARED * ((t - 1) % 2):SHARED * ((t - 1) % 2 + 1)]).then_inc(sem(f"s_hT{f}"), 1)
            for n in range(NT // 2):
                act.wait_ge(sem(f"gt{f}"), n + 1)
                if n >= 1:
                    act.wait_ge(sem(f"c{f}"), 2 * n)
                act.copy(gateT[:].rearrange("e t q -> e (t q)"), ps[0:E + 1, PS_XT + n % 2, 0:2 * P]).then_inc(sem(f"gateT{f}"), 1)

            def gather_copy(j, par):
                act.wait_ge(sem(f"xgt{f}"), j + 1)
                act.copy(xgT[:, par].rearrange("p c q -> p (c q)"), ps[:, PS_XT + par, :]).then_inc(sem(f"xgT{f}"), 1)

            def silu(j, par):
                act.wait_ge(sem(f"gu{f}"), j + 1)
                act.activation(sg[:, par, 0:INTER], ps[:, PS_GU + par, 0:INTER], ACT.Silu).then_inc(sem(f"silu{f}"), 1)

            def h_copy(j, par):
                act.wait_ge(sem(f"ht{f}"), j + 1)
                act.copy(hT[:, par, 0:INTER], ps[:, PS_HT, P * par:P * par + P]).then_inc(sem(f"hT{f}"), 1)

            def body(j, par, last=False):
                h_copy(j - 1, 1 - par)
                silu(j, par)
                if not last:
                    gather_copy(j + 1, 1 - par)
            gather_copy(0, 0)
            silu(0, 0)
            gather_copy(1, 1)
            with act.Fori(0, JOBS // 2 - 1) as i:
                body(2 * i + 1, 1)
                body(2 * i + 2, 0)
            body(JOBS - 2, 1)
            body(JOBS - 1, 0, last=True)
            h_copy(JOBS - 1, 0)

        def att_act():
            act = nc.scalar

            def qkv(b):
                for c in range(4):
                    act.wait_ge(sem("a_xt"), 4 * b + c + 1)
                    act.copy(xaT[:, :, (c // 2) * P:(c // 2 + 1) * P][:, 2 * (c % 2):2 * (c % 2) + 2, :],
                             ps[:, PS_ST + c % 4, 0:2 * P].rearrange("p (c q) -> p c q", c=2)).then_inc(sem("a_xaT"), 1)
                if b >= 1:
                    act.wait_ge(sem(f"q_out{(b - 1) % 2}"), 64 * ((b - 1) // 2 + 1))
                for c in range(KC):
                    act.wait_ge(sem("a_q"), KC * b + c + 1)
                    act.copy(qp[:, 0, c, :], ps[:, PS_ST + c, 0:SEQ]).then_inc(sem("q1"), 1)
                act.wait_ge(sem("a_k"), b + 1)
                act.mul(kp[:, 0, :], ps[0:HD, PS_S, 0:SEQ], HD ** -0.5).then_inc(sem("k1"), 1)

            def out_proj(b):
                for q in range(QT):
                    act.wait_ge(sem("a_at"), QT * b + q + 1)
                    if q >= 1 or b >= 1:
                        act.wait_ge(sem("a_wo"), QT * b + q)
                    act.copy(aT[:].rearrange("p c q -> p (c q)"), ps[:, PS_A, :]).then_inc(sem("a_aT"), 1)

            def exp(n, par):
                act.wait_ge(sem("st_done"), n + 1)
                act.activation(pr[:, par, :], ps[:, PS_ST + 2 * par:PS_ST + 2 * par + 2, :].rearrange("p a b -> p (a b)")[:, 0:768],
                               ACT.Exp).then_inc(sem("exp"), 1)

            qkv(0)
            qkv(1)
            for b in range(BATCH):
                if b > 0:
                    act.wait_ge(sem("pv"), 16 * b)
                nb = min(b + 1, BATCH - 1)
                act.wait_ge(sem(f"q_out{nb % 2}"), 64 * (nb // 2 + 1))
                exp(16 * b, 0)
                exp(16 * b + 1, 1)
                with act.Fori(1, HEADS // 4) as i:
                    for par in range(2):
                        act.wait_ge(sem("pv"), 16 * b + 2 * i + par - 1)
                        exp(16 * b + 2 * i + par, par)
                out_proj(b)
                if b + 2 < BATCH:
                    qkv(b + 2)

        @block.scalar
        def _(act):
            act.dma_start(sw12[:, :, 0:SHARED], sw1.rearrange("(c p) f -> p c f", p=P)).then_inc(sem("sw_in"), 16)
            act.dma_start(sw12[:, :, SHARED:], sw2.rearrange("(c p) f -> p c f", p=P)).then_inc(sem("sw_in"), 16)
            act.dma_start(sw3s[:], sw3.rearrange("(c p) d -> p c d", p=P)).then_inc(sem("sw_in"), 16)
            for e in range(E):
                act.dma_start(w12[:, e, :, 0:INTER], ew1[e].rearrange("(c p) f -> p c f", p=P)).then_inc(sem("ew_in"), 16)
                act.dma_start(w12[:, e, :, INTER:], ew2[e].rearrange("(c p) f -> p c f", p=P)).then_inc(sem("ew_in"), 16)
                act.dma_start(w3[:, e, :], ew3[e]).then_inc(sem("ew_in"), 16)
            act.dma_start(wqkv[:], wqkv_in.rearrange("(c p) n -> p c n", p=P)).then_inc(sem("aw_in"), 16)
            act.dma_start(wo[:], wo_in.rearrange("(c p) n -> p c n", p=P)).then_inc(sem("aw_in"), 16)
            ffn_act(0)
            att_act()
            ffn_act(1)


        def ffn_dve(f):
            dve = nc.vector
            count = [0]
            chain = sem(f"chain{f}")

            def link(ins):
                count[0] += 1
                ins.then_inc(chain, 1)
                dve.wait_ge(chain, count[0])

            for t in range(NT):
                if f == 0 and t % (NT // 2) == 0:
                    dve.wait_ge(sem(f"x_in{t // (NT // 2)}"), 16)
                if f == 1 and t == 0:
                    dve.wait_ge(sem("att_x"), NT)
                ins = dve.bn_stats(st[:, t, :], x[:, t, :])
            link(ins)
            for t in range(NT):
                ins = dve.bn_aggr(mv[:, t, :], st[:, t, :])
            link(ins)
            dve.tensor_scalar(varE[:], mv[:, :, 1], EPS, None, ALU.add).then_inc(sem(f"var{f}"), 1)
            dve.wait_ge(sem(f"rstd{f}"), 1)
            for t in range(NT):
                if t >= 2:
                    dve.wait_ge(sem(f"xt{f}"), t - 1)
                    dve.wait_ge(sem(f"xn_out{f}_{t % 2}"), 16 * (t // 2))
                dve.tensor_scalar(xn[:, t % 2, :], x[:, t, :], mv[:, t, 0:1], rstd[:, t:t + 1],
                                  ALU.subtract, ALU.mult).then_inc(sem(f"xn{f}"), 1)

            def logits():
                if f == 0:
                    dve.wait_ge(sem("small_in"), 96)
                dve.wait_ge(sem(f"logit{f}"), 1)
                link(dve.tensor_tensor(lg[:], ps_logit, bc(rbc[:, 0:1, :], [P, NT, E]), ALU.add))
                link(dve.tensor_reduce(red[:], lg[:], AX_X, ALU.max))
                dve.tensor_tensor(lg[:], lg[:], bc(red[:, :, None], [P, NT, E]), ALU.subtract).then_inc(sem(f"lg{f}"), 1)

            def scores():
                dve.wait_ge(sem(f"rexp{f}"), 1)
                link(dve.tensor_reduce(red[:], t16[:], AX_X, ALU.add))
                link(dve.reciprocal(red[:], red[:]))
                link(dve.tensor_tensor(t16[:], t16[:], bc(red[:, :, None], [P, NT, E]), ALU.mult))
                link(dve.tensor_tensor(sc[:], t16[:], bc(rbc[:, 1:2, :], [P, NT, E]), ALU.add))

            def groups():
                link(dve.memset(gm8[:], -3e38))
                link(dve.tensor_reduce(gm8[:, :, 0:GROUPS], sc[:].rearrange("p t (g j) -> p t g j", g=GROUPS), AX_X, ALU.max))
                for t in range(NT):
                    ins = dve.max(gtop[:, t, :], gm8[:, t, :])
                link(ins)
                for t in range(NT):
                    ins = dve.max_index(gidx[:, t, :], gtop[:, t, :], gm8[:, t, :])
                link(ins)
                link(dve.tensor_copy(idxf[:], gidx[:, :, 0:2]))
                iota4 = bc(iota[:, None, 0:GROUPS], [P, NT, GROUPS])
                dve.tensor_tensor(keep[:], iota4, bc(idxf[:, :, 0:1], [P, NT, GROUPS]), ALU.is_equal)
                link(dve.tensor_tensor(keep2[:], iota4, bc(idxf[:, :, 1:2], [P, NT, GROUPS]), ALU.is_equal))
                link(dve.tensor_tensor(keep[:], keep[:], keep2[:], ALU.add))
                link(dve.tensor_scalar(keep[:], keep[:], -NEG, NEG, ALU.mult, ALU.add))
                link(dve.tensor_tensor(t16[:].rearrange("p t (g j) -> p t g j", g=GROUPS),
                                       sc[:].rearrange("p t (g j) -> p t g j", g=GROUPS),
                                       bc(keep[:, :, :, None], [P, NT, GROUPS, E // GROUPS]), ALU.add))

            def experts():
                for t in range(NT):
                    ins = dve.max(etop[:, t, :], t16[:, t, :])
                link(ins)
                for t in range(NT):
                    ins = dve.max_index(eidx[:, t, :], etop[:, t, :], t16[:, t, :])
                link(ins)
                link(dve.tensor_copy(idxf[:], eidx[:, :, 0:2]))
                dve.tensor_scalar(hv[:], etop[:, :, 0:CHOICES], 0.5, None, ALU.mult)
                iota16 = bc(iota[:, None, 0:E], [P, NT, E])
                dve.tensor_tensor(oh[:, 0], iota16, bc(idxf[:, :, 0:1], [P, NT, E]), ALU.is_equal)
                link(dve.tensor_tensor(oh[:, 1], iota16, bc(idxf[:, :, 1:2], [P, NT, E]), ALU.is_equal))
                dve.tensor_tensor(taken[:], oh[:, 0], oh[:, 1], ALU.add).then_inc(sem(f"taken{f}"), 1)

            def gates():
                dve.memset(gate[:], 1.0)
                dve.tensor_tensor(t16[:], oh[:, 1], bc(etop[:, :, 1:2], [P, NT, E]), ALU.mult)
                link(dve.tensor_tensor(lg[:], oh[:, 0], bc(etop[:, :, 0:1], [P, NT, E]), ALU.mult))
                dve.tensor_tensor(gate[:, :, 0:E], lg[:], t16[:], ALU.add).then_inc(sem(f"gate{f}"), 1)

            def slots():
                dve.wait_ge(sem(f"rank{f}"), 1)
                link(dve.tensor_scalar(cnti[:], ps_count, float(P - 1), None, ALU.add))
                link(dve.tensor_scalar(cnti[:], cnti[:], P.bit_length() - 1, None, ALU.arith_shift_right))
                link(dve.tensor_copy(cnt[:, 0, :], cnti[:]))
                link(dve.tensor_copy(cnt[:, 1, :], cnti[:]))
                a, b, s = 1, 2, 1
                while s < E:
                    dve.tensor_copy(cnt[:, b, 0:s], cnt[:, a, 0:s])
                    link(dve.tensor_tensor(cnt[:, b, s:], cnt[:, a, s:], cnt[:, a, 0:E - s], ALU.add))
                    a, b, s = b, a, 2 * s
                end = cnt[0:1, a, :]
                link(dve.tensor_tensor(jcmp[:], bc(end[:, None, :], [1, JP, E]), bc(iota[0:1, 0:JP, None], [1, JP, E]), ALU.is_le))
                link(dve.tensor_reduce(jexf[:], jcmp[:], AX_X, ALU.add))
                dve.tensor_scalar(jex[:], jexf[:], float(E - 1), None, ALU.min).then_inc(sem(f"jex{f}"), 1)
                link(dve.tensor_tensor(cnt[:, 3, :], cnt[:, a, :], cnt[:, 0, :], ALU.subtract))
                link(dve.tensor_scalar(cnt[:, 3, :], cnt[:, 3, :], float(P), None, ALU.mult))
                link(dve.tensor_tensor(t16[:], ps_rank, bc(cnt[:, 3:4, :], [P, NT, E]), ALU.add))
                for c in range(CHOICES):
                    ins = dve.tensor_tensor(oh[:, c], oh[:, c], t16[:], ALU.mult)
                link(ins)
                link(dve.tensor_reduce(slot[:].rearrange("p c t -> p (c t)"), oh[:].rearrange("p c t e -> p (c t) e"), AX_X, ALU.add))
                dve.tensor_copy(slotu[:], slot[:])
                link(dve.tensor_copy(sloti[:], slot[:]))
                si = sloti[:].rearrange("p c t -> p (c t)")
                dve.tensor_scalar(sji[:, 0, :], si, P.bit_length() - 1, None, ALU.arith_shift_right)
                link(dve.tensor_scalar(sji[:, 1, :], si, P - 1, None, ALU.bitwise_and))
                link(dve.tensor_copy(sjf[:], sji[:]))
                n = CHOICES * NT
                dve.tensor_tensor(onehot_p[:], bc(iota[:, None, :], [P, n, P]), bc(sjf[:, 1, :, None], [P, n, P]), ALU.is_equal)
                link(dve.tensor_tensor(onehot_j[:, :, 1, :], bc(iota[:, None, 0:JP], [P, n, JP]), bc(sjf[:, 0, :, None], [P, n, JP]), ALU.is_equal))
                link(dve.tensor_scalar(onehot_j[:, :, 0, :], onehot_j[:, :, 1, :], cf[:, C_PIDX:C_PIDX + 1], None, ALU.mult))
                dve.tensor_tensor(onehot_j[:, :, 1, :], onehot_j[:, :, 1, :], bc(cf[:, C_TILE:C_TILE + n, None], [P, n, JP]),
                                  ALU.mult).then_inc(sem(f"onehot{f}"), 1)

            def token_list():
                dve.wait_ge(sem(f"listed{f}"), 1)
                link(dve.tensor_copy(listf[:], ps_list[:, 0:JP]))
                dve.tensor_tensor(listu[:], listf[:], ps_list[:, JP:], ALU.add).then_inc(sem(f"list{f}"), 1)

            logits()
            for t in range(NT + 1):
                if t < NT:
                    dve.wait_ge(sem(f"s_silu{f}"), t + 1)
                    dve.tensor_tensor(hh[:, t % 2, :], ps[:, PS_GU + t % 2, SHARED:], sg[:, t % 2, :], ALU.mult).then_inc(sem(f"s_h{f}"), 1)
                if t >= 1:
                    dve.wait_ge(sem(f"s_z{f}"), t)
                    dve.scalar_tensor_tensor(out=x[:, t - 1, :], in0=ps[:, PS_Y + (t - 1) % 2, :], scalar=0.5, in1=x[:, t - 1, :],
                                             op0=ALU.mult, op1=ALU.add).then_inc(sem(f"s_x{f}"), 1)
                if t == 0:
                    scores()
                    groups()
                if t == 1:
                    experts()
                if t == 2:
                    gates()
                if t == 3:
                    slots()
                if t == 5:
                    token_list()
            for t in range(NT):
                dve.wait_ge(sem(f"c{f}"), t + 1)
                dve.wait_ge(sem(f"s_x{f}"), t + 1)
                dve.scalar_tensor_tensor(out=x[:, t, :], in0=ps[:, PS_Y + t % 2, :], scalar=0.5, in1=x[:, t, :],
                                         op0=ALU.mult, op1=ALU.add).then_inc(sem(f"c_x{f}"), 1)

            def gated(j, par):
                dve.wait_ge(sem(f"silu{f}"), j + 1)
                dve.tensor_tensor(hh[:, par, 0:INTER], ps[:, PS_GU + par, INTER:2 * INTER], sg[:, par, 0:INTER], ALU.mult).then_inc(sem(f"h{f}"), 1)

            def rows_out(j, par, first=False):
                dve.wait_ge(sem(f"y{f}"), j + 1)
                if not first:
                    dve.wait_ge(sem(f"y_out{f}_{par}"), first_stores(j, par))
                dve.tensor_copy(ysb[:, par, :], ps[:, PS_Y + par, :]).then_inc(sem(f"y_sb{f}"), 1)

            def first_stores(j, par):
                return 8 * (j - par)

            gated(0, 0)
            gated(1, 1)
            rows_out(0, 0, first=True)
            gated(2, 0)
            rows_out(1, 1, first=True)
            with dve.Fori(1, JOBS // 2) as i:
                gated(2 * i + 1, 1)
                rows_out(2 * i, 0)
                gated(2 * i + 2, 0)
                rows_out(2 * i + 1, 1)
            rows_out(JOBS - 1, 0)
            for t in range(NT):
                dve.wait_ge(sem(f"yg{f}_{t % 2}"), 32 * (t // 2 + 1))
                dve.wait_ge(sem(f"c_x{f}"), t + 1)
                link(dve.scalar_tensor_tensor(out=x[:, t, :], in0=yg[:, t % 2, 0, :], scalar=hv[:, t, 0:1], in1=x[:, t, :],
                                              op0=ALU.mult, op1=ALU.add))
                dve.scalar_tensor_tensor(out=x[:, t, :], in0=yg[:, t % 2, 1, :], scalar=hv[:, t, 1:2], in1=x[:, t, :],
                                         op0=ALU.mult, op1=ALU.add).then_inc(sem(f"final{f}"), 1)

        def att_dve():
            dve = nc.vector
            count = [0]
            chain = sem("chain_a")

            def link(ins):
                count[0] += 1
                ins.then_inc(chain, 1)
                dve.wait_ge(chain, count[0])

            dve.wait_ge(sem("final0"), NT)
            link(dve.memset(vv[:], 1.0))
            for b in range(BATCH):
                for t in (2 * b, 2 * b + 1):
                    ins = dve.bn_stats(st[:, t, :], x[:, t, :])
                link(ins)
                for t in (2 * b, 2 * b + 1):
                    ins = dve.bn_aggr(mv[:, t, :], st[:, t, :])
                link(ins)
                dve.tensor_scalar(varE[:, 2 * b:2 * b + 2], mv[:, 2 * b:2 * b + 2, 1], EPS, None, ALU.add).then_inc(sem("a_var"), 1)

            def qkv(b):
                dve.wait_ge(sem("a_rstd"), b + 1)
                for q in range(QT):
                    t = QT * b + q
                    if b >= 1:
                        dve.wait_ge(sem("a_xt"), 4 * b)
                    if b >= 2:
                        dve.wait_ge(sem("a_at"), QT * (b - 1))
                    dve.tensor_scalar(xn[:, q, :], x[:, t, :], mv[:, t, 0:1], rstd[:, t:t + 1],
                                      ALU.subtract, ALU.mult).then_inc(sem("a_xn"), 1)
                for c in range(KC):
                    dve.wait_ge(sem("q1"), KC * b + c + 1)
                    dve.wait_ge(sem("q_parts"), 3 * (KC * b + c))
                    link(dve.tensor_tensor(qr[:], ps[:, PS_ST + c, 0:SEQ], qp[:, 0, c, :], ALU.subtract))
                    link(dve.tensor_copy(qp[:, 1, c, :], qr[:]))
                    dve.tensor_tensor(qp[:, 2, c, :], qr[:], qp[:, 1, c, :], ALU.subtract).then_inc(sem("q_parts"), 3)
                dve.wait_ge(sem("k1"), b + 1)
                dve.wait_ge(sem("q_parts"), 3 * KC * (b + 1))
                link(dve.scalar_tensor_tensor(out=kr[:], in0=ps[0:HD, PS_S, 0:SEQ], scalar=HD ** -0.5, in1=kp[:, 0, :],
                                              op0=ALU.mult, op1=ALU.subtract))
                link(dve.tensor_copy(kp[:, 1, :], kr[:]))
                dve.tensor_tensor(kp[:, 2, :], kr[:], kp[:, 1, :], ALU.subtract).then_inc(sem("k_parts"), 3)
                dve.wait_ge(sem("a_v"), b + 1)
                dve.tensor_copy(vv[:, b % 2, :, 0:HD], ps[:, PS_S + 1, 0:QT * HD].rearrange("p (t d) -> p t d", t=QT)).then_inc(sem("v_in"), 1)

            def block_maxima(b, g):
                dve.wait_ge(sem("s_done"), 16 * b + g + 1)
                dve.tensor_reduce(m3[:, ds(2 * g, 2), :], ps[:, PS_S:PS_S + 2, 0:3 * P].rearrange("p h (n k) -> p h n k", n=3),
                                  AX_X, ALU.max).then_inc(sem("s_max"), 1)

            def maxima(b):
                dve.wait_ge(sem("s_max"), 16 * (b + 1))
                if b >= 1:
                    dve.wait_ge(sem("m_t"), b)
                link(dve.tensor_tensor(m3[:, :, 1], m3[:, :, 1], m3[:, :, 2], ALU.max))
                dve.tensor_scalar(nm[:, 0, :], m3[:, :, 0], -1.0, None, ALU.mult)
                dve.tensor_scalar(nm[:, 1, :], m3[:, :, 1], -1.0, None, ALU.mult).then_inc(sem("m_nm"), 1)
                dve.wait_ge(sem("m_t"), b + 1)
                if b >= 1:
                    dve.wait_ge(sem(f"m_out{(b - 1) % 2}"), 16 * ((b - 1) // 2 + 1))
                src = ps[0:QT * HEADS, PS_O, 0:P]
                link(dve.tensor_copy(mp[:, 0, :], src))
                link(dve.tensor_tensor(mr[:], src, mp[:, 0, :], ALU.subtract))
                link(dve.tensor_copy(mp[:, 1, :], mr[:]))
                dve.tensor_tensor(mp[:, 2, :], mr[:], mp[:, 1, :], ALU.subtract).then_inc(sem("m_parts"), 3)

            def normalise(n, g, par):
                o = ps[:, PS_O + par, 0:QT * 2 * (HD + 1)].rearrange("p (t h d) -> p t h d", t=QT, h=2)
                dve.wait_ge(sem("pv"), n + 1)
                dve.reciprocal(rec[:, par], o[:, :, :, HD]).then_inc(sem("a_rec"), 1)
                dve.wait_ge(sem("a_rec"), n + 1)
                dve.tensor_tensor(attn[:, :, ds(g * 2 * HD, 2 * HD)].rearrange("p t (h d) -> p t h d", h=2), o[:, :, :, 0:HD],
                                  bc(rec[:, par, :, :, None], [P, QT, 2, HD]), ALU.mult).then_inc(sem("normed"), 1)

            qkv(0)
            qkv(1)
            with dve.Fori(0, HEADS // 2) as g:
                block_maxima(0, g)
            maxima(0)
            for b in range(BATCH):
                if b + 1 < BATCH:
                    block_maxima(b + 1, 0)
                    if b >= 1:
                        dve.wait_ge(sem("a_at"), QT * b)
                with dve.Fori(0, HEADS // 4 - 1) as i:
                    for par in range(2):
                        normalise(16 * b + 2 * i + par, 2 * i + par, par)
                        if b + 1 < BATCH:
                            block_maxima(b + 1, 2 * i + par + 1)
                normalise(16 * b + 14, 14, 0)
                if b + 1 < BATCH:
                    block_maxima(b + 1, 15)
                normalise(16 * b + 15, 15, 1)
                if b + 1 < BATCH:
                    maxima(b + 1)
                for q in range(QT):
                    dve.wait_ge(sem("a_wo"), QT * b + q + 1)
                    dve.tensor_tensor(x[:, QT * b + q, :], ps[:, PS_O, :], x[:, QT * b + q, :], ALU.add).then_inc(sem("att_x"), 1)
                if b + 2 < BATCH:
                    qkv(b + 2)

        @block.vector
        def _(dve):
            parts = b12p
            dve.wait_ge(sem("bias_in"), 64)
            dve.tensor_copy(parts[:, 0, :], b12f).then_inc(sem("bias_split"), 1)
            dve.wait_ge(sem("bias_split"), 1)
            dve.tensor_tensor(b12f, b12f, parts[:, 0, :], ALU.subtract).then_inc(sem("bias_split"), 1)
            dve.wait_ge(sem("bias_split"), 2)
            dve.tensor_copy(parts[:, 1, :], b12f).then_inc(sem("bias_split"), 1)
            dve.wait_ge(sem("bias_split"), 3)
            dve.tensor_tensor(b12f, b12f, parts[:, 1, :], ALU.subtract).then_inc(sem("bias_split"), 1)
            dve.wait_ge(sem("bias_split"), 4)
            dve.tensor_copy(parts[:, 2, :], b12f).then_inc(sem("bias_split"), 1)
            ffn_dve(0)
            att_dve()
            ffn_dve(1)


        def ffn_pe(f):
            pe = nc.tensor

            def logit(t):
                pe.wait_ge(sem(f"xnT{f}"), t + 1)
                for c in range(KC):
                    ins = pe.matmul(ps_logit[:, t, :], xnT[:, t, c, :], rw[:, c, :], start=(c == 0), stop=(c == KC - 1))
                if t == NT - 1:
                    ins.then_inc(sem(f"logit{f}"), 1)

            for t in range(NT):
                pe.wait_ge(sem(f"xn{f}"), t + 1)
                if t >= 2:
                    pe.wait_ge(sem(f"xnT{f}"), t - 1)
                for c in range(KC):
                    ins = pe.transpose(ps[:, PS_XT + t % 2, c * P:(c + 1) * P], xn[:, t % 2, c * P:(c + 1) * P], ident)
                ins.then_inc(sem(f"xt{f}"), 1)
                if t >= 1:
                    logit(t - 1)
            logit(NT - 1)
            if f == 0:
                pe.wait_ge(sem("sw_in"), 48)
                pe.wait_ge(sem("bias_rows"), 16)
                pe.wait_ge(sem("cb_in"), 16)

            def shared_up(t, chunks):
                o = ps[:, PS_GU + t % 2, :]
                if 0 in chunks:
                    if t >= 2:
                        pe.wait_ge(sem(f"s_h{f}"), t - 1)
                    pe.matmul(o, ones[0:3, :], b12x[:, E * 2 * INTER:], start=True, stop=False)
                for c in chunks:
                    ins = pe.matmul(o, xnT[:, t, c, :], sw12[:, c, :], start=False, stop=(c == KC - 1))
                if KC - 1 in chunks:
                    ins.then_inc(sem(f"s_gu{f}"), 1)

            def shared_turn(t):
                pe.wait_ge(sem(f"s_h{f}"), t + 1)
                if t >= 2:
                    pe.wait_ge(sem(f"s_hT{f}"), t - 1)
                for c in range(SHARED // P):
                    ins = pe.transpose(ps[:, PS_HT, (t % 2) * SHARED + c * P:(t % 2) * SHARED + (c + 1) * P],
                                       hh[:, t % 2, c * P:(c + 1) * P], ident)
                ins.then_inc(sem(f"s_ht{f}"), 1)

            def shared_down(t):
                pe.wait_ge(sem(f"s_hT{f}"), t + 1)
                if t >= 2:
                    pe.wait_ge(sem(f"s_x{f}"), t - 1)
                for c in range(SHARED // P):
                    ins = pe.matmul(ps[:, PS_Y + t % 2, :], hT[:, t % 2, c * P:(c + 1) * P], sw3s[:, c, :],
                                    start=(c == 0), stop=(c == SHARED // P - 1))
                ins.then_inc(sem(f"s_z{f}"), 1)

            def ranks():
                pe.wait_ge(sem(f"taken{f}"), 1)
                pe.matmul(ps_rank, upper, taken[:], start=True, stop=True)
                for t in range(NT - 1):
                    n = NT - 1 - t
                    pe.matmul(ps_rank[:, t + 1:, :], ones, bc(taken[:, t:t + 1, :], [P, n, E]), start=False, stop=True,
                              skip_group_check=True)
                for t in range(NT):
                    ins = pe.matmul(ps_count, ones, taken[:, t, :], start=(t == 0), stop=(t == NT - 1))
                ins.then_inc(sem(f"rank{f}"), 1)

            def listing():
                pe.wait_ge(sem(f"onehot{f}"), 1)
                n = CHOICES * NT
                for k in range(n):
                    ins = pe.matmul(ps_list, onehot_p[:, k, :], onehot_j[:, k].rearrange("p a j -> p (a j)"),
                                    start=(k == 0), stop=(k == n - 1))
                ins.then_inc(sem(f"listed{f}"), 1)

            for t in range(NT + 1):
                if t < NT:
                    shared_up(t, (0, 1))
                if t >= 1:
                    shared_turn(t - 1)
                if t < NT:
                    shared_up(t, (2, 3))
                if t >= 1:
                    shared_down(t - 1)
                if t == 3:
                    ranks()
                if t == 5:
                    listing()
            pe.wait_ge(sem(f"gate{f}"), 1)
            for n in range(NT // 2):
                if n >= 2:
                    pe.wait_ge(sem(f"gateT{f}"), n - 1)
                for t in range(2):
                    ins = pe.transpose(ps[0:E + 1, PS_XT + n % 2, t * P:(t + 1) * P], gate[:, 2 * n + t, :], ident)
                ins.then_inc(sem(f"gt{f}"), 1)
                pe.wait_ge(sem(f"gateT{f}"), n + 1)
                for t in range(2 * n, 2 * n + 2):
                    pe.wait_ge(sem(f"s_x{f}"), NT - 1 + t % 2)
                    if t >= 2:
                        pe.wait_ge(sem(f"c_x{f}"), t - 1)
                    pe.matmul(ps[:, PS_Y + t % 2, :], gateT[:, t % 2, :], eb3x[:], start=True, stop=True).then_inc(sem(f"c{f}"), 1)

            if f == 0:
                pe.wait_ge(sem("ew_in"), 16 * 3 * E)
            pe.wait_ge(sem(f"jex{f}"), 1)
            pe.wait_ge(sem(f"gateT{f}"), NT // 2)

            def turn(j, par, n):
                pe.wait_ge(sem(f"xg{f}_{par}"), n)
                for c in range(KC):
                    ins = pe.transpose(ps[:, PS_XT + par, c * P:(c + 1) * P], xg[:, par, c * P:(c + 1) * P], ident)
                ins.then_inc(sem(f"xgt{f}"), 1)

            def up(j, par, first=False):
                e = pe.value_load(jex[0:1, ds(j, 1)], min_val=0, max_val=E - 1)
                pe.wait_ge(sem(f"xgT{f}"), j + 1)
                if not first:
                    pe.wait_ge(sem(f"h{f}"), j - 1)
                o = ps[:, PS_GU + par, 0:2 * INTER]
                pe.matmul(o, ones[0:3, :], b12x[:, ds(e * 2 * INTER, 2 * INTER)], start=True, stop=False)
                for c in range(KC):
                    ins = pe.matmul(o, xgT[:, par, c, :], w12[:, ds(e, 1), c, :], start=False, stop=(c == KC - 1))
                ins.then_inc(sem(f"gu{f}"), 1)
                return e

            def h_turn(j, par):
                pe.wait_ge(sem(f"h{f}"), j + 1)
                pe.transpose(ps[:, PS_HT, P * par:P * par + P], hh[:, par, 0:INTER], ident).then_inc(sem(f"ht{f}"), 1)

            def down(j, par, first=False):
                e = pe.value_load(jex[0:1, ds(j, 1)], min_val=0, max_val=E - 1)
                pe.wait_ge(sem(f"hT{f}"), j + 1)
                if not first:
                    pe.wait_ge(sem(f"y_sb{f}"), j - 1)
                pe.matmul(ps[:, PS_Y + par, :], hT[:, par, 0:INTER], w3[:, ds(e, 1), :], start=True, stop=True).then_inc(sem(f"y{f}"), 1)

            turn(0, 0, 16)
            up(0, 0, first=True)
            turn(1, 1, 16)
            h_turn(0, 0)
            pe.wait_ge(sem(f"c_x{f}"), NT)
            up(1, 1, first=True)
            turn(2, 0, 32)
            down(0, 0, first=True)
            h_turn(1, 1)
            up(2, 0)
            turn(3, 1, 32)
            down(1, 1, first=True)
            with pe.Fori(1, JOBS // 2 - 1) as i:
                h_turn(2 * i, 0)
                up(2 * i + 1, 1)
                turn(2 * i + 2, 0, 16 * i + 32)
                down(2 * i, 0)
                h_turn(2 * i + 1, 1)
                up(2 * i + 2, 0)
                turn(2 * i + 3, 1, 16 * i + 32)
                down(2 * i + 1, 1)
            L = JOBS // 2 - 1
            h_turn(2 * L, 0)
            up(2 * L + 1, 1)
            turn(2 * L + 2, 0, 16 * L + 32)
            down(2 * L, 0)
            h_turn(2 * L + 1, 1)
            up(2 * L + 2, 0)
            down(2 * L + 1, 1)
            h_turn(2 * L + 2, 0)
            down(2 * L + 2, 0)

        def att_pe():
            pe = nc.tensor
            pe.wait_ge(sem("aw_in"), 32)

            def qkv(b):
                for c in range(4):
                    q, half = c // 2, c % 2
                    pe.wait_ge(sem("a_xn"), QT * b + q + 1)
                    if b == 1:
                        pe.wait_ge(sem("q_parts"), 3 * (c + 1))
                    if b >= 2 and c == 0:
                        pe.wait_ge(sem("exp"), 16 * (b - 1))
                    for k in range(2):
                        ins = pe.transpose(ps[:, PS_ST + c, k * P:(k + 1) * P], xn[:, q, (2 * half + k) * P:(2 * half + k + 1) * P], ident)
                    ins.then_inc(sem("a_xt"), 1)
                pe.wait_ge(sem("a_xaT"), 4 * (b + 1))
                for c in range(KC):
                    for k in range(KC):
                        ins = pe.matmul(ps[:, PS_ST + c, 0:SEQ], wqkv[:, k, c * P:(c + 1) * P], xaT[:, k, :], start=(k == 0), stop=(k == KC - 1))
                    ins.then_inc(sem("a_q"), 1)
                if b == 1:
                    pe.wait_ge(sem("v_in"), 1)
                if b >= 2:
                    pe.wait_ge(sem("s_max"), 16 * b)
                for k in range(KC):
                    ins = pe.matmul(ps[0:HD, PS_S, 0:SEQ], wqkv[:, k, DIM:DIM + HD], xaT[:, k, :], start=(k == 0), stop=(k == KC - 1))
                ins.then_inc(sem("a_k"), 1)
                for q in range(QT):
                    for k in range(KC):
                        ins = pe.matmul(ps[:, PS_S + 1, q * HD:(q + 1) * HD], xaT[:, k, q * P:(q + 1) * P], wqkv[:, k, DIM + HD:],
                                        start=(k == 0), stop=(k == KC - 1))
                ins.then_inc(sem("a_v"), 1)

            def scores(b, g):
                p = b % 2
                for hh_ in range(2):
                    h = 2 * g + hh_
                    o = ps[:, PS_S + hh_, :]
                    pe.matmul(o.rearrange("p (n k) -> p n k", k=P)[:, 0:3:2, :], identb, mask, start=True, stop=True)
                    pe.matmul(o[:, 0:P], qside[0:R_MAX, p, ds(h, 1), 0:P], kT[0:R_MAX, p, 0:P], start=False, stop=True, skip_group_check=True)
                    ins = pe.matmul(o[:, P:3 * P], qside[0:R_MAX, p, ds(h, 1), P:2 * P], kT[0:R_MAX, p, :], start=False, stop=True, skip_group_check=True)
                ins.then_inc(sem("s_done"), 1)

            def scores_t(b, g, par):
                p = b % 2
                o = ps[:, PS_ST + 2 * par:PS_ST + 2 * par + 2, :]
                pe.matmul(o[:, 0, :].rearrange("p (h q) -> p h q", h=2)[:, :, 0:P], identb, mask_t, start=True, stop=True)
                pe.matmul(o[:, 0, :], kT[0:ROWS, p, 0:P], qside[0:ROWS, p, ds(2 * g, 2), :], start=False, stop=True,
                          skip_group_check=True)
                pe.matmul(o[:, 1, 0:2 * P], identb, mask_t, start=True, stop=True)
                pe.matmul(o[:, 1, 0:2 * P], kT[0:ROWS, p, P:2 * P], qside[0:ROWS, p, ds(2 * g, 2), P:2 * P],
                          start=False, stop=True, skip_group_check=True).then_inc(sem("st_done"), 1)

            def weigh(b, n, par):
                pe.wait_ge(sem("exp"), n + 1)
                o = ps[:, PS_O + par, 0:QT * 2 * (HD + 1)].rearrange("p (t h d) -> p t h d", t=QT, h=2)
                k0 = pr[:, par, 0:2 * SEQ].rearrange("p (h q) -> p h q", h=2)
                k1 = pr[:, par, 2 * SEQ:].rearrange("p (h q) -> p h q", h=2)
                for h in range(2):
                    pe.matmul(o[:, 0, h, :], k0[:, h, 0:P], vv[:, b % 2, 0, :], start=True, stop=True)
                    pe.matmul(o[:, 1, h, :], k0[:, h, P:], vv[:, b % 2, 0, :], start=True, stop=False)
                    ins = pe.matmul(o[:, 1, h, :], k1[:, h, :], vv[:, b % 2, 1, :], start=False, stop=True)
                ins.then_inc(sem("pv"), 1)

            def max_turn(b):
                pe.wait_ge(sem("m_nm"), b + 1)
                if b >= 1:
                    pe.wait_ge(sem("normed"), 16 * b - 1)
                pe.transpose(ps[0:QT * HEADS, PS_O, 0:P], nm[:].rearrange("p t h -> p (t h)"), ident).then_inc(sem("m_t"), 1)

            def out_proj(b):
                pe.wait_ge(sem("normed"), 16 * (b + 1))
                if b + 1 < BATCH:
                    pe.wait_ge(sem("m_parts"), 3 * (b + 2))
                for q in range(QT):
                    if q >= 1:
                        pe.wait_ge(sem("a_aT"), QT * b + q)
                    for c in range(KC):
                        ins = pe.transpose(ps[:, PS_A, c * P:(c + 1) * P], attn[:, q, c * P:(c + 1) * P], ident)
                    ins.then_inc(sem("a_at"), 1)
                    pe.wait_ge(sem("a_aT"), QT * b + q + 1)
                    if q >= 1:
                        pe.wait_ge(sem("att_x"), QT * b + q)
                    for c in range(KC):
                        ins = pe.matmul(ps[:, PS_O, :], aT[:, c, :], wo[:, c, :], start=(c == 0), stop=(c == KC - 1))
                    ins.then_inc(sem("a_wo"), 1)

            qkv(0)
            qkv(1)
            pe.wait_ge(sem("rows_in"), 64)
            pe.wait_ge(sem("q_in0"), 192)
            pe.wait_ge(sem("v_in"), 2)
            scores(0, 0)
            with pe.Fori(1, HEADS // 2) as g:
                pe.wait_ge(sem("s_max"), g)
                scores(0, g)
            max_turn(0)
            for b in range(BATCH):
                nxt = b + 1 < BATCH
                n0 = 16 * b
                if b >= 1:
                    pe.wait_ge(sem("att_x"), QT * b)
                if nxt:
                    pe.wait_ge(sem(f"q_in{(b + 1) % 2}"), 192 * ((b + 1) // 2 + 1))
                    pe.wait_ge(sem("s_max"), n0 + 16)
                    pe.wait_ge(sem("v_in"), min(b + 2, BATCH))
                pe.wait_ge(sem(f"q_parts"), 3 * KC * min(b + 2, BATCH))
                pe.wait_ge(sem(f"m_in{b % 2}"), 32 * (b // 2 + 1))

                def group(g, par, lag):
                    scores_t(b, g, par)
                    if lag:
                        weigh(b, n0 + g - 1, 1 - par)
                    if nxt:
                        if lag:
                            pe.wait_ge(sem("s_max"), n0 + 16 + g)
                        scores(b + 1, g)
                def freed(n):
                    pe.wait_ge(sem("exp"), n - 1)
                    if not (type(n) is int and n < 3):
                        pe.wait_ge(sem("normed"), n - 2)
                group(0, 0, False)
                group(1, 1, True)
                for g in (2, 3):
                    freed(n0 + g)
                    group(g, g % 2, True)
                with pe.Fori(2, HEADS // 4) as i:
                    for par in range(2):
                        freed(n0 + 2 * i + par)
                        group(2 * i + par, par, True)
                pe.wait_ge(sem("normed"), n0 + 14)
                weigh(b, n0 + 15, 1)
                if nxt:
                    max_turn(b + 1)
                out_proj(b)
                if b + 2 < BATCH:
                    qkv(b + 2)

        @block.tensor
        def _(pe):
            pe.wait_ge(sem("small_in"), 96)
            ffn_pe(0)
            att_pe()
            ffn_pe(1)


_INS = ['L0_attn_hidden_states', 'L0_attn_Wqkv', 'L0_attn_Wo', 'L0_ffn_router_w', 'L0_ffn_router_b', 'L0_ffn_router_bias',
        'L0_ffn_ew1', 'L0_ffn_eb1', 'L0_ffn_ew2', 'L0_ffn_eb2', 'L0_ffn_ew3', 'L0_ffn_eb3',
        'L0_ffn_sw1', 'L0_ffn_sb1', 'L0_ffn_sw2', 'L0_ffn_sb2', 'L0_ffn_sw3', 'L0_ffn_sb3']


def kernel(**inputs):
    import numpy as _np
    import concourse.bacc as _bacc
    from concourse import mybir as _mybir
    from concourse.bass_utils import run_bass_kernel_spmd as _run

    nc = _bacc.Bacc("TRN2", target_bir_lowering=False, num_devices=1)
    arrays, args = {}, []
    named = {name: _np.ascontiguousarray(inputs[name]) for name in _INS}
    named.update(shape_constants())
    for name, a in named.items():
        if name == 'L0_attn_hidden_states':
            a = a.reshape(TOKENS, DIM)
        arrays[f"in_{name}_dram"] = a
        args.append(nc.dram_tensor(f"in_{name}_dram", a.shape, _mybir.dt.from_np(a.dtype), kind="ExternalInput").ap())
    args.append(nc.dram_tensor("out_0_dram", (TOKENS, DIM), _mybir.dt.float32, kind="ExternalOutput").ap())
    build(nc, *args)
    r = _run(nc, [arrays], core_ids=[0])
    return r.results[0]["out_0_dram"].reshape(BATCH, SEQ, DIM)
```

```python
from contextlib import ExitStack

import numpy as np

import concourse.bass as bass
from concourse import mybir
from concourse.alu_op_type import AluOpType as ALU

F32 = mybir.dt.float32
BF16 = mybir.dt.bfloat16
I32 = mybir.dt.int32
U32 = mybir.dt.uint32
ACT = mybir.ActivationFunctionType
AX_X = mybir.AxisListType.X
ds = bass.ds

P = 128
BATCH, SEQ, DIM = 4, 256, 512
TOKENS = BATCH * SEQ
NT = TOKENS // P
KC = DIM // P
E, GROUPS, INTER = 16, 4, 128
SHARED = 256
CHOICES = 2
JOBS = CHOICES * TOKENS // P + E - 1
EG = 4
JOBS_LEAST = CHOICES * TOKENS // P
JP = 32
HEADS, HD = 32, 16
QT = SEQ // P
NEG = -1e30
EPS = 1e-5

QPART = (0, 0, 0, 1, 1, 2)
KPART = (0, 1, 2, 0, 1, 0)
R_ALIBI = len(QPART) * HD
R_MAX = R_ALIBI + 6
ROWS = R_MAX + 3

FIRST = 6

C_ID, C_IOTA, C_PIDX, C_TILE, C_END = 0, 128, 256, 257, 273
B_UP, B_ONE, B_ID, B_MASK, B_END = 0, 128, 256, 384, 640


def bf16_parts(a):
    parts, rest = [], a.astype(np.float64)
    for _ in range(3):
        bits = rest.astype(np.float32).view(np.uint32)
        bits = (bits + 0x7FFF + ((bits >> 16) & 1)) & np.uint32(0xFFFF0000)
        part = bits.astype(np.uint32).view(np.float32)
        parts.append(part)
        rest = rest - part
    return np.stack(parts)


def shape_constants():
    i = np.arange(P)
    const_f = np.zeros((P, C_END), np.float32)
    const_f[:, C_ID:C_ID + P] = np.eye(P)
    const_f[:, C_IOTA:C_IOTA + P] = i[None, :]
    const_f[:, C_PIDX] = i
    const_f[:, C_TILE:C_TILE + CHOICES * NT] = np.tile(np.arange(NT) * P, CHOICES)[None, :]
    const_b = np.zeros((P, B_END), np.float32)
    const_b[:, B_UP:B_UP + P] = i[:, None] < i[None, :]
    const_b[:, B_ONE:B_ONE + P] = 1.0
    const_b[:, B_ID:B_ID + P] = np.eye(P)
    later = np.where(i[None, :] <= i[:, None], 0.0, NEG)
    const_b[:, B_MASK:B_MASK + 2 * P] = np.concatenate([later, later.T], 1)
    slopes = (2.0 ** (-2.0 ** (-(np.log2(HEADS) - 3)))) ** np.arange(1, HEADS + 1, dtype=np.float64)
    slopes = slopes.astype(np.float32).astype(np.float64)
    pos = np.arange(SEQ, dtype=np.float64)
    rows_q = np.concatenate([
        np.broadcast_to(bf16_parts(slopes)[:, :, None], (3, HEADS, SEQ)),
        bf16_parts(-slopes[:, None] * pos[None, :])]).astype(np.float32)
    rows_k = np.concatenate([np.tile(pos, (3, 1)), np.ones((6, SEQ))]).astype(np.float32)
    return {"const_f": const_f, "const_b": const_b, "rows_q": np.ascontiguousarray(rows_q), "rows_k": rows_k}


def build(nc, x_in, wqkv_in, wo_in, rw_in, rb_in, rbias_in, ew1, eb1, ew2, eb2, ew3, eb3,
          sw1, sb1, sw2, sb2, sw3, sb3, const_f, const_b, rows_q, rows_k, out):
    with ExitStack() as ctx:
        def sb(name, shape, dt=F32):
            return ctx.enter_context(nc.sbuf_tensor(name, shape, dt))

        sems = {}

        def sem(name):
            if name not in sems:
                sems[name] = ctx.enter_context(nc.semaphore(name))
            return sems[name]

        xn_dram = nc.dram_tensor("xn_dram", (TOKENS, DIM), F32).ap()
        y_dram = nc.dram_tensor("y_dram", (JOBS * P, DIM), F32).ap()
        b12_dram = nc.dram_tensor("b12_dram", (3, E + 2, 2 * INTER), BF16).ap()
        q_dram = nc.dram_tensor("q_dram", (2, 3, DIM, SEQ), BF16).ap()
        k_dram = nc.dram_tensor("k_dram", (2, 3, HD, SEQ), BF16).ap()
        m_dram = nc.dram_tensor("m_dram", (2, 3, QT * HEADS, P), BF16).ap()

        x = sb("x", [P, NT, DIM])
        w12 = sb("w12", [P, E, KC, 2 * INTER])
        w3 = sb("w3", [P, E, DIM])
        turns = sb("turns", [P, KC * (DIM + 2 * HD)])
        sw12 = turns[:, 0:KC * 2 * SHARED].rearrange("p (c f) -> p c f", c=KC)
        wqkv = turns[:].rearrange("p (c f) -> p c f", c=KC)
        turns2 = sb("turns2", [P, KC * DIM])
        sw3s = turns2[:, 0:SHARED // P * DIM].rearrange("p (c d) -> p c d", d=DIM)
        eb3x = turns2[0:E + 1, SHARED // P * DIM:SHARED // P * DIM + DIM]
        wo = turns2[:].rearrange("p (c d) -> p c d", d=DIM)
        rw = sb("rw", [P, KC, 2 * E])
        cf = sb("cf", [P, C_END])
        cb = sb("cb", [P, B_END], BF16)
        b12x = sb("b12x", [3, (E + 2) * 2 * INTER], BF16)
        rbc = sb("rbc", [P, 2, E])
        neghalf = sb("neghalf", [P, NT])
        mark = sb("mark", [P, 2])
        st = sb("st", [P, NT, 6])
        mv = sb("mv", [P, NT, 2])
        varE = sb("varE", [P, NT])
        rstd = sb("rstd", [P, NT])
        ident = cf[:, C_ID:C_ID + P]
        iota = cf[:, C_IOTA:C_IOTA + P]
        upper = cb[:, B_UP:B_UP + P]
        ones = cb[:, B_ONE:B_ONE + P]
        identb = cb[:, B_ID:B_ID + P]
        mask = cb[:, None, B_MASK:B_MASK + P].to_broadcast([P, 2, P])
        mask_t = cb[:, None, B_MASK + P:B_MASK + 2 * P].to_broadcast([P, 2, P])

        WORDS = 16960
        arena = sb("arena", [P, WORDS])
        used = {"ffn": 0, "att": 0}

        def view(kind, shape, dt=F32, at=None):
            n = int(np.prod(shape[1:]))
            words = n if dt != BF16 else (n + 1) // 2
            if at is None:
                at = used[kind]
                used[kind] += words
                assert used[kind] <= WORDS, (kind, used[kind])
            v = arena[0:shape[0], at:at + words]
            if dt != F32:
                v = v.bitcast(dt)
            if len(shape) == 2:
                return v
            names = "abcd"[:len(shape) - 1]
            return v.rearrange(f"p ({' '.join(names)}) -> p {' '.join(names)}",
                               **{c: s for c, s in zip(names, shape[1:])})

        xn = view("ffn", [P, NT, DIM])
        yg = view("ffn", [P, 4, CHOICES, DIM], at=0)
        xnT = view("ffn", [P, NT, KC, P])
        hv = view("ffn", [P, NT, CHOICES])
        slotu = view("ffn", [P, CHOICES, NT], U32)
        sg = view("ffn", [P, 2, SHARED])
        hh = view("ffn", [P, 2, SHARED])
        hT = view("ffn", [P, 2, SHARED])
        gateT = view("ffn", [E + 1, NT, P])
        early = used["ffn"]
        listu = view("ffn", [P, JP], U32)
        xg_at = used["ffn"]
        xg = view("ffn", [P, 2, DIM])
        xgT = view("ffn", [P, 2, KC, P])
        onehot_p = view("ffn", [P, CHOICES * NT, P], BF16, at=xg_at)
        onehot_j = view("ffn", [P, CHOICES * NT, 2, JP], BF16, at=xg_at + CHOICES * NT * P // 2)
        jcmp = view("ffn", [1, JP, E], at=xg_at + CHOICES * NT * P // 2 + CHOICES * NT * JP)
        ysb = view("ffn", [P, 2, DIM])
        lgT = view("ffn", [P, 2 * P])
        lg = view("ffn", [P, NT, E])
        sc = view("ffn", [P, NT, E])
        t16 = view("ffn", [P, NT, E])
        red = view("ffn", [P, NT])
        gm8 = view("ffn", [P, NT, 8])
        gtop = view("ffn", [P, NT, 8])
        gidx = view("ffn", [P, NT, 8], U32)
        etop = view("ffn", [P, NT, 8])
        eidx = view("ffn", [P, NT, 8], U32)
        idxf = view("ffn", [P, NT, 2])
        keep = view("ffn", [P, NT, GROUPS])
        keep2 = view("ffn", [P, NT, GROUPS])
        oh = view("ffn", [P, CHOICES, NT, E])
        taken = view("ffn", [P, NT, E], BF16)
        gate = view("ffn", [P, NT, E + 1])
        cnt = view("ffn", [P, 4, E])
        cnti = view("ffn", [P, E], I32)
        slot = view("ffn", [P, CHOICES, NT])
        sloti = view("ffn", [P, CHOICES, NT], I32)
        sji = view("ffn", [P, 2, CHOICES * NT], I32)
        sjf = view("ffn", [P, 2, CHOICES * NT])
        listf = view("ffn", [P, JP])
        jexf = view("ffn", [1, JP])
        jex = view("ffn", [1, JP], I32)
        jm = view("ffn", [1, 1], I32)
        qside = view("att", [P, 2, HEADS, SEQ], BF16)
        kT = view("att", [P, 2, SEQ], BF16)
        attn = view("att", [P, QT, HEADS * HD])
        aT = view("att", [P, KC, P])
        oT = view("att", [P, SEQ])
        rec = view("att", [P, QT, 4])
        m3 = view("att", [P, HEADS, 3])
        nm = view("att", [P, QT, HEADS])
        mr = view("att", [QT * HEADS, P])
        mp = view("att", [QT * HEADS, 3, P], BF16)
        pr = view("att", [P, 2, 2, 3 * 2 * P])
        qp_at = used["att"] - 3 * 2 * P * 2
        assert qp_at >= early
        qp = view("att", [P, 3, KC, SEQ], BF16, at=qp_at)
        xaT = view("att", [P, KC, SEQ])
        qr = view("att", [P, SEQ])
        kp = view("att", [HD, 3, SEQ], BF16)
        kr = qr[0:HD, :]
        kvT = view("att", [2 * HD, SEQ])
        vv = view("att", [P, 2, QT, 32])
        xa = view("att", [P, QT, DIM])

        ps = ctx.enter_context(nc.psum_tensor("ps", [P, 8, 512], F32))
        PS_GU, PS_HT, PS_Y, PS_XT, PS_MISC = 0, 2, 3, 5, 7
        ps_logit = ps[:, PS_MISC, 0:256].rearrange("p (c j e) -> p j c e", c=2, j=NT // 2)[:, :, :, 0:E]
        ps_rank = ps[:, PS_MISC, 256:384].rearrange("p (t e) -> p t e", e=E)
        ps_count = ps[:, PS_MISC, 384:384 + E]
        ps_list = ps[:, PS_MISC, 416:416 + 2 * JP]
        PS_ST, PS_S, PS_O, PS_A = 0, 4, 6, 7

        def bc(ap, shape):
            return ap.to_broadcast(shape)

        b12f = hT[0:E + 2, 0, :]
        b12p = ysb[0:E + 2, 0, 0:3 * INTER].bitcast(BF16).rearrange("p (k f) -> p k f", k=3)

        block = ctx.enter_context(nc.Block())

        def ffn_sp(f):
            for t in range(NT):
                sp_ = nc.sync
                sp_.wait_ge(sem(f"xn{f}"), t + 1)
                sp_.dma_start(xn_dram[t * P:(t + 1) * P, :], xn[:, t, :]).then_inc(sem(f"xn_out{f}"), 16)
            if f == 1:
                nc.sync.wait_ge(sem("a_wo"), NT)
                nc.sync.dma_start(sw3s, sw3.rearrange("(c p) d -> p c d", p=P)).then_inc(sem("sw3_back"), 16)
                nc.sync.dma_start(eb3x[0:E, :], eb3).then_inc(sem("sw3_back"), 16)
                nc.sync.dma_start(eb3x[E:E + 1, :], sb3.rearrange("(a d) -> a d", a=1)).then_inc(sem("sw3_back"), 16)

            if f == 0:
                for e in range(0, E, EG):
                    for part, w in ((0, ew1), (1, ew2)):
                        nc.sync.dma_start(w12[:, e:e + EG, :, part * INTER:(part + 1) * INTER].rearrange("p e c f -> p (e c) f"),
                                          w[e:e + EG].rearrange("e (c p) f -> p (e c) f", p=P)).then_inc(sem("ew_in"), 16)
                    nc.sync.dma_start(w3[:, e:e + EG, :], ew3[e:e + EG].rearrange("e p d -> p e d")).then_inc(sem("ew_in"), 16)

            def store(j, par):
                nc.sync.wait_ge(sem(f"y_sb{f}"), j + 1)
                nc.sync.dma_start(y_dram[ds(j * P, P), :], ysb[:, par, :]).then_inc(sem(f"y_out{f}_{par}"), 16)
            nc.sync.wait_ge(sem(f"jex{f}"), 1)
            pairs = nc.sync.value_load(jm[:], min_val=JOBS_LEAST // 2, max_val=JOBS // 2)
            if f == 0:
                first_spare = JOBS_LEAST + 1
                with nc.sync.Fori(0, (JOBS - first_spare) // 2) as i:
                    store(2 * i, 0)
                    store(2 * i + 1, 1)
                    nc.sync.dma_start(y_dram[ds((2 * i + first_spare) * P, 2 * P), :], x_in[0:2 * P, :]).then_inc(sem("y_spare"), 16)
                nc.sync.wait_ge(sem("y_spare"), 16 * ((JOBS - first_spare) // 2))
                with nc.sync.Fori((JOBS - first_spare) // 2, pairs) as i:
                    store(2 * i, 0)
                    store(2 * i + 1, 1)
            else:
                with nc.sync.Fori(0, pairs) as i:
                    store(2 * i, 0)
                    store(2 * i + 1, 1)
            store(2 * pairs, 0)
            if f == 0:
                nc.sync.wait_ge(sem("s_gu0"), NT)
                nc.sync.dma_start(wqkv, wqkv_in.rearrange("(c p) n -> p c n", p=P)).then_inc(sem("wqkv_in"), 16)
                nc.sync.wait_ge(sem("s_z0"), NT)
                nc.sync.wait_ge(sem("c0"), NT)
                nc.sync.dma_start(wo, wo_in.rearrange("(c p) n -> p c n", p=P)).then_inc(sem("wo_in"), 16)

        def att_sp():
            def q_rows(b):
                p = b % 2
                nc.sync.wait_ge(sem("q_parts"), 3 * KC * (b + 1))
                for k in range(3):
                    nc.sync.dma_start(q_dram[p, k].rearrange("(c p) t -> p c t", p=P), qp[:, k]).then_inc(sem(f"q_out{p}"), 16)
                nc.sync.wait_ge(sem("k_parts"), 3 * (b + 1))
                nc.sync.dma_start(k_dram[p].rearrange("k d t -> d k t"), kp[:]).then_inc(sem(f"q_out{p}"), 16)
                nc.sync.wait_ge(sem(f"q_out{p}"), 64 * (b // 2 + 1))
                if b >= 2:
                    nc.sync.wait_ge(sem("st_done"), HEADS // 2 * (b - 1))
                if b == 0:
                    nc.sync.wait_ge(sem("comb0"), NT)
                for r in range(6):
                    nc.sync.dma_start(qside[r * HD:(r + 1) * HD, p],
                                      q_dram[p, QPART[r]].rearrange("(h d) t -> d h t", d=HD)).then_inc(sem(f"q_in{p}"), 16)
                    nc.sync.dma_start(kT[r * HD:(r + 1) * HD, p], k_dram[p, KPART[r]]).then_inc(sem(f"q_in{p}"), 16)

            def m_rows(b):
                p = b % 2
                nc.sync.wait_ge(sem("m_parts"), 3 * (b + 1))
                nc.sync.dma_start(m_dram[p].rearrange("k r q -> r k q"), mp[:]).then_inc(sem(f"m_out{p}"), 16)
                nc.sync.wait_ge(sem(f"m_out{p}"), 16 * (b // 2 + 1))
                for q in range(QT):
                    nc.sync.dma_start(qside[R_MAX:ROWS, p, :, q * P:(q + 1) * P],
                                      m_dram[p, :, q * HEADS:(q + 1) * HEADS, :]).then_inc(sem(f"m_in{p}"), 16)

            q_rows(0)
            q_rows(1)
            m_rows(0)
            for b in range(BATCH):
                if b + 1 < BATCH:
                    m_rows(b + 1)
                if b + 2 < BATCH:
                    q_rows(b + 2)
                if b + 3 == BATCH:
                    nc.sync.wait_ge(sem("a_k"), BATCH)
                    nc.sync.dma_start(sw12[:, :, 0:SHARED], sw1.rearrange("(c p) f -> p c f", p=P)).then_inc(sem("sw_back"), 16)
                    nc.sync.dma_start(sw12[:, :, SHARED:], sw2.rearrange("(c p) f -> p c f", p=P)).then_inc(sem("sw_back"), 16)

        @block.sync
        def _(sp):
            for n in range(0, NT, 2):
                sp.dma_start(x[:, n:n + 2, :], x_in[n * P:(n + 2) * P, :].rearrange("(t p) d -> p t d", p=P)).then_inc(sem(f"x_in{n // 2}"), 16)
            sp.dma_start(cf[:], const_f).then_inc(sem("small_in"), 16)
            sp.wait_ge(sem("pool_set"), 1)
            sp.dma_start(rw[:, :, 0:E], rw_in.rearrange("(c p) e -> p c e", p=P)).then_inc(sem("small_in"), 16)
            sp.dma_start(rbc[:, 0, :], rb_in.partition_broadcast(P)).then_inc(sem("small_in"), 16)
            sp.dma_start(rbc[:, 1, :], rbias_in.partition_broadcast(P)).then_inc(sem("small_in"), 16)
            sp.dma_start(eb3x[0:E, :], eb3).then_inc(sem("small_in"), 16)
            sp.dma_start(eb3x[E:E + 1, :], sb3.rearrange("(a d) -> a d", a=1)).then_inc(sem("small_in"), 16)
            sp.dma_start(b12f[0:E, 0:INTER], eb1).then_inc(sem("bias_in"), 16)
            sp.dma_start(b12f[0:E, INTER:2 * INTER], eb2).then_inc(sem("bias_in"), 16)
            sp.dma_start(b12f[E:E + 1, :], sb1.rearrange("(a d) -> a d", a=1)).then_inc(sem("bias_in"), 16)
            sp.dma_start(b12f[E + 1:E + 2, :], sb2.rearrange("(a d) -> a d", a=1)).then_inc(sem("bias_in"), 16)
            sp.wait_ge(sem("bias_split"), 5)
            sp.dma_start(b12_dram.rearrange("k e f -> e k f"), b12p).then_inc(sem("bias_out"), 16)
            sp.wait_ge(sem("bias_out"), 16)
            sp.dma_start(b12x[:], b12_dram.rearrange("k e f -> k (e f)")).then_inc(sem("bias_out"), 16)
            ffn_sp(0)
            att_sp()
            ffn_sp(1)
            for t in range(NT):
                sp.wait_ge(sem("comb1"), t + 1)
                sp.wait_ge(sem("biased1"), t + 1)
                sp.dma_start(out[t * P:(t + 1) * P, :], x[:, t, :]).then_inc(sem("stored"), 16)
            sp.wait_ge(sem("stored"), 16 * NT)


        def bias_split(steps):
            pool = nc.gpsimd
            for n in steps:
                if n == 0:
                    pool.wait_ge(sem("bias_in"), 64)
                else:
                    pool.wait_ge(sem("bias_split"), n)
                if n % 2 == 0:
                    pool.tensor_copy(b12p[:, n // 2, :], b12f).then_inc(sem("bias_split"), 1)
                else:
                    pool.tensor_tensor(b12f, b12f, b12p[:, n // 2, :], ALU.subtract).then_inc(sem("bias_split"), 1)

        def ffn_pool(f):
            pool = nc.gpsimd
            for n in range(2):
                pool.wait_ge(sem(f"var{f}"), n + 1)
                half = slice(n * NT // 2, (n + 1) * NT // 2)
                pool.tensor_tensor(rstd[:, half], varE[:, half], neghalf[:, half], ALU.pow).then_inc(sem(f"rstd{f}"), 1)
                if f == 0:
                    bias_split((0, 1) if n == 0 else (2, 3, 4))
            pool.wait_ge(sem(f"list{f}"), 1)
            pool.wait_ge(sem(f"xn_out{f}"), 16 * NT)
            pairs = pool.value_load(jm[:], min_val=JOBS_LEAST // 2, max_val=JOBS // 2)

            def gather(j):
                if j >= 2:
                    pool.wait_ge(sem(f"xgt{f}"), j - 1)
                pool.indirect_dma_start(xg[:, j % 2, :], None, xn_dram,
                                        bass.IndirectOffsetOnAxis(ap=listu[:, j:j + 1], axis=0)).then_inc(sem(f"xg{f}_{j % 2}"), 16)
            for j in range(JOBS_LEAST + 2):
                gather(j)
            for i in range(JOBS_LEAST // 2 + 1, JOBS // 2 + 1):
                with pool.If_lt(pool.to_reg(i - 1), pool.to_reg(pairs)):
                    gather(2 * i)
                    gather(2 * i + 1)
            pool.wait_ge(sem(f"y_all{f}"), 2)
            for t in range(NT):
                if t >= 4:
                    pool.wait_ge(sem(f"comb{f}"), t - 3)
                for c in range(CHOICES):
                    pool.indirect_dma_start(yg[:, t % 4, c, :], None, y_dram,
                                            bass.IndirectOffsetOnAxis(ap=slotu[:, c, t:t + 1], axis=0)).then_inc(sem(f"yg{f}_{t % 4}"), 16)
                if f == 0 and t == 3:
                    att_rstd(0)
            if f == 0:
                for b in range(1, BATCH):
                    att_rstd(b)

        def att_rstd(b):
            nc.gpsimd.wait_ge(sem("a_var"), b + 1)
            nc.gpsimd.tensor_tensor(rstd[:, 2 * b:2 * b + 2], varE[:, 2 * b:2 * b + 2], neghalf[:, 0:2], ALU.pow).then_inc(sem("a_rstd"), 1)

        def att_pool():
            pool = nc.gpsimd
            pool.wait_ge(sem("comb0"), NT)
            for p in range(2):
                pool.dma_start(qside[R_ALIBI:R_MAX, p], rows_q).then_inc(sem("rows_in"), 16)
                pool.dma_start(kT[R_ALIBI:ROWS, p], rows_k).then_inc(sem("rows_in"), 16)
        @block.gpsimd
        def _(pool):
            pool.memset(rw[:], 0.0).then_inc(sem("pool_set"), 1)
            pool.dma_start(cb[:], const_b).then_inc(sem("cb_in"), 16)
            pool.memset(neghalf[:], -0.5).then_inc(sem("pool_set"), 1)
            pool.wait_ge(sem("pool_set"), 2)
            ffn_pool(0)
            att_pool()
            ffn_pool(1)


        def ffn_act(f):
            act = nc.scalar
            for t in range(NT):
                act.wait_ge(sem(f"xt{f}"), t + 1)
                act.copy(xnT[:, t].rearrange("p c q -> p (c q)"), ps[:, PS_XT + t % 2, :]).then_inc(sem(f"xnT{f}"), 1)
            act.wait_ge(sem(f"lt{f}"), 1)
            act.copy(lgT[:], ps[:, PS_XT, 0:2 * P]).then_inc(sem(f"lgT{f}"), 1)
            act.wait_ge(sem(f"lg{f}"), 1)
            act.activation(t16[:].rearrange("p t e -> p (t e)"), lg[:].rearrange("p t e -> p (t e)"), ACT.Exp).then_inc(sem(f"rexp{f}"), 1)
            def shared(first, last):
                for t in range(first, last + 1):
                    if t > first:
                        act.wait_ge(sem(f"s_ht{f}"), t)
                        act.copy(hT[:, (t - 1) % 2, :], ps[:, PS_HT, SHARED * ((t - 1) % 2):SHARED * ((t - 1) % 2 + 1)]).then_inc(sem(f"s_hT{f}"), 1)
                    if t == 4 and first == 0:
                        for n in range(2):
                            act.wait_ge(sem(f"gt{f}"), n + 1)
                            act.copy(gateT[:, 4 * n:4 * n + 4, :].rearrange("e t q -> e (t q)"), ps[0:E + 1, PS_XT + n, :]).then_inc(sem(f"gateT{f}"), 1)
                    if t < last:
                        act.wait_ge(sem(f"s_gu{f}"), t + 1)
                        act.activation(sg[:, t % 2, :], ps[:, PS_GU + t % 2, 0:SHARED], ACT.Silu).then_inc(sem(f"s_silu{f}"), 1)

            shared(0, FIRST)

            def gather_copy(j, par):
                act.wait_ge(sem(f"xgt{f}"), j + 1)
                act.copy(xgT[:, par].rearrange("p c q -> p (c q)"), ps[:, PS_XT + par, :]).then_inc(sem(f"xgT{f}"), 1)

            def silu(j, par):
                act.wait_ge(sem(f"gu{f}"), j + 1)
                act.activation(sg[:, par, 0:INTER], ps[:, PS_GU + par, 0:INTER], ACT.Silu).then_inc(sem(f"silu{f}"), 1)

            def h_copy(j, par):
                act.wait_ge(sem(f"ht{f}"), j + 1)
                act.copy(hT[:, par, 0:INTER], ps[:, PS_HT, P * par:P * par + P]).then_inc(sem(f"hT{f}"), 1)

            def body(j, par):
                h_copy(j - 1, 1 - par)
                silu(j, par)
                gather_copy(j + 1, 1 - par)
            act.wait_ge(sem(f"jex{f}"), 1)
            pairs = act.value_load(jm[:], min_val=JOBS_LEAST // 2, max_val=JOBS // 2)
            gather_copy(0, 0)
            silu(0, 0)
            gather_copy(1, 1)
            with act.Fori(0, pairs) as i:
                body(2 * i + 1, 1)
                body(2 * i + 2, 0)
            h_copy(2 * pairs, 0)
            shared(FIRST, NT)

        def att_act():
            act = nc.scalar

            def qkv(b):
                for c in range(4):
                    act.wait_ge(sem("a_xt"), 4 * b + c + 1)
                    act.copy(xaT[:, :, (c // 2) * P:(c // 2 + 1) * P][:, 2 * (c % 2):2 * (c % 2) + 2, :],
                             ps[:, PS_ST + c % 4, 0:2 * P].rearrange("p (c q) -> p c q", c=2)).then_inc(sem("a_xaT"), 1)
                if b >= 1:
                    act.wait_ge(sem(f"q_out{(b - 1) % 2}"), 64 * ((b - 1) // 2 + 1))
                for c in range(KC):
                    act.wait_ge(sem("a_q"), KC * b + c + 1)
                    act.copy(qp[:, 0, c, :], ps[:, PS_ST + c, 0:SEQ]).then_inc(sem("q1"), 1)
                act.wait_ge(sem("a_k"), b + 1)
                act.mul(kp[:, 0, :], ps[0:HD, PS_S, 0:SEQ], HD ** -0.5).then_inc(sem("k1"), 1)
                act.copy(kvT[:], ps[0:2 * HD, PS_S, 0:SEQ]).then_inc(sem("kvT"), 1)

            def out_proj(b):
                for q in range(QT):
                    act.wait_ge(sem("a_at"), QT * b + q + 1)
                    if q >= 1 or b >= 1:
                        act.wait_ge(sem("a_wo"), QT * b + q)
                    act.copy(aT[:].rearrange("p c q -> p (c q)"), ps[:, PS_A, :]).then_inc(sem("a_aT"), 1)

            def outputs(n):
                act.wait_ge(sem("pv"), n + 1)
                if not (type(n) is int and n < 1):
                    act.wait_ge(sem("ot"), n)
                act.copy(oT[:], ps[:, PS_O, 0:SEQ]).then_inc(sem("oT"), 1)

            def quad(b, q, par, lag):
                n = 8 * b + q
                if not (type(n) is int and n < 2):
                    act.wait_ge(sem("pv"), n - 1)
                act.wait_ge(sem("st_done"), 2 * n + 1)
                act.activation(pr[:, par, 0, :], ps[:, PS_ST:PS_ST + 2, :].rearrange("p a b -> p (a b)")[:, 0:768], ACT.Exp).then_inc(sem("exp"), 1)
                if lag:
                    outputs(n - 1)
                act.wait_ge(sem("st_done"), 2 * n + 2)
                act.activation(pr[:, par, 1, :], ps[:, PS_ST + 2:PS_ST + 4, :].rearrange("p a b -> p (a b)")[:, 0:768], ACT.Exp).then_inc(sem("exp"), 1)

            qkv(0)
            qkv(1)
            for b in range(BATCH):
                nb = min(b + 1, BATCH - 1)
                act.wait_ge(sem(f"q_out{nb % 2}"), 64 * (nb // 2 + 1))
                quad(b, 0, 0, False)
                quad(b, 1, 1, True)
                with act.Fori(1, HEADS // 8) as i:
                    for par in range(2):
                        quad(b, 2 * i + par, par, True)
                outputs(8 * b + 7)
                if b + 2 < BATCH:
                    qkv(b + 2)
                out_proj(b)

        @block.scalar
        def _(act):
            act.wait_ge(sem("x_in2"), 16)
            act.dma_start(sw12[:, :, 0:SHARED], sw1.rearrange("(c p) f -> p c f", p=P)).then_inc(sem("sw_in"), 16)
            act.dma_start(sw12[:, :, SHARED:], sw2.rearrange("(c p) f -> p c f", p=P)).then_inc(sem("sw_in"), 16)
            act.dma_start(sw3s[:], sw3.rearrange("(c p) d -> p c d", p=P)).then_inc(sem("sw_in"), 16)
            ffn_act(0)
            att_act()
            ffn_act(1)


        def ffn_dve(f):
            dve = nc.vector
            count = [0]
            chain = sem(f"chain{f}")

            def link(ins):
                count[0] += 1
                ins.then_inc(chain, 1)
                dve.wait_ge(chain, count[0])

            half = NT // 2
            for n in range(2):
                if f == 0:
                    for t in range(n * half, (n + 1) * half):
                        if t % 2 == 0:
                            dve.wait_ge(sem(f"x_in{t // 2}"), 16)
                        ins = dve.bn_stats(st[:, t, :], x[:, t, :])
                    link(ins)
                elif n == 0:
                    dve.wait_ge(sem("stats"), NT)
                for t in range(n * half, (n + 1) * half):
                    ins = dve.bn_aggr(mv[:, t, :], st[:, t, :])
                link(ins)
                dve.tensor_scalar(varE[:, n * half:(n + 1) * half], mv[:, n * half:(n + 1) * half, 1], EPS, None, ALU.add).then_inc(sem(f"var{f}"), 1)
            for t in range(NT):
                if t % half == 0:
                    dve.wait_ge(sem(f"rstd{f}"), t // half + 1)
                dve.tensor_scalar(xn[:, t, :], x[:, t, :], mv[:, t, 0:1], rstd[:, t:t + 1],
                                  ALU.subtract, ALU.mult).then_inc(sem(f"xn{f}"), 1)
            def logits():
                if f == 0:
                    dve.wait_ge(sem("small_in"), 96)
                dve.wait_ge(sem(f"logit{f}"), 1)
                link(dve.tensor_tensor(lg[:].rearrange("p (j c) e -> p j c e", c=2), ps_logit,
                                       bc(rbc[:, 0:1, None, :], [P, NT // 2, 2, E]), ALU.add))
                link(dve.tensor_reduce(red[:], lg[:], AX_X, ALU.max))
                dve.tensor_tensor(lg[:], lg[:], bc(red[:, :, None], [P, NT, E]), ALU.subtract).then_inc(sem(f"lg{f}"), 1)

            def scores():
                dve.wait_ge(sem(f"rexp{f}"), 1)
                link(dve.tensor_reduce(red[:], t16[:], AX_X, ALU.add))
                link(dve.reciprocal(red[:], red[:]))
                link(dve.tensor_tensor(t16[:], t16[:], bc(red[:, :, None], [P, NT, E]), ALU.mult))
                link(dve.tensor_tensor(sc[:], t16[:], bc(rbc[:, 1:2, :], [P, NT, E]), ALU.add))

            def groups():
                link(dve.memset(gm8[:], -3e38))
                link(dve.tensor_reduce(gm8[:, :, 0:GROUPS], sc[:].rearrange("p t (g j) -> p t g j", g=GROUPS), AX_X, ALU.max))
                for t in range(NT):
                    ins = dve.max(gtop[:, t, :], gm8[:, t, :])
                link(ins)
                for t in range(NT):
                    ins = dve.max_index(gidx[:, t, :], gtop[:, t, :], gm8[:, t, :])
                link(ins)
                link(dve.tensor_copy(idxf[:], gidx[:, :, 0:2]))
                iota4 = bc(iota[:, None, 0:GROUPS], [P, NT, GROUPS])
                dve.tensor_tensor(keep[:], iota4, bc(idxf[:, :, 0:1], [P, NT, GROUPS]), ALU.is_equal)
                link(dve.tensor_tensor(keep2[:], iota4, bc(idxf[:, :, 1:2], [P, NT, GROUPS]), ALU.is_equal))
                link(dve.tensor_tensor(keep[:], keep[:], keep2[:], ALU.add))
                link(dve.tensor_scalar(keep[:], keep[:], -NEG, NEG, ALU.mult, ALU.add))
                link(dve.tensor_tensor(t16[:].rearrange("p t (g j) -> p t g j", g=GROUPS),
                                       sc[:].rearrange("p t (g j) -> p t g j", g=GROUPS),
                                       bc(keep[:, :, :, None], [P, NT, GROUPS, E // GROUPS]), ALU.add))

            def experts():
                for t in range(NT):
                    ins = dve.max(etop[:, t, :], t16[:, t, :])
                link(ins)
                for t in range(NT):
                    ins = dve.max_index(eidx[:, t, :], etop[:, t, :], t16[:, t, :])
                link(ins)
                link(dve.tensor_copy(idxf[:], eidx[:, :, 0:2]))
                dve.tensor_scalar(hv[:], etop[:, :, 0:CHOICES], 0.5, None, ALU.mult)
                iota16 = bc(iota[:, None, 0:E], [P, NT, E])
                dve.tensor_tensor(oh[:, 0], iota16, bc(idxf[:, :, 0:1], [P, NT, E]), ALU.is_equal)
                link(dve.tensor_tensor(oh[:, 1], iota16, bc(idxf[:, :, 1:2], [P, NT, E]), ALU.is_equal))
                dve.tensor_tensor(taken[:], oh[:, 0], oh[:, 1], ALU.add).then_inc(sem(f"taken{f}"), 1)

            def gates():
                dve.memset(gate[:], 1.0)
                dve.tensor_tensor(t16[:], oh[:, 1], bc(etop[:, :, 1:2], [P, NT, E]), ALU.mult)
                link(dve.tensor_tensor(lg[:], oh[:, 0], bc(etop[:, :, 0:1], [P, NT, E]), ALU.mult))
                dve.tensor_tensor(gate[:, :, 0:E], lg[:], t16[:], ALU.add).then_inc(sem(f"gate{f}"), 1)

            def slots(between):
                dve.wait_ge(sem(f"rank{f}"), 1)
                link(dve.tensor_scalar(cnti[:], ps_count, float(P - 1), None, ALU.add))
                link(dve.tensor_scalar(cnti[:], cnti[:], P.bit_length() - 1, None, ALU.arith_shift_right))
                link(dve.tensor_copy(cnt[:, 0, :], cnti[:]))
                link(dve.tensor_copy(cnt[:, 1, :], cnti[:]))
                a, b, s = 1, 2, 1
                while s < E:
                    dve.tensor_copy(cnt[:, b, 0:s], cnt[:, a, 0:s])
                    link(dve.tensor_tensor(cnt[:, b, s:], cnt[:, a, s:], cnt[:, a, 0:E - s], ALU.add))
                    a, b, s = b, a, 2 * s
                end = cnt[0:1, a, :]
                link(dve.tensor_copy(jm[:], end[:, E - 1:E]))
                link(dve.tensor_scalar(jm[:], jm[:], 1, None, ALU.arith_shift_right))
                link(dve.tensor_tensor(jcmp[:], bc(end[:, None, :], [1, JP, E]), bc(iota[0:1, 0:JP, None], [1, JP, E]), ALU.is_le))
                link(dve.tensor_reduce(jexf[:], jcmp[:], AX_X, ALU.add))
                dve.tensor_scalar(jex[:], jexf[:], float(E - 1), None, ALU.min).then_inc(sem(f"jex{f}"), 1)
                link(dve.tensor_tensor(cnt[:, 3, :], cnt[:, a, :], cnt[:, 0, :], ALU.subtract))
                link(dve.tensor_scalar(cnt[:, 3, :], cnt[:, 3, :], float(P), None, ALU.mult))
                link(dve.tensor_tensor(t16[:], ps_rank, bc(cnt[:, 3:4, :], [P, NT, E]), ALU.add))
                for c in range(CHOICES):
                    ins = dve.tensor_tensor(oh[:, c], oh[:, c], t16[:], ALU.mult)
                link(ins)
                link(dve.tensor_reduce(slot[:].rearrange("p c t -> p (c t)"), oh[:].rearrange("p c t e -> p (c t) e"), AX_X, ALU.add))
                dve.tensor_copy(slotu[:], slot[:])
                link(dve.tensor_copy(sloti[:], slot[:]))
                si = sloti[:].rearrange("p c t -> p (c t)")
                dve.tensor_scalar(sji[:, 0, :], si, P.bit_length() - 1, None, ALU.arith_shift_right)
                link(dve.tensor_scalar(sji[:, 1, :], si, P - 1, None, ALU.bitwise_and))
                link(dve.tensor_copy(sjf[:], sji[:]))
                between()
                n = CHOICES * NT
                dve.tensor_tensor(onehot_p[:], bc(iota[:, None, :], [P, n, P]), bc(sjf[:, 1, :, None], [P, n, P]), ALU.is_equal)
                link(dve.tensor_tensor(onehot_j[:, :, 1, :], bc(iota[:, None, 0:JP], [P, n, JP]), bc(sjf[:, 0, :, None], [P, n, JP]), ALU.is_equal))
                link(dve.tensor_scalar(onehot_j[:, :, 0, :], onehot_j[:, :, 1, :], cf[:, C_PIDX:C_PIDX + 1], None, ALU.mult))
                dve.tensor_tensor(onehot_j[:, :, 1, :], onehot_j[:, :, 1, :], bc(cf[:, C_TILE:C_TILE + n, None], [P, n, JP]),
                                  ALU.mult).then_inc(sem(f"onehot{f}"), 1)

            def token_list():
                dve.wait_ge(sem(f"listed{f}"), 1)
                link(dve.tensor_copy(listf[:], ps_list[:, 0:JP]))
                dve.tensor_tensor(listu[:], listf[:], ps_list[:, JP:], ALU.add).then_inc(sem(f"list{f}"), 1)

            def shared_h(t):
                dve.wait_ge(sem(f"s_silu{f}"), t + 1)
                dve.tensor_tensor(hh[:, t % 2, :], ps[:, PS_GU + t % 2, SHARED:], sg[:, t % 2, :], ALU.mult).then_inc(sem(f"s_h{f}"), 1)

            def shared_x(t):
                dve.wait_ge(sem(f"s_z{f}"), t + 1)
                dve.scalar_tensor_tensor(out=x[:, t, :], in0=ps[:, PS_Y + t % 2, :], scalar=0.5, in1=x[:, t, :],
                                         op0=ALU.mult, op1=ALU.add).then_inc(sem(f"s_x{f}"), 1)

            def pairs_x(t):
                dve.wait_ge(sem(f"yg{f}_{t % 4}"), 32 * (t // 4 + 1))
                dve.wait_ge(sem(f"biased{f}"), t + 1)
                link(dve.scalar_tensor_tensor(out=x[:, t, :], in0=yg[:, t % 4, 0, :], scalar=hv[:, t, 0:1], in1=x[:, t, :],
                                              op0=ALU.mult, op1=ALU.add))
                dve.scalar_tensor_tensor(out=x[:, t, :], in0=yg[:, t % 4, 1, :], scalar=hv[:, t, 1:2], in1=x[:, t, :],
                                         op0=ALU.mult, op1=ALU.add).then_inc(sem(f"comb{f}"), 1)

            def biases_x(t):
                dve.wait_ge(sem(f"c{f}"), t + 1)
                dve.wait_ge(sem(f"s_x{f}"), t + 1)
                dve.scalar_tensor_tensor(out=x[:, t, :], in0=ps[:, PS_XT + t % 3, :], scalar=0.5, in1=x[:, t, :],
                                         op0=ALU.mult, op1=ALU.add).then_inc(sem(f"biased{f}"), 1)

            logits()
            shared_h(0)
            scores()
            groups()
            shared_h(1)
            shared_x(0)
            experts()
            shared_h(2)
            shared_x(1)
            gates()
            shared_h(3)
            shared_x(2)
            slots(lambda: (shared_h(4), shared_x(3)))
            shared_h(5)
            shared_x(4)
            token_list()
            shared_x(5)

            def gated(j, par):
                dve.wait_ge(sem(f"silu{f}"), j + 1)
                dve.tensor_tensor(hh[:, par, 0:INTER], ps[:, PS_GU + par, INTER:2 * INTER], sg[:, par, 0:INTER], ALU.mult).then_inc(sem(f"h{f}"), 1)

            def rows_out(j, par, first=False):
                dve.wait_ge(sem(f"y{f}"), j + 1)
                if not first:
                    dve.wait_ge(sem(f"y_out{f}_{par}"), first_stores(j, par))
                dve.tensor_copy(ysb[:, par, :], ps[:, PS_Y + par, :]).then_inc(sem(f"y_sb{f}"), 1)

            def first_stores(j, par):
                return 8 * (j - par)

            gated(0, 0)
            gated(1, 1)
            rows_out(0, 0, first=True)
            gated(2, 0)
            rows_out(1, 1, first=True)
            dve.wait_ge(sem(f"jex{f}"), 1)
            pairs = dve.value_load(jm[:], min_val=JOBS_LEAST // 2, max_val=JOBS // 2)
            with dve.Fori(0, pairs - 1) as i:
                gated(2 * i + 3, 1)
                rows_out(2 * i + 2, 0)
                gated(2 * i + 4, 0)
                rows_out(2 * i + 3, 1)
            rows_out(2 * pairs, 0)
            biases_x(0)
            biases_x(1)
            dve.wait_ge(sem(f"y_out{f}_1"), 16 * pairs)
            dve.tensor_copy(mark[:, 1:2], neghalf[:, 0:1]).then_inc(sem(f"y_all{f}"), 1)
            dve.wait_ge(sem(f"y_out{f}_0"), 16 * pairs + 16)
            dve.tensor_copy(mark[:, 0:1], neghalf[:, 0:1]).then_inc(sem(f"y_all{f}"), 1)
            biases_x(2)
            pairs_x(0)
            shared_h(6)
            pairs_x(1)
            biases_x(3)
            if f == 0:
                att_stats(0)
            shared_h(7)
            pairs_x(2)
            biases_x(4)
            shared_x(6)
            pairs_x(3)
            if f == 0:
                att_norm(0)
            biases_x(5)
            shared_x(7)
            biases_x(6)
            biases_x(7)
            if f == 0:
                att_stats(1)
            for t in range(4, NT):
                pairs_x(t)
                if f == 0 and t % 2 == 1:
                    att_stats(t // 2)


        chain_a = [0]

        def link_a(ins):
            chain_a[0] += 1
            ins.then_inc(sem("chain_a"), 1)
            nc.vector.wait_ge(sem("chain_a"), chain_a[0])

        def att_stats(b):
            dve = nc.vector
            dve.wait_ge(sem("comb0"), 2 * b + 2)
            dve.wait_ge(sem("biased0"), 2 * b + 2)
            dve.bn_stats(st[:, 2 * b, :], x[:, 2 * b, :])
            link_a(dve.bn_stats(st[:, 2 * b + 1, :], x[:, 2 * b + 1, :]))
            dve.bn_aggr(mv[:, 2 * b, :], st[:, 2 * b, :])
            link_a(dve.bn_aggr(mv[:, 2 * b + 1, :], st[:, 2 * b + 1, :]))
            dve.tensor_scalar(varE[:, 2 * b:2 * b + 2], mv[:, 2 * b:2 * b + 2, 1], EPS, None, ALU.add).then_inc(sem("a_var"), 1)

        def att_norm(b):
            dve = nc.vector
            dve.wait_ge(sem("a_rstd"), b + 1)
            if b >= 1:
                dve.wait_ge(sem("a_xt"), 4 * b)
            for q in range(QT):
                t = QT * b + q
                dve.tensor_scalar(xa[:, q, :], x[:, t, :], mv[:, t, 0:1], rstd[:, t:t + 1],
                                  ALU.subtract, ALU.mult).then_inc(sem("a_xn"), 1)

        def att_dve():
            dve = nc.vector
            link = link_a

            link(dve.memset(vv[:], 0.0))
            link(dve.memset(vv[:, :, :, HD:HD + 1], 1.0))

            def qkv(b):
                for c in range(KC):
                    dve.wait_ge(sem("q1"), KC * b + c + 1)
                    dve.wait_ge(sem("q_parts"), 3 * (KC * b + c))
                    link(dve.tensor_tensor(qr[:], ps[:, PS_ST + c, 0:SEQ], qp[:, 0, c, :], ALU.subtract))
                    link(dve.tensor_copy(qp[:, 1, c, :], qr[:]))
                    dve.tensor_tensor(qp[:, 2, c, :], qr[:], qp[:, 1, c, :], ALU.subtract).then_inc(sem("q_parts"), 3)
                dve.wait_ge(sem("kvT"), b + 1)
                dve.wait_ge(sem("q_parts"), 3 * KC * (b + 1))
                link(dve.scalar_tensor_tensor(out=kr[:], in0=kvT[0:HD, :], scalar=HD ** -0.5, in1=kp[:, 0, :],
                                              op0=ALU.mult, op1=ALU.subtract))
                link(dve.tensor_copy(kp[:, 1, :], kr[:]))
                dve.tensor_tensor(kp[:, 2, :], kr[:], kp[:, 1, :], ALU.subtract).then_inc(sem("k_parts"), 3)
                dve.wait_ge(sem("a_v"), b + 1)
                dve.tensor_copy(vv[:, b % 2, :, 0:HD], ps[:, PS_S + 1, 0:QT * 2 * HD].rearrange("p (t d) -> p t d", t=QT)[:, :, HD:]).then_inc(sem("v_in"), 1)

            def head_maxima(b, h, bank):
                dve.wait_ge(sem("s_done"), HEADS * b + h + 1)
                dve.tensor_reduce(m3[:, ds(h, 1), :], ps[:, PS_S + bank, 0:3 * P].rearrange("p (n k) -> p n k", n=3),
                                  AX_X, ALU.max).then_inc(sem("s_max"), 1)

            def maxima(b):
                dve.wait_ge(sem("s_max"), HEADS * (b + 1))
                link(dve.tensor_tensor(m3[:, :, 1], m3[:, :, 1], m3[:, :, 2], ALU.max))
                dve.tensor_scalar(nm[:, 0, :], m3[:, :, 0], -1.0, None, ALU.mult)
                dve.tensor_scalar(nm[:, 1, :], m3[:, :, 1], -1.0, None, ALU.mult).then_inc(sem("m_nm"), 1)
                dve.wait_ge(sem("m_t"), b + 1)
                if b >= 1:
                    dve.wait_ge(sem(f"m_out{(b - 1) % 2}"), 16 * ((b - 1) // 2 + 1))
                src = ps[0:QT * HEADS, PS_S, 0:P]
                link(dve.tensor_copy(mp[:, 0, :], src))
                link(dve.tensor_tensor(mr[:], src, mp[:, 0, :], ALU.subtract))
                link(dve.tensor_copy(mp[:, 1, :], mr[:]))
                dve.tensor_tensor(mp[:, 2, :], mr[:], mp[:, 1, :], ALU.subtract).then_inc(sem("m_parts"), 3)

            def normalise(n, q):
                o = ps[:, PS_A, 0:QT * P].rearrange("p (t h d) -> p t h d", t=QT, h=4)
                dve.wait_ge(sem("ot"), n + 1)
                dve.reciprocal(rec[:], o[:, :, :, HD]).then_inc(sem("a_rec"), 1)
                dve.wait_ge(sem("a_rec"), n + 1)
                dve.tensor_tensor(attn[:, :, ds(q * 4 * HD, 4 * HD)].rearrange("p t (h d) -> p t h d", h=4), o[:, :, :, 0:HD],
                                  bc(rec[:, :, :, None], [P, QT, 4, HD]), ALU.mult).then_inc(sem("normed"), 1)

            def quad(b, q, lag):
                if b + 1 < BATCH:
                    for h in range(4):
                        head_maxima(b + 1, 4 * q + h, h % 2)
                if lag:
                    normalise(8 * b + q - 1, q - 1)

            qkv(0)
            att_norm(1)
            qkv(1)
            with dve.Fori(0, HEADS // 2) as g:
                head_maxima(0, 2 * g, 0)
                head_maxima(0, 2 * g + 1, 1)
            maxima(0)
            for b in range(BATCH):
                if b + 2 < BATCH:
                    att_norm(b + 2)
                if b >= 1:
                    dve.wait_ge(sem("a_at"), QT * b)
                quad(b, 0, False)
                quad(b, 1, True)
                with dve.Fori(2, HEADS // 4) as q:
                    quad(b, q, True)
                normalise(8 * b + 7, 7)
                if b + 1 < BATCH:
                    maxima(b + 1)
                if b + 2 < BATCH:
                    qkv(b + 2)
                for q in range(QT):
                    t = QT * b + q
                    dve.wait_ge(sem("a_wo"), t + 1)
                    dve.tensor_tensor(x[:, t, :], ps[:, PS_O, :], x[:, t, :], ALU.add).then_inc(sem("att_x"), 1)
                    dve.wait_ge(sem("att_x"), t + 1)
                    dve.bn_stats(st[:, t, :], x[:, t, :]).then_inc(sem("stats"), 1)

        @block.vector
        def _(dve):
            ffn_dve(0)
            att_dve()
            ffn_dve(1)


        def ffn_pe(f):
            pe = nc.tensor

            for t in range(NT):
                pe.wait_ge(sem(f"xn{f}"), t + 1)
                if t >= 2:
                    pe.wait_ge(sem(f"xnT{f}"), t - 1)
                for c in range(KC):
                    ins = pe.transpose(ps[:, PS_XT + t % 2, c * P:(c + 1) * P], xn[:, t, c * P:(c + 1) * P], ident)
                ins.then_inc(sem(f"xt{f}"), 1)
            pe.wait_ge(sem(f"xnT{f}"), NT)
            for c in range(KC):
                for j in range(NT // 2):
                    for t in range(2):
                        ins = pe.matmul(ps[32 * j:32 * j + 32, PS_XT, t * P:(t + 1) * P], rw[:, c, :], xnT[:, 2 * j + t, c, :],
                                        start=(c == 0 and t == 0), stop=(c == KC - 1), skip_group_check=True)
            ins.then_inc(sem(f"lt{f}"), 1)
            if f == 1:
                pe.wait_ge(sem("sw_back"), 32)
            if f == 0:
                pe.wait_ge(sem("sw_in"), 48)
                pe.wait_ge(sem("bias_out"), 32)
                pe.wait_ge(sem("cb_in"), 16)

            def logits():
                pe.wait_ge(sem(f"lgT{f}"), 1)
                for t in range(2):
                    ins = pe.transpose(ps[:, PS_MISC, t * P:(t + 1) * P], lgT[:, t * P:(t + 1) * P], ident)
                ins.then_inc(sem(f"logit{f}"), 1)

            def shared_up(t, chunks):
                o = ps[:, PS_GU + t % 2, :]
                if 0 in chunks:
                    if t >= 2:
                        pe.wait_ge(sem(f"s_h{f}"), t - 1)
                    pe.matmul(o, ones[0:3, :], b12x[:, E * 2 * INTER:], start=True, stop=False)
                for c in chunks:
                    ins = pe.matmul(o, xnT[:, t, c, :], sw12[:, c, :], start=False, stop=(c == KC - 1))
                if KC - 1 in chunks:
                    ins.then_inc(sem(f"s_gu{f}"), 1)

            def shared_turn(t):
                pe.wait_ge(sem(f"s_h{f}"), t + 1)
                if t >= 2:
                    pe.wait_ge(sem(f"s_hT{f}"), t - 1)
                for c in range(SHARED // P):
                    ins = pe.transpose(ps[:, PS_HT, (t % 2) * SHARED + c * P:(t % 2) * SHARED + (c + 1) * P],
                                       hh[:, t % 2, c * P:(c + 1) * P], ident)
                ins.then_inc(sem(f"s_ht{f}"), 1)

            def shared_down(t):
                pe.wait_ge(sem(f"s_hT{f}"), t + 1)
                if t >= 2:
                    pe.wait_ge(sem(f"s_x{f}"), t - 1)
                for c in range(SHARED // P):
                    ins = pe.matmul(ps[:, PS_Y + t % 2, :], hT[:, t % 2, c * P:(c + 1) * P], sw3s[:, c, :],
                                    start=(c == 0), stop=(c == SHARED // P - 1))
                ins.then_inc(sem(f"s_z{f}"), 1)

            def ranks():
                pe.wait_ge(sem(f"taken{f}"), 1)
                pe.matmul(ps_rank, upper, taken[:], start=True, stop=True)
                for t in range(NT - 1):
                    n = NT - 1 - t
                    pe.matmul(ps_rank[:, t + 1:, :], ones, bc(taken[:, t:t + 1, :], [P, n, E]), start=False, stop=True,
                              skip_group_check=True)
                for t in range(NT):
                    ins = pe.matmul(ps_count, ones, taken[:, t, :], start=(t == 0), stop=(t == NT - 1))
                ins.then_inc(sem(f"rank{f}"), 1)

            def listing():
                pe.wait_ge(sem(f"onehot{f}"), 1)
                n = CHOICES * NT
                for k in range(n):
                    ins = pe.matmul(ps_list, onehot_p[:, k, :], onehot_j[:, k].rearrange("p a j -> p (a j)"),
                                    start=(k == 0), stop=(k == n - 1))
                ins.then_inc(sem(f"listed{f}"), 1)

            def gates():
                pe.wait_ge(sem(f"gate{f}"), 1)
                pe.wait_ge(sem(f"lgT{f}"), 1)
                for t in range(NT):
                    ins = pe.transpose(ps[0:E + 1, PS_XT + t // 4, (t % 4) * P:(t % 4 + 1) * P], gate[:, t, :], ident)
                    if t % 4 == 3:
                        ins.then_inc(sem(f"gt{f}"), 1)

            def shared(first, last):
                for t in range(first, last + 1):
                    if t < last:
                        shared_up(t, (0, 1))
                    if t == 0:
                        logits()
                    if t > first:
                        shared_turn(t - 1)
                    if t < last:
                        shared_up(t, (2, 3))
                    if f == 1 and t == 1:
                        pe.wait_ge(sem("sw3_back"), 48)
                    if t > first:
                        shared_down(t - 1)
                    if t == 3 and first == 0:
                        ranks()
                        gates()
                    if t == 5 and first == 0:
                        listing()

            shared(0, FIRST)
            if f == 0:
                pe.wait_ge(sem("ew_in"), 16 * 3 * E // EG)
            pe.wait_ge(sem(f"jex{f}"), 1)
            pe.wait_ge(sem(f"gateT{f}"), 2)
            pairs = pe.value_load(jm[:], min_val=JOBS_LEAST // 2, max_val=JOBS // 2)

            def turn(j, par, n):
                pe.wait_ge(sem(f"xg{f}_{par}"), n)
                for c in range(KC):
                    ins = pe.transpose(ps[:, PS_XT + par, c * P:(c + 1) * P], xg[:, par, c * P:(c + 1) * P], ident)
                ins.then_inc(sem(f"xgt{f}"), 1)

            def expert(j):
                return pe.value_load(jex[0:1, ds(j, 1)], min_val=0, max_val=E - 1)

            def up(j, par, e, before=None):
                pe.wait_ge(sem(f"xgT{f}"), j + 1)
                if before is not None:
                    pe.wait_ge(sem(f"h{f}"), before)
                o = ps[:, PS_GU + par, 0:2 * INTER]
                pe.matmul(o, ones[0:3, :], b12x[:, ds(e * 2 * INTER, 2 * INTER)], start=True, stop=False)
                for c in range(KC):
                    ins = pe.matmul(o, xgT[:, par, c, :], w12[:, ds(e, 1), c, :], start=False, stop=(c == KC - 1))
                ins.then_inc(sem(f"gu{f}"), 1)

            def h_turn(j, par):
                pe.wait_ge(sem(f"h{f}"), j + 1)
                pe.transpose(ps[:, PS_HT, P * par:P * par + P], hh[:, par, 0:INTER], ident).then_inc(sem(f"ht{f}"), 1)

            def down(j, par, e, before=None):
                pe.wait_ge(sem(f"hT{f}"), j + 1)
                if before is not None:
                    pe.wait_ge(sem(f"y_sb{f}"), before)
                pe.matmul(ps[:, PS_Y + par, :], hT[:, par, 0:INTER], w3[:, ds(e, 1), :], start=True, stop=True).then_inc(sem(f"y{f}"), 1)

            turn(0, 0, 16)
            pe.wait_ge(sem(f"s_h{f}"), FIRST)
            up(0, 0, expert(0))
            turn(1, 1, 16)
            h_turn(0, 0)
            up(1, 1, expert(1))
            turn(2, 0, 32)
            pe.wait_ge(sem(f"s_x{f}"), FIRST)
            down(0, 0, expert(0))
            h_turn(1, 1)
            up(2, 0, expert(2), 1)
            turn(3, 1, 32)
            down(1, 1, expert(1))

            with pe.Fori(0, pairs - 1) as i:
                e0, e1 = expert(2 * i + 2), expert(2 * i + 3)
                h_turn(2 * i + 2, 0)
                up(2 * i + 3, 1, e1, 2 * i + 2)
                turn(2 * i + 4, 0, 16 * i + 48)
                down(2 * i + 2, 0, e0, 2 * i + 1)
                e2 = expert(2 * i + 4)
                h_turn(2 * i + 3, 1)
                up(2 * i + 4, 0, e2, 2 * i + 3)
                turn(2 * i + 5, 1, 16 * i + 48)
                down(2 * i + 3, 1, e1, 2 * i + 2)
            e = expert(2 * pairs)
            h_turn(2 * pairs, 0)
            down(2 * pairs, 0, e, 2 * pairs)

            def biases(tiles):
                for t in tiles:
                    if t >= 3:
                        pe.wait_ge(sem(f"biased{f}"), t - 2)
                    pe.matmul(ps[:, PS_XT + t % 3, :], gateT[:, t, :], eb3x, start=True, stop=True).then_inc(sem(f"c{f}"), 1)

            pe.wait_ge(sem(f"xgT{f}"), 2 * pairs + 2)
            biases((0, 1))
            pe.wait_ge(sem(f"h{f}"), 2 * pairs + 1)
            pe.wait_ge(sem(f"y_sb{f}"), 2 * pairs + 1)
            shared_up(6, range(KC))
            biases((2, 3))
            shared_up(7, range(KC))
            shared_turn(6)
            biases((4,))
            shared_down(6)
            shared_turn(7)
            biases((5,))
            shared_down(7)
            biases((6, 7))

        def att_pe():
            pe = nc.tensor
            pe.wait_ge(sem("wqkv_in"), 16)
            pe.wait_ge(sem("biased0"), NT)

            def qkv(b):
                for c in range(4):
                    q, half = c // 2, c % 2
                    pe.wait_ge(sem("a_xn"), QT * b + q + 1)
                    if b == 1:
                        pe.wait_ge(sem("q_parts"), 3 * (c + 1))
                    if b >= 2 and c == 0:
                        pe.wait_ge(sem("exp"), 16 * (b - 1))
                    for k in range(2):
                        ins = pe.transpose(ps[:, PS_ST + c, k * P:(k + 1) * P], xa[:, q, (2 * half + k) * P:(2 * half + k + 1) * P], ident)
                    ins.then_inc(sem("a_xt"), 1)
                pe.wait_ge(sem("a_xaT"), 4 * (b + 1))
                for c in range(KC):
                    for k in range(KC):
                        ins = pe.matmul(ps[:, PS_ST + c, 0:SEQ], wqkv[:, k, c * P:(c + 1) * P], xaT[:, k, :], start=(k == 0), stop=(k == KC - 1))
                    ins.then_inc(sem("a_q"), 1)
                if b == 1:
                    pe.wait_ge(sem("v_in"), 1)
                if b >= 2:
                    pe.wait_ge(sem("m_parts"), 3 * b)
                for k in range(KC):
                    ins = pe.matmul(ps[0:2 * HD, PS_S, 0:SEQ], wqkv[:, k, DIM:], xaT[:, k, :], start=(k == 0), stop=(k == KC - 1))
                ins.then_inc(sem("a_k"), 1)
                pe.wait_ge(sem("kvT"), b + 1)
                for q in range(QT):
                    ins = pe.transpose(ps[:, PS_S + 1, q * 2 * HD:(q + 1) * 2 * HD], kvT[:, q * P:(q + 1) * P], cf[0:2 * HD, C_ID:C_ID + 2 * HD])
                ins.then_inc(sem("a_v"), 1)

            def scores(b, h, bank):
                n = HEADS * b + h
                if not (type(n) is int and n < 2):
                    pe.wait_ge(sem("s_max"), n - 1)
                p = b % 2
                o = ps[:, PS_S + bank, :]
                pe.matmul(o.rearrange("p (n k) -> p n k", k=P)[:, 0:3:2, :], identb, mask, start=True, stop=True)
                pe.matmul(o[:, 0:P], qside[0:R_MAX, p, ds(h, 1), 0:P], kT[0:R_MAX, p, 0:P], start=False, stop=True, skip_group_check=True)
                pe.matmul(o[:, P:3 * P], qside[0:R_MAX, p, ds(h, 1), P:2 * P], kT[0:R_MAX, p, :], start=False, stop=True,
                          skip_group_check=True).then_inc(sem("s_done"), 1)

            def scores_t(b, g, pair):
                n = 16 * b + g
                if not (type(n) is int and n < 2):
                    pe.wait_ge(sem("exp"), n - 1)
                p = b % 2
                o = ps[:, PS_ST + 2 * pair:PS_ST + 2 * pair + 2, :]
                pe.matmul(o[:, 0, :].rearrange("p (h q) -> p h q", h=2)[:, :, 0:P], identb, mask_t, start=True, stop=True)
                pe.matmul(o[:, 0, :], kT[0:ROWS, p, 0:P], qside[0:ROWS, p, ds(2 * g, 2), :], start=False, stop=True,
                          skip_group_check=True)
                pe.matmul(o[:, 1, 0:2 * P], identb, mask_t, start=True, stop=True)
                pe.matmul(o[:, 1, 0:2 * P], kT[0:ROWS, p, P:2 * P], qside[0:ROWS, p, ds(2 * g, 2), P:2 * P],
                          start=False, stop=True, skip_group_check=True).then_inc(sem("st_done"), 1)

            def weigh(b, n, par):
                pe.wait_ge(sem("exp"), 2 * n + 2)
                if not (type(n) is int and n < 1):
                    pe.wait_ge(sem("oT"), n)
                for k in range(QT):
                    for h in range(4):
                        o = ps[32 * h:32 * h + 32, PS_O, k * P:SEQ]
                        w = QT * P - k * P
                        at = k * 2 * SEQ + (h % 2) * w
                        ins = pe.matmul(o, vv[:, b % 2, k, :], pr[:, par, h // 2, at:at + w], start=(k == 0), stop=True,
                                        skip_group_check=True)
                ins.then_inc(sem("pv"), 1)

            def turn_back(n):
                pe.wait_ge(sem("oT"), n + 1)
                if not (type(n) is int and n < 1):
                    pe.wait_ge(sem("normed"), n)
                for q in range(QT):
                    ins = pe.transpose(ps[:, PS_A, q * P:(q + 1) * P], oT[:, q * P:(q + 1) * P], ident)
                ins.then_inc(sem("ot"), 1)

            def max_turn(b):
                pe.wait_ge(sem("m_nm"), b + 1)
                pe.transpose(ps[0:QT * HEADS, PS_S, 0:P], nm[:].rearrange("p t h -> p (t h)"), ident).then_inc(sem("m_t"), 1)

            def out_proj(b):
                pe.wait_ge(sem("normed"), 8 * (b + 1))
                if b == 0:
                    pe.wait_ge(sem("wo_in"), 16)
                for q in range(QT):
                    if q >= 1:
                        pe.wait_ge(sem("a_aT"), QT * b + q)
                    for c in range(KC):
                        ins = pe.transpose(ps[:, PS_A, c * P:(c + 1) * P], attn[:, q, c * P:(c + 1) * P], ident)
                    ins.then_inc(sem("a_at"), 1)
                    pe.wait_ge(sem("a_aT"), QT * b + q + 1)
                    if q >= 1:
                        pe.wait_ge(sem("att_x"), QT * b + q)
                    for c in range(KC):
                        ins = pe.matmul(ps[:, PS_O, :], aT[:, c, :], wo[:, c, :], start=(c == 0), stop=(c == KC - 1))
                    ins.then_inc(sem("a_wo"), 1)

            qkv(0)
            qkv(1)
            pe.wait_ge(sem("rows_in"), 64)
            pe.wait_ge(sem("q_in0"), 192)
            pe.wait_ge(sem("v_in"), 2)
            scores(0, 0, 0)
            scores(0, 1, 1)
            with pe.Fori(1, HEADS // 2) as g:
                scores(0, 2 * g, 0)
                scores(0, 2 * g + 1, 1)
            max_turn(0)
            for b in range(BATCH):
                nxt = b + 1 < BATCH
                if b >= 1:
                    pe.wait_ge(sem("att_x"), QT * b)
                if nxt:
                    pe.wait_ge(sem(f"q_in{(b + 1) % 2}"), 192 * ((b + 1) // 2 + 1))
                    pe.wait_ge(sem("m_parts"), 3 * (b + 1))
                    pe.wait_ge(sem("v_in"), min(b + 2, BATCH))
                pe.wait_ge(sem("q_parts"), 3 * KC * min(b + 2, BATCH))
                pe.wait_ge(sem(f"m_in{b % 2}"), 32 * (b // 2 + 1))

                def quad(q, par, lag):
                    if nxt:
                        scores(b + 1, 4 * q, 0)
                    scores_t(b, 2 * q, 0)
                    if nxt:
                        scores(b + 1, 4 * q + 1, 1)
                    if lag:
                        weigh(b, 8 * b + q - 1, 1 - par)
                    if nxt:
                        scores(b + 1, 4 * q + 2, 0)
                    scores_t(b, 2 * q + 1, 1)
                    if nxt:
                        scores(b + 1, 4 * q + 3, 1)
                    if lag:
                        turn_back(8 * b + q - 1)
                quad(0, 0, False)
                quad(1, 1, True)
                with pe.Fori(1, HEADS // 8) as i:
                    for par in range(2):
                        quad(2 * i + par, par, True)
                weigh(b, 8 * b + 7, 1)
                turn_back(8 * b + 7)
                if nxt:
                    max_turn(b + 1)
                if b + 2 < BATCH:
                    qkv(b + 2)
                out_proj(b)

        @block.tensor
        def _(pe):
            pe.wait_ge(sem("small_in"), 96)
            ffn_pe(0)
            att_pe()
            ffn_pe(1)


_INS = ['L0_attn_hidden_states', 'L0_attn_Wqkv', 'L0_attn_Wo', 'L0_ffn_router_w', 'L0_ffn_router_b', 'L0_ffn_router_bias',
        'L0_ffn_ew1', 'L0_ffn_eb1', 'L0_ffn_ew2', 'L0_ffn_eb2', 'L0_ffn_ew3', 'L0_ffn_eb3',
        'L0_ffn_sw1', 'L0_ffn_sb1', 'L0_ffn_sw2', 'L0_ffn_sb2', 'L0_ffn_sw3', 'L0_ffn_sb3']


def kernel(**inputs):
    import numpy as _np
    import concourse.bacc as _bacc
    from concourse import mybir as _mybir
    from concourse.bass_utils import run_bass_kernel_spmd as _run

    nc = _bacc.Bacc("TRN2", target_bir_lowering=False, num_devices=1)
    arrays, args = {}, []
    named = {name: _np.ascontiguousarray(inputs[name]) for name in _INS}
    named.update(shape_constants())
    for name, a in named.items():
        if name == 'L0_attn_hidden_states':
            a = a.reshape(TOKENS, DIM)
        arrays[f"in_{name}_dram"] = a
        args.append(nc.dram_tensor(f"in_{name}_dram", a.shape, _mybir.dt.from_np(a.dtype), kind="ExternalInput").ap())
    args.append(nc.dram_tensor("out_0_dram", (TOKENS, DIM), _mybir.dt.float32, kind="ExternalOutput").ap())
    build(nc, *args)
    r = _run(nc, [arrays], core_ids=[0])
    return r.results[0]["out_0_dram"].reshape(BATCH, SEQ, DIM)
```

```python
from contextlib import ExitStack

import numpy as np

import concourse.bass as bass
from concourse import mybir
from concourse.alu_op_type import AluOpType as ALU

F32 = mybir.dt.float32
BF16 = mybir.dt.bfloat16
I32 = mybir.dt.int32
U32 = mybir.dt.uint32
ACT = mybir.ActivationFunctionType
AX_X = mybir.AxisListType.X
ds = bass.ds

P = 128
BATCH, SEQ, DIM = 4, 256, 512
TOKENS = BATCH * SEQ
NT = TOKENS // P
KC = DIM // P
E, GROUPS, INTER = 16, 4, 128
SHARED = 256
CHOICES = 2
JOBS = CHOICES * TOKENS // P + E - 1
JOBS_LEAST = CHOICES * TOKENS // P
EG = 4
FIRST = 6
BIASED = 5
JP = 32
HEADS, HD = 32, 16
QT = SEQ // P
NEG = -1e30
EPS = 1e-5

QPART = (0, 0, 0, 1, 1, 2)
KPART = (0, 1, 2, 0, 1, 0)
KRUNS = (3, 2, 1)
R_ALIBI = len(QPART) * HD
R_MAX = R_ALIBI + 6
ROWS = R_MAX + 3

C_ID, C_IOTA, C_PIDX, C_TILE, C_END = 0, 128, 256, 257, 273
B_UP, B_ONE, B_ID, B_MASK, B_END = 0, 128, 256, 384, 640


def bf16_parts(a):
    parts, rest = [], a.astype(np.float64)
    for _ in range(3):
        bits = rest.astype(np.float32).view(np.uint32)
        bits = (bits + 0x7FFF + ((bits >> 16) & 1)) & np.uint32(0xFFFF0000)
        part = bits.astype(np.uint32).view(np.float32)
        parts.append(part)
        rest = rest - part
    return np.stack(parts)


def shape_constants():
    i = np.arange(P)
    const_f = np.zeros((P, C_END), np.float32)
    const_f[:, C_ID:C_ID + P] = np.eye(P)
    const_f[:, C_IOTA:C_IOTA + P] = i[None, :]
    const_f[:, C_PIDX] = i
    const_f[:, C_TILE:C_TILE + CHOICES * NT] = np.tile(np.arange(NT) * P, CHOICES)[None, :]
    const_b = np.zeros((P, B_END), np.float32)
    const_b[:, B_UP:B_UP + P] = i[:, None] < i[None, :]
    const_b[:, B_ONE:B_ONE + P] = 1.0
    const_b[:, B_ID:B_ID + P] = np.eye(P)
    later = np.where(i[None, :] <= i[:, None], 0.0, NEG)
    const_b[:, B_MASK:B_MASK + 2 * P] = np.concatenate([later, later.T], 1)
    slopes = (2.0 ** (-2.0 ** (-(np.log2(HEADS) - 3)))) ** np.arange(1, HEADS + 1, dtype=np.float64)
    slopes = slopes.astype(np.float32).astype(np.float64)
    pos = np.arange(SEQ, dtype=np.float64)
    rows_q = np.concatenate([
        np.broadcast_to(bf16_parts(slopes)[:, :, None], (3, HEADS, SEQ)),
        bf16_parts(-slopes[:, None] * pos[None, :])]).astype(np.float32)
    rows_k = np.concatenate([np.tile(pos, (3, 1)), np.ones((6, SEQ))]).astype(np.float32)
    return {"const_f": const_f, "const_b": const_b, "rows_q": np.ascontiguousarray(rows_q), "rows_k": rows_k}


def build(nc, x_in, wqkv_in, wo_in, rw_in, rb_in, rbias_in, ew1, eb1, ew2, eb2, ew3, eb3,
          sw1, sb1, sw2, sb2, sw3, sb3, const_f, const_b, rows_q, rows_k, out):
    with ExitStack() as ctx:
        def sb(name, shape, dt=F32):
            return ctx.enter_context(nc.sbuf_tensor(name, shape, dt))

        sems = {}

        def sem(name):
            if name not in sems:
                sems[name] = ctx.enter_context(nc.semaphore(name))
            return sems[name]

        xn_dram = nc.dram_tensor("xn_dram", (TOKENS, DIM), F32).ap()
        y_dram = nc.dram_tensor("y_dram", (JOBS * P, DIM), F32).ap()
        b12_dram = nc.dram_tensor("b12_dram", (3, E + 2, 2 * INTER), BF16).ap()
        q_dram = nc.dram_tensor("q_dram", (2, 3, DIM, SEQ), BF16).ap()
        k_dram = nc.dram_tensor("k_dram", (2, 3, HD, SEQ), BF16).ap()
        m_dram = nc.dram_tensor("m_dram", (2, 3, QT * HEADS, P), BF16).ap()

        x = sb("x", [P, NT, DIM])
        w12 = sb("w12", [P, E, KC, 2 * INTER])
        w3 = sb("w3", [P, E, DIM])
        turns = sb("turns", [P, KC * (DIM + 2 * HD)])
        sw12 = turns[:, 0:KC * 2 * SHARED].rearrange("p (c f) -> p c f", c=KC)
        wqkv = turns[:].rearrange("p (c f) -> p c f", c=KC)
        turns2 = sb("turns2", [P, KC * DIM])
        sw3s = turns2[:, 0:SHARED // P * DIM].rearrange("p (c d) -> p c d", d=DIM)
        eb3x = turns2[0:E + 1, SHARED // P * DIM:SHARED // P * DIM + DIM]
        wo = turns2[:].rearrange("p (c d) -> p c d", d=DIM)
        rw = sb("rw", [P, KC, 2 * E])
        cf = sb("cf", [P, C_END])
        cb = sb("cb", [P, B_END], BF16)
        b12x = sb("b12x", [3, (E + 2) * 2 * INTER], BF16)
        rbc = sb("rbc", [P, 2, E])
        neghalf = sb("neghalf", [P, NT])
        mark = sb("mark", [P, 2])
        st = sb("st", [P, NT, 6])
        mv = sb("mv", [P, NT, 2])
        varE = sb("varE", [P, NT])
        rstd = sb("rstd", [P, NT])
        ident = cf[:, C_ID:C_ID + P]
        iota = cf[:, C_IOTA:C_IOTA + P]
        upper = cb[:, B_UP:B_UP + P]
        ones = cb[:, B_ONE:B_ONE + P]
        identb = cb[:, B_ID:B_ID + P]
        mask = cb[:, None, B_MASK:B_MASK + P].to_broadcast([P, 2, P])
        mask_t = cb[:, None, B_MASK + P:B_MASK + 2 * P].to_broadcast([P, 2, P])

        WORDS = 16960
        arena = sb("arena", [P, WORDS])
        used = {"ffn": 0, "att": 0}

        def view(kind, shape, dt=F32, at=None):
            n = int(np.prod(shape[1:]))
            words = n if dt != BF16 else (n + 1) // 2
            if at is None:
                at = used[kind]
                used[kind] += words
                assert used[kind] <= WORDS, (kind, used[kind])
            v = arena[0:shape[0], at:at + words]
            if dt != F32:
                v = v.bitcast(dt)
            if len(shape) == 2:
                return v
            names = "abcd"[:len(shape) - 1]
            return v.rearrange(f"p ({' '.join(names)}) -> p {' '.join(names)}",
                               **{c: s for c, s in zip(names, shape[1:])})

        xn = view("ffn", [P, NT, DIM])
        yg = view("ffn", [P, 4, CHOICES, DIM], at=0)
        xnT = view("ffn", [P, NT, KC, P])
        hv = view("ffn", [P, NT, CHOICES])
        slotu = view("ffn", [P, CHOICES, NT], U32)
        sg = view("ffn", [P, 2, SHARED])
        hh = view("ffn", [P, 2, SHARED])
        hT = view("ffn", [P, 2, SHARED])
        gateT = view("ffn", [E + 1, NT, P])
        early = used["ffn"]
        listu = view("ffn", [P, JP], U32)
        xg_at = used["ffn"]
        xg = view("ffn", [P, 2, DIM])
        xgT = view("ffn", [P, 2, KC, P])
        onehot_p = view("ffn", [P, CHOICES * NT, P], BF16, at=xg_at)
        onehot_j = view("ffn", [P, CHOICES * NT, 2, JP], BF16, at=xg_at + CHOICES * NT * P // 2)
        jcmp = view("ffn", [1, JP, E], at=xg_at + CHOICES * NT * P // 2 + CHOICES * NT * JP)
        ysb = view("ffn", [P, 2, DIM])
        lgT = view("ffn", [P, 2 * P])
        lg = view("ffn", [P, NT, E])
        sc = view("ffn", [P, NT, E])
        t16 = view("ffn", [P, NT, E])
        red = view("ffn", [P, NT])
        gm8 = view("ffn", [P, NT, 8])
        gtop = view("ffn", [P, NT, 8])
        gidx = view("ffn", [P, NT, 8], U32)
        etop = view("ffn", [P, NT, 8])
        eidx = view("ffn", [P, NT, 8], U32)
        idxf = view("ffn", [P, NT, 2])
        keep = view("ffn", [P, NT, GROUPS])
        keep2 = view("ffn", [P, NT, GROUPS])
        oh = view("ffn", [P, CHOICES, NT, E])
        taken = view("ffn", [P, NT, E], BF16)
        gate = view("ffn", [P, NT, E + 1])
        cnt = view("ffn", [P, 4, E])
        cnti = view("ffn", [P, E], I32)
        slot = view("ffn", [P, CHOICES, NT])
        sloti = view("ffn", [P, CHOICES, NT], I32)
        sji = view("ffn", [P, 2, CHOICES * NT], I32)
        sjf = view("ffn", [P, 2, CHOICES * NT])
        listf = view("ffn", [P, JP])
        jexf = view("ffn", [1, JP])
        jex = view("ffn", [1, JP], I32)
        jm = view("ffn", [1, 1], I32)
        qside = view("att", [P, 2, HEADS, SEQ], BF16)
        kT = view("att", [P, 2, SEQ], BF16)
        attn = view("att", [P, QT, HEADS * HD])
        aT = view("att", [P, KC, P])
        oT = view("att", [P, SEQ])
        rec = view("att", [P, QT, 4])
        m3 = view("att", [P, HEADS, 3])
        nm = view("att", [P, QT, HEADS])
        mr = view("att", [QT * HEADS, P])
        mp = view("att", [QT * HEADS, 3, P], BF16)
        pr = view("att", [P, 2, 2, 3 * 2 * P])
        qp_at = used["att"] - 3 * 2 * P * 2
        assert qp_at >= early
        qp = view("att", [P, 3, KC, SEQ], BF16, at=qp_at)
        xaT = view("att", [P, KC, SEQ])
        aT = (aT, xaT.rearrange("p c t -> p (c t)")[:, 0:KC * P].rearrange("p (c q) -> p c q", c=KC))
        qr = view("att", [P, SEQ])
        kp = view("att", [HD, 3, SEQ], BF16)
        kr = qr[0:HD, :]
        kvT = view("att", [2 * HD, SEQ])
        vv = view("att", [P, 2, QT, 32])
        xa = view("att", [P, QT, DIM])

        ps = ctx.enter_context(nc.psum_tensor("ps", [P, 8, 512], F32))
        PS_GU, PS_HT, PS_Y, PS_XT, PS_MISC = 0, 2, 3, 5, 7
        ps_logit = ps[:, PS_MISC, 0:256].rearrange("p (c j e) -> p j c e", c=2, j=NT // 2)[:, :, :, 0:E]
        ps_rank = ps[:, PS_MISC, 256:384].rearrange("p (t e) -> p t e", e=E)
        ps_count = ps[:, PS_MISC, 384:384 + E]
        ps_list = ps[:, PS_MISC, 416:416 + 2 * JP]
        PS_ST, PS_S, PS_O, PS_A = 0, 4, 6, 7
        AT_BANK, WO_BANK = (PS_A, PS_ST), (PS_O, PS_A)

        def bc(ap, shape):
            return ap.to_broadcast(shape)

        b12f = hT[0:E + 2, 0, :]
        b12p = ysb[0:E + 2, 0, 0:3 * INTER].bitcast(BF16).rearrange("p (k f) -> p k f", k=3)

        def kv_bank(b):
            return PS_ST if b == 1 else PS_S

        block = ctx.enter_context(nc.Block())

        LN = ((range(0, NT // 2), range(NT // 2, NT)), (range(0, NT - QT), range(NT - QT, NT)))

        Q_ORDER = (0, 1, None, 2, 3)
        Q_OUTS, Q_INS, Q_LATE = 16 * len(Q_ORDER), 16 * (len(QPART) + len(KRUNS)), 16 * len(QPART)

        def experts_in(eng, e, part):
            w = (ew1, ew2)[part]
            eng.dma_start(w12[:, e:e + EG, :, part * INTER:(part + 1) * INTER].rearrange("p e c f -> p (e c) f"),
                          w[e:e + EG].rearrange("e (c p) f -> p (e c) f", p=P)).then_inc(sem("ew_in"), 16)

        def k_rows(eng, b):
            p, row = b % 2, 0
            for n in KRUNS:
                eng.dma_start(kT[row:row + n * HD, p], k_dram[p, 0:n].rearrange("k d t -> (k d) t")).then_inc(sem(f"q_in{p}"), 16)
                row += n * HD

        def m_outs(b):
            return 16 * (b // 2 + 1) + (48 if b % 2 == 0 else 0)

        def m_ins(b):
            return 32 * (b // 2 + 1) + 32 * (b % 2)

        def ffn_sp(f):
            for t in range(NT):
                nc.sync.wait_ge(sem(f"xn{f}"), t + 1)
                nc.sync.dma_start(xn_dram[t * P:(t + 1) * P, :], xn[:, t, :]).then_inc(sem(f"xn_out{f}"), 16)
            if f == 1:
                nc.sync.wait_ge(sem("a_wo"), NT)
                nc.sync.dma_start(sw3s, sw3.rearrange("(c p) d -> p c d", p=P)).then_inc(sem("wo_in"), 16)
                nc.sync.dma_start(eb3x[0:E, :], eb3).then_inc(sem("wo_in"), 16)
                nc.sync.dma_start(eb3x[E:E + 1, :], sb3.rearrange("(a d) -> a d", a=1)).then_inc(sem("wo_in"), 16)

            if f == 0:
                for e in range(0, E, EG):
                    for part in range(2):
                        if e > 0:
                            experts_in(nc.sync, e, part)
                    nc.sync.dma_start(w3[:, e:e + EG, :], ew3[e:e + EG].rearrange("e p d -> p e d")).then_inc(sem("ew_in"), 16)

            def store(j, par):
                nc.sync.wait_ge(sem(f"y_sb{f}"), j + 1)
                nc.sync.dma_start(y_dram[ds(j * P, P), :], ysb[:, par, :]).then_inc(sem(f"y_out{f}_{par}"), 16)
            nc.sync.wait_ge(sem(f"jex{f}"), 1)
            pairs = nc.sync.value_load(jm[:], min_val=JOBS_LEAST // 2, max_val=JOBS // 2)
            if f == 0:
                first_spare = JOBS_LEAST + 1
                with nc.sync.Fori(0, (JOBS - first_spare) // 2) as i:
                    store(2 * i, 0)
                    store(2 * i + 1, 1)
                    nc.sync.dma_start(y_dram[ds((2 * i + first_spare) * P, 2 * P), :], x_in[0:2 * P, :]).then_inc(sem("y_spare"), 16)
                nc.sync.wait_ge(sem("y_spare"), 16 * ((JOBS - first_spare) // 2))
                with nc.sync.Fori((JOBS - first_spare) // 2, pairs) as i:
                    store(2 * i, 0)
                    store(2 * i + 1, 1)
            else:
                with nc.sync.Fori(0, pairs) as i:
                    store(2 * i, 0)
                    store(2 * i + 1, 1)
            store(2 * pairs, 0)
            if f == 0:
                nc.sync.wait_ge(sem("s_gu0"), NT)
                nc.sync.dma_start(wqkv, wqkv_in.rearrange("(c p) n -> p c n", p=P)).then_inc(sem("wqkv_in"), 16)
                nc.sync.wait_ge(sem("s_z0"), NT)
                nc.sync.wait_ge(sem("c0"), BIASED)
                nc.sync.dma_start(wo, wo_in.rearrange("(c p) n -> p c n", p=P)).then_inc(sem("wo_in"), 16)

        def att_sp():
            def q_rows(b):
                p = b % 2
                outs = Q_OUTS * (b // 2)
                for half in range(2):
                    for c in (Q_ORDER[0:3], Q_ORDER[3:])[half]:
                        if c is None:
                            nc.sync.wait_ge(sem("k_parts"), 3 * (b + 1))
                            nc.sync.dma_start(k_dram[p].rearrange("k d t -> d k t"), kp[:]).then_inc(sem(f"q_out{p}"), 16)
                        else:
                            nc.sync.wait_ge(sem("q_parts"), 3 * (KC * b + c + 1))
                            nc.sync.dma_start(q_dram[p, :, c * P:(c + 1) * P, :].rearrange("k p t -> p k t"), qp[:, :, c, :]).then_inc(sem(f"q_out{p}"), 16)
                        outs += 16
                    nc.sync.wait_ge(sem(f"q_out{p}"), outs)
                    if half == 0:
                        if b >= 2:
                            nc.sync.wait_ge(sem("st_done"), HEADS // 2 * (b - 1))
                        if b == 0:
                            nc.sync.wait_ge(sem("comb0"), NT)
                        k_rows(nc.sync, b)
                    heads = slice(half * HEADS // 2, (half + 1) * HEADS // 2)
                    for r in range(len(QPART)):
                        nc.sync.dma_start(qside[r * HD:(r + 1) * HD, p, heads],
                                          q_dram[p, QPART[r], heads.start * HD:heads.stop * HD].rearrange("(h d) t -> d h t", d=HD)
                                          ).then_inc(sem((f"q_in{p}", f"q_late{p}")[half]), 16)

            def m_rows_half(n):
                heads = slice(n * HEADS // 2, (n + 1) * HEADS // 2)
                nc.sync.wait_ge(sem("m_parts"), 3 * (n + 1))
                rows = [slice(q * HEADS + heads.start, q * HEADS + heads.stop) for q in range(QT)]
                for q in range(QT):
                    nc.sync.dma_start(m_dram[0, :, rows[q], :].rearrange("k r q -> r k q"), mp[rows[q]]).then_inc(sem("m_out0"), 16)
                nc.sync.wait_ge(sem("m_out0"), 32 * (n + 1))
                for q in range(QT):
                    nc.sync.dma_start(qside[R_MAX:ROWS, 0, heads, q * P:(q + 1) * P], m_dram[0, :, rows[q], :]).then_inc(sem(f"m_in{n}"), 16)

            def m_rows(b):
                p = b % 2
                nc.sync.wait_ge(sem("m_parts"), 3 * (b + 2))
                nc.sync.dma_start(m_dram[p].rearrange("k r q -> r k q"), mp[:]).then_inc(sem(f"m_out{p}"), 16)
                nc.sync.wait_ge(sem(f"m_out{p}"), m_outs(b))
                for q in range(QT):
                    nc.sync.dma_start(qside[R_MAX:ROWS, p, :, q * P:(q + 1) * P],
                                      m_dram[p, :, q * HEADS:(q + 1) * HEADS, :]).then_inc(sem(f"m_in{p}"), 16)

            q_rows(0)
            m_rows_half(0)
            q_rows(1)
            m_rows_half(1)
            for b in range(BATCH):
                if b + 1 < BATCH:
                    m_rows(b + 1)
                if b + 2 < BATCH:
                    q_rows(b + 2)
                if b + 3 == BATCH:
                    nc.sync.wait_ge(sem("a_k"), BATCH)
                    nc.sync.dma_start(sw12[:, :, 0:SHARED], sw1.rearrange("(c p) f -> p c f", p=P)).then_inc(sem("sw_in"), 16)
                    nc.sync.dma_start(sw12[:, :, SHARED:], sw2.rearrange("(c p) f -> p c f", p=P)).then_inc(sem("sw_in"), 16)

        @block.sync
        def _(sp):
            for n in range(0, NT, 2):
                sp.dma_start(x[:, n:n + 2, :], x_in[n * P:(n + 2) * P, :].rearrange("(t p) d -> p t d", p=P)).then_inc(sem(f"x_in{n // 2}"), 16)
            sp.dma_start(cf[:], const_f).then_inc(sem("small_in"), 16)
            sp.wait_ge(sem("pool_set"), 1)
            sp.dma_start(rw[:, :, 0:E], rw_in.rearrange("(c p) e -> p c e", p=P)).then_inc(sem("small_in"), 16)
            sp.dma_start(rbc[:, 0, :], rb_in.partition_broadcast(P)).then_inc(sem("small_in"), 16)
            sp.dma_start(rbc[:, 1, :], rbias_in.partition_broadcast(P)).then_inc(sem("small_in"), 16)
            sp.dma_start(eb3x[0:E, :], eb3).then_inc(sem("small_in"), 16)
            sp.dma_start(eb3x[E:E + 1, :], sb3.rearrange("(a d) -> a d", a=1)).then_inc(sem("small_in"), 16)
            sp.dma_start(b12f[0:E, 0:INTER], eb1).then_inc(sem("bias_in"), 16)
            sp.dma_start(b12f[0:E, INTER:2 * INTER], eb2).then_inc(sem("bias_in"), 16)
            sp.dma_start(b12f[E:E + 1, :], sb1.rearrange("(a d) -> a d", a=1)).then_inc(sem("bias_in"), 16)
            sp.dma_start(b12f[E + 1:E + 2, :], sb2.rearrange("(a d) -> a d", a=1)).then_inc(sem("bias_in"), 16)
            sp.wait_ge(sem("bias_split"), 5)
            sp.dma_start(b12_dram.rearrange("k e f -> e k f"), b12p).then_inc(sem("bias_out"), 16)
            experts_in(sp, 0, 1)
            sp.wait_ge(sem("bias_out"), 16)
            sp.dma_start(b12x[:], b12_dram.rearrange("k e f -> k (e f)")).then_inc(sem("bias_out"), 16)
            ffn_sp(0)
            att_sp()
            ffn_sp(1)
            for t in range(NT):
                sp.wait_ge(sem("comb1"), t + 1)
                sp.dma_start(out[t * P:(t + 1) * P, :], x[:, t, :]).then_inc(sem("stored"), 16)
            sp.wait_ge(sem("stored"), 16 * NT)


        def bias_split(steps):
            pool = nc.gpsimd
            for n in steps:
                if n == 0:
                    pool.wait_ge(sem("bias_in"), 64)
                else:
                    pool.wait_ge(sem("bias_split"), n)
                if n % 2 == 0:
                    pool.tensor_copy(b12p[:, n // 2, :], b12f).then_inc(sem("bias_split"), 1)
                else:
                    pool.tensor_tensor(b12f, b12f, b12p[:, n // 2, :], ALU.subtract).then_inc(sem("bias_split"), 1)

        def ffn_pool(f):
            pool = nc.gpsimd
            for n in range(2):
                pool.wait_ge(sem(f"var{f}"), n + 1)
                at = slice(LN[f][n][0], LN[f][n][-1] + 1)
                pool.tensor_tensor(rstd[:, at], varE[:, at], neghalf[:, at], ALU.pow).then_inc(sem(f"rstd{f}"), 1)
                if f == 0:
                    bias_split((0, 1) if n == 0 else (2, 3, 4))
            pool.wait_ge(sem(f"list{f}"), 1)
            pool.wait_ge(sem(f"xn_out{f}"), 16 * NT)
            pairs = pool.value_load(jm[:], min_val=JOBS_LEAST // 2, max_val=JOBS // 2)

            def gather(j):
                if j >= 2:
                    pool.wait_ge(sem(f"xgt{f}"), j - 1)
                pool.indirect_dma_start(xg[:, j % 2, :], None, xn_dram,
                                        bass.IndirectOffsetOnAxis(ap=listu[:, j:j + 1], axis=0)).then_inc(sem(f"xg{f}_{j % 2}"), 16)
            for j in range(JOBS_LEAST + 2):
                gather(j)
            for i in range(JOBS_LEAST // 2 + 1, JOBS // 2 + 1):
                with pool.If_lt(pool.to_reg(i - 1), pool.to_reg(pairs)):
                    gather(2 * i)
                    gather(2 * i + 1)
            pool.wait_ge(sem(f"y_all{f}"), 2)
            for t in range(NT):
                if t >= 4:
                    pool.wait_ge(sem(f"comb{f}"), t - 3)
                for c in range(CHOICES):
                    pool.indirect_dma_start(yg[:, t % 4, c, :], None, y_dram,
                                            bass.IndirectOffsetOnAxis(ap=slotu[:, c, t:t + 1], axis=0)).then_inc(sem(f"yg{f}_{t % 4}"), 16)
                if f == 0 and t == 3:
                    att_rstd(0)
            if f == 0:
                att_rstd(1)

        def att_rstd(b):
            nc.gpsimd.wait_ge(sem("a_var"), b + 1)
            nc.gpsimd.tensor_tensor(rstd[:, 2 * b:2 * b + 2], varE[:, 2 * b:2 * b + 2], neghalf[:, 0:2], ALU.pow).then_inc(sem("a_rstd"), 1)

        def att_pool():
            pool = nc.gpsimd
            pool.wait_ge(sem("comb0"), NT)
            for p in range(2):
                pool.dma_start(qside[R_ALIBI:R_MAX, p], rows_q).then_inc(sem("rows_in"), 16)
                pool.dma_start(kT[R_ALIBI:ROWS, p], rows_k).then_inc(sem("rows_in"), 16)
            att_rstd(2)
            att_rstd(3)

        @block.gpsimd
        def _(pool):
            pool.memset(rw[:], 0.0).then_inc(sem("pool_set"), 1)
            pool.dma_start(cb[:], const_b).then_inc(sem("cb_in"), 16)
            pool.memset(neghalf[:], -0.5).then_inc(sem("pool_set"), 1)
            pool.wait_ge(sem("pool_set"), 2)
            ffn_pool(0)
            att_pool()
            ffn_pool(1)


        def ffn_act(f):
            act = nc.scalar
            for t in range(NT):
                act.wait_ge(sem(f"xt{f}"), t + 1)
                act.copy(xnT[:, t].rearrange("p c q -> p (c q)"), ps[:, PS_XT + t % 2, :]).then_inc(sem(f"xnT{f}"), 1)
            act.wait_ge(sem(f"lt{f}"), 1)
            act.copy(lgT[:], ps[:, PS_XT, 0:2 * P]).then_inc(sem(f"lgT{f}"), 1)
            act.wait_ge(sem(f"lg{f}"), 1)
            act.activation(t16[:].rearrange("p t e -> p (t e)"), lg[:].rearrange("p t e -> p (t e)"), ACT.Exp).then_inc(sem(f"rexp{f}"), 1)
            def shared(first, last):
                for t in range(first, last + 1):
                    if t > first:
                        act.wait_ge(sem(f"s_ht{f}"), t)
                        act.copy(hT[:, (t - 1) % 2, :], ps[:, PS_HT, SHARED * ((t - 1) % 2):SHARED * ((t - 1) % 2 + 1)]).then_inc(sem(f"s_hT{f}"), 1)
                    if t == 4 and first == 0:
                        for n in range(2):
                            act.wait_ge(sem(f"gt{f}"), n + 1)
                            act.copy(gateT[:, 4 * n:4 * n + 4, :].rearrange("e t q -> e (t q)"), ps[0:E + 1, PS_XT + n, :]).then_inc(sem(f"gateT{f}"), 1)
                    if t < last:
                        act.wait_ge(sem(f"s_gu{f}"), t + 1)
                        act.activation(sg[:, t % 2, :], ps[:, PS_GU + t % 2, 0:SHARED], ACT.Silu).then_inc(sem(f"s_silu{f}"), 1)

            shared(0, FIRST)

            def gather_copy(j, par):
                act.wait_ge(sem(f"xgt{f}"), j + 1)
                act.copy(xgT[:, par].rearrange("p c q -> p (c q)"), ps[:, PS_XT + par, :]).then_inc(sem(f"xgT{f}"), 1)

            def silu(j, par):
                act.wait_ge(sem(f"gu{f}"), j + 1)
                act.activation(sg[:, par, 0:INTER], ps[:, PS_GU + par, 0:INTER], ACT.Silu).then_inc(sem(f"silu{f}"), 1)

            def h_copy(j, par):
                act.wait_ge(sem(f"ht{f}"), j + 1)
                act.copy(hT[:, par, 0:INTER], ps[:, PS_HT, P * par:P * par + P]).then_inc(sem(f"hT{f}"), 1)

            def body(j, par):
                h_copy(j - 1, 1 - par)
                silu(j, par)
                gather_copy(j + 1, 1 - par)
            act.wait_ge(sem(f"jex{f}"), 1)
            pairs = act.value_load(jm[:], min_val=JOBS_LEAST // 2, max_val=JOBS // 2)
            gather_copy(0, 0)
            silu(0, 0)
            gather_copy(1, 1)
            with act.Fori(0, pairs) as i:
                body(2 * i + 1, 1)
                body(2 * i + 2, 0)
            h_copy(2 * pairs, 0)
            shared(FIRST, NT)

        def att_act():
            act = nc.scalar

            def xa_copy(b, chunks):
                if b >= 3:
                    act.wait_ge(sem("a_wo"), QT * (b - 2))
                for c in chunks:
                    act.wait_ge(sem("a_xt"), 4 * b + c + 1)
                    act.copy(xaT[:, :, (c // 2) * P:(c // 2 + 1) * P][:, 2 * (c % 2):2 * (c % 2) + 2, :],
                             ps[:, PS_ST + c % 4, 0:2 * P].rearrange("p (c q) -> p c q", c=2)).then_inc(sem("a_xaT"), 1)

            def qkv_copy(b):
                if b >= 1:
                    act.wait_ge(sem(f"q_out{(b - 1) % 2}"), Q_OUTS * ((b - 1) // 2 + 1))
                for c in Q_ORDER:
                    if c is None:
                        act.wait_ge(sem("a_k"), b + 1)
                        act.mul(kp[:, 0, :], ps[0:HD, kv_bank(b), 0:SEQ], HD ** -0.5)
                        act.copy(kvT[:], ps[0:2 * HD, kv_bank(b), 0:SEQ]).then_inc(sem("kvT"), 1)
                    else:
                        act.wait_ge(sem("a_q"), KC * b + c + 1)
                        act.copy(qp[:, 0, c, :], ps[:, PS_ST + c, 0:SEQ]).then_inc(sem("q1"), 1)

            def out_proj(b):
                for q in range(QT):
                    act.wait_ge(sem("a_at"), QT * b + q + 1)
                    if q == 0 and b >= 1:
                        act.wait_ge(sem("a_wo"), QT * b - 1)
                    act.copy(aT[q].rearrange("p c q -> p (c q)"), ps[:, AT_BANK[q], :]).then_inc(sem("a_aT"), 1)

            def outputs(n):
                act.wait_ge(sem("pv"), n + 1)
                if not (type(n) is int and n < 1):
                    act.wait_ge(sem("ot"), n)
                act.copy(oT[:], ps[:, PS_O, 0:SEQ]).then_inc(sem("oT"), 1)

            def quad(b, q, par, lag):
                n = 8 * b + q
                if not (type(n) is int and n < 2):
                    act.wait_ge(sem("pv"), n - 1)
                act.wait_ge(sem("st_done"), 2 * n + 1)
                act.activation(pr[:, par, 0, :], ps[:, PS_ST:PS_ST + 2, :].rearrange("p a b -> p (a b)")[:, 0:768], ACT.Exp).then_inc(sem("exp"), 1)
                if lag:
                    outputs(n - 1)
                act.wait_ge(sem("st_done"), 2 * n + 2)
                act.activation(pr[:, par, 1, :], ps[:, PS_ST + 2:PS_ST + 4, :].rearrange("p a b -> p (a b)")[:, 0:768], ACT.Exp).then_inc(sem("exp"), 1)

            for b in range(2):
                xa_copy(b, range(4))
                qkv_copy(b)
            act.activation(mark[:, 0:1], neghalf[:, 0:1], ACT.Exp)
            for b in range(BATCH):
                nb = min(b + 1, BATCH - 1)
                act.wait_ge(sem(f"q_out{nb % 2}"), Q_OUTS * (nb // 2 + 1))
                quad(b, 0, 0, False)
                quad(b, 1, 1, True)
                with act.Fori(1, HEADS // 8) as i:
                    for par in range(2):
                        quad(b, 2 * i + par, par, True)
                if b + 2 < BATCH:
                    xa_copy(b + 2, (0, 1))
                outputs(8 * b + 7)
                if b + 2 < BATCH:
                    xa_copy(b + 2, (2, 3))
                    qkv_copy(b + 2)
                out_proj(b)

        @block.scalar
        def _(act):
            act.wait_ge(sem("x_in2"), 16)
            act.dma_start(sw12[:, :, 0:SHARED], sw1.rearrange("(c p) f -> p c f", p=P)).then_inc(sem("sw_in"), 16)
            act.dma_start(sw12[:, :, SHARED:], sw2.rearrange("(c p) f -> p c f", p=P)).then_inc(sem("sw_in"), 16)
            act.dma_start(sw3s[:], sw3.rearrange("(c p) d -> p c d", p=P)).then_inc(sem("sw_in"), 16)
            experts_in(act, 0, 0)
            ffn_act(0)
            att_act()
            ffn_act(1)


        def ln_sums(tiles):
            dve = nc.vector
            dve.wait_ge(sem(f"x_in{tiles[0] // 2}"), 16)
            for t in tiles:
                ins = dve.bn_stats(st[:, t, :], x[:, t, :])
            if tiles[-1] in (LN[0][0][-1], LN[0][1][-1]):
                ins.then_inc(sem("ln"), 1)

        def ln_stats(f, n):
            dve = nc.vector
            tiles = LN[f][n]
            if f == 0:
                dve.wait_ge(sem("ln"), 2 * n + 1)
            else:
                dve.wait_ge(sem("stats"), tiles[-1] + 1)
            for t in tiles:
                ins = dve.bn_aggr(mv[:, t, :], st[:, t, :])
            ins.then_inc(sem("ln"), 1)
            dve.wait_ge(sem("ln"), 2 * n + 2 if f == 0 else 5 + n)
            at = slice(tiles[0], tiles[-1] + 1)
            dve.tensor_scalar(varE[:, at], mv[:, at, 1], EPS, None, ALU.add).then_inc(sem(f"var{f}"), 1)

        def ln_rows(f, t):
            dve = nc.vector
            dve.wait_ge(sem(f"rstd{f}"), 1 if t in LN[f][0] else 2)
            dve.tensor_scalar(xn[:, t, :], x[:, t, :], mv[:, t, 0:1], rstd[:, t:t + 1],
                              ALU.subtract, ALU.mult).then_inc(sem(f"xn{f}"), 1)

        def ffn_dve(f):
            dve = nc.vector
            count = [0]
            chain = sem(f"chain{f}")

            def link(ins):
                count[0] += 1
                ins.then_inc(chain, 1)
                dve.wait_ge(chain, count[0])

            if f == 0:
                ln_sums((0, 1))
                ln_sums((2, 3))
                ln_stats(0, 0)
                ln_sums((4, 5))
                ln_rows(0, 0)
                ln_rows(0, 1)
                ln_sums((6, 7))
                ln_stats(0, 1)
                for t in range(2, NT):
                    ln_rows(0, t)
            else:
                ln_stats(1, 1)
                for t in LN[1][1]:
                    ln_rows(1, t)

            def logits():
                if f == 0:
                    dve.wait_ge(sem("small_in"), 96)
                dve.wait_ge(sem(f"logit{f}"), 1)
                link(dve.tensor_tensor(lg[:].rearrange("p (j c) e -> p j c e", c=2), ps_logit,
                                       bc(rbc[:, 0:1, None, :], [P, NT // 2, 2, E]), ALU.add))
                link(dve.tensor_reduce(red[:], lg[:], AX_X, ALU.max))
                dve.tensor_tensor(lg[:], lg[:], bc(red[:, :, None], [P, NT, E]), ALU.subtract).then_inc(sem(f"lg{f}"), 1)

            def scores():
                dve.wait_ge(sem(f"rexp{f}"), 1)
                link(dve.tensor_reduce(red[:], t16[:], AX_X, ALU.add))
                link(dve.reciprocal(red[:], red[:]))
                link(dve.tensor_tensor(t16[:], t16[:], bc(red[:, :, None], [P, NT, E]), ALU.mult))
                link(dve.tensor_tensor(sc[:], t16[:], bc(rbc[:, 1:2, :], [P, NT, E]), ALU.add))

            def groups():
                link(dve.memset(gm8[:], -3e38))
                link(dve.tensor_reduce(gm8[:, :, 0:GROUPS], sc[:].rearrange("p t (g j) -> p t g j", g=GROUPS), AX_X, ALU.max))
                for t in range(NT):
                    ins = dve.max(gtop[:, t, :], gm8[:, t, :])
                link(ins)
                for t in range(NT):
                    ins = dve.max_index(gidx[:, t, :], gtop[:, t, :], gm8[:, t, :])
                link(ins)
                link(dve.tensor_copy(idxf[:], gidx[:, :, 0:2]))
                iota4 = bc(iota[:, None, 0:GROUPS], [P, NT, GROUPS])
                dve.tensor_tensor(keep[:], iota4, bc(idxf[:, :, 0:1], [P, NT, GROUPS]), ALU.is_equal)
                link(dve.tensor_tensor(keep2[:], iota4, bc(idxf[:, :, 1:2], [P, NT, GROUPS]), ALU.is_equal))
                link(dve.tensor_tensor(keep[:], keep[:], keep2[:], ALU.add))
                link(dve.tensor_scalar(keep[:], keep[:], -NEG, NEG, ALU.mult, ALU.add))
                link(dve.tensor_tensor(t16[:].rearrange("p t (g j) -> p t g j", g=GROUPS),
                                       sc[:].rearrange("p t (g j) -> p t g j", g=GROUPS),
                                       bc(keep[:, :, :, None], [P, NT, GROUPS, E // GROUPS]), ALU.add))

            def experts():
                for t in range(NT):
                    ins = dve.max(etop[:, t, :], t16[:, t, :])
                link(ins)
                for t in range(NT):
                    ins = dve.max_index(eidx[:, t, :], etop[:, t, :], t16[:, t, :])
                link(ins)
                link(dve.tensor_copy(idxf[:], eidx[:, :, 0:2]))
                dve.tensor_scalar(hv[:], etop[:, :, 0:CHOICES], 0.5, None, ALU.mult)
                iota16 = bc(iota[:, None, 0:E], [P, NT, E])
                dve.tensor_tensor(oh[:, 0], iota16, bc(idxf[:, :, 0:1], [P, NT, E]), ALU.is_equal)
                link(dve.tensor_tensor(oh[:, 1], iota16, bc(idxf[:, :, 1:2], [P, NT, E]), ALU.is_equal))
                dve.tensor_tensor(taken[:], oh[:, 0], oh[:, 1], ALU.add).then_inc(sem(f"taken{f}"), 1)

            def gates():
                dve.memset(gate[:], 1.0)
                dve.tensor_tensor(t16[:], oh[:, 1], bc(etop[:, :, 1:2], [P, NT, E]), ALU.mult)
                link(dve.tensor_tensor(lg[:], oh[:, 0], bc(etop[:, :, 0:1], [P, NT, E]), ALU.mult))
                dve.tensor_tensor(gate[:, :, 0:E], lg[:], t16[:], ALU.add).then_inc(sem(f"gate{f}"), 1)

            def slots(between):
                dve.wait_ge(sem(f"rank{f}"), 1)
                link(dve.tensor_scalar(cnti[:], ps_count, float(P - 1), None, ALU.add))
                link(dve.tensor_scalar(cnti[:], cnti[:], P.bit_length() - 1, None, ALU.arith_shift_right))
                link(dve.tensor_copy(cnt[:, 0, :], cnti[:]))
                link(dve.tensor_copy(cnt[:, 1, :], cnti[:]))
                a, b, s = 1, 2, 1
                while s < E:
                    dve.tensor_copy(cnt[:, b, 0:s], cnt[:, a, 0:s])
                    link(dve.tensor_tensor(cnt[:, b, s:], cnt[:, a, s:], cnt[:, a, 0:E - s], ALU.add))
                    a, b, s = b, a, 2 * s
                end = cnt[0:1, a, :]
                link(dve.tensor_copy(jm[:], end[:, E - 1:E]))
                link(dve.tensor_scalar(jm[:], jm[:], 1, None, ALU.arith_shift_right))
                link(dve.tensor_tensor(jcmp[:], bc(end[:, None, :], [1, JP, E]), bc(iota[0:1, 0:JP, None], [1, JP, E]), ALU.is_le))
                link(dve.tensor_reduce(jexf[:], jcmp[:], AX_X, ALU.add))
                dve.tensor_scalar(jex[:], jexf[:], float(E - 1), None, ALU.min).then_inc(sem(f"jex{f}"), 1)
                link(dve.tensor_tensor(cnt[:, 3, :], cnt[:, a, :], cnt[:, 0, :], ALU.subtract))
                link(dve.tensor_scalar(cnt[:, 3, :], cnt[:, 3, :], float(P), None, ALU.mult))
                link(dve.tensor_tensor(t16[:], ps_rank, bc(cnt[:, 3:4, :], [P, NT, E]), ALU.add))
                for c in range(CHOICES):
                    ins = dve.tensor_tensor(oh[:, c], oh[:, c], t16[:], ALU.mult)
                link(ins)
                link(dve.tensor_reduce(slot[:].rearrange("p c t -> p (c t)"), oh[:].rearrange("p c t e -> p (c t) e"), AX_X, ALU.add))
                dve.tensor_copy(slotu[:], slot[:])
                link(dve.tensor_copy(sloti[:], slot[:]))
                si = sloti[:].rearrange("p c t -> p (c t)")
                dve.tensor_scalar(sji[:, 0, :], si, P.bit_length() - 1, None, ALU.arith_shift_right)
                link(dve.tensor_scalar(sji[:, 1, :], si, P - 1, None, ALU.bitwise_and))
                link(dve.tensor_copy(sjf[:], sji[:]))
                between()
                n = CHOICES * NT
                dve.tensor_tensor(onehot_p[:], bc(iota[:, None, :], [P, n, P]), bc(sjf[:, 1, :, None], [P, n, P]), ALU.is_equal)
                link(dve.tensor_tensor(onehot_j[:, :, 1, :], bc(iota[:, None, 0:JP], [P, n, JP]), bc(sjf[:, 0, :, None], [P, n, JP]), ALU.is_equal))
                link(dve.tensor_scalar(onehot_j[:, :, 0, :], onehot_j[:, :, 1, :], cf[:, C_PIDX:C_PIDX + 1], None, ALU.mult))
                dve.tensor_tensor(onehot_j[:, :, 1, :], onehot_j[:, :, 1, :], bc(cf[:, C_TILE:C_TILE + n, None], [P, n, JP]),
                                  ALU.mult).then_inc(sem(f"onehot{f}"), 1)

            def token_list():
                dve.wait_ge(sem(f"listed{f}"), 1)
                link(dve.tensor_copy(listf[:], ps_list[:, 0:JP]))
                dve.tensor_tensor(listu[:], listf[:], ps_list[:, JP:], ALU.add).then_inc(sem(f"list{f}"), 1)

            def shared_h(t):
                dve.wait_ge(sem(f"s_silu{f}"), t + 1)
                dve.tensor_tensor(hh[:, t % 2, :], ps[:, PS_GU + t % 2, SHARED:], sg[:, t % 2, :], ALU.mult).then_inc(sem(f"s_h{f}"), 1)

            def shared_x(t):
                dve.wait_ge(sem(f"s_z{f}"), t + 1)
                dve.scalar_tensor_tensor(out=x[:, t, :], in0=ps[:, PS_Y + t % 2, :], scalar=0.5, in1=x[:, t, :],
                                         op0=ALU.mult, op1=ALU.add).then_inc(sem(f"s_x{f}"), 1)

            def pairs_x(t):
                dve.wait_ge(sem(f"yg{f}_{t % 4}"), 32 * (t // 4 + 1))
                dve.wait_ge(sem(f"biased{f}" if t < BIASED else f"s_x{f}"), t + 1)
                link(dve.scalar_tensor_tensor(out=x[:, t, :], in0=yg[:, t % 4, 0, :], scalar=hv[:, t, 0:1], in1=x[:, t, :],
                                              op0=ALU.mult, op1=ALU.add))
                dve.scalar_tensor_tensor(out=x[:, t, :], in0=yg[:, t % 4, 1, :], scalar=hv[:, t, 1:2], in1=x[:, t, :],
                                         op0=ALU.mult, op1=ALU.add).then_inc(sem(f"comb{f}"), 1)

            def biases_x(t):
                dve.wait_ge(sem(f"c{f}"), t + 1)
                dve.wait_ge(sem(f"s_x{f}"), t + 1)
                dve.scalar_tensor_tensor(out=x[:, t, :], in0=ps[:, PS_XT + t % 3, :], scalar=0.5, in1=x[:, t, :],
                                         op0=ALU.mult, op1=ALU.add).then_inc(sem(f"biased{f}"), 1)

            logits()
            shared_h(0)
            scores()
            groups()
            shared_h(1)
            shared_x(0)
            experts()
            shared_h(2)
            shared_x(1)
            gates()
            shared_h(3)
            shared_x(2)
            slots(lambda: (shared_h(4), shared_x(3)))
            shared_h(5)
            shared_x(4)
            token_list()
            shared_x(5)

            def gated(j, par):
                dve.wait_ge(sem(f"silu{f}"), j + 1)
                dve.tensor_tensor(hh[:, par, 0:INTER], ps[:, PS_GU + par, INTER:2 * INTER], sg[:, par, 0:INTER], ALU.mult).then_inc(sem(f"h{f}"), 1)

            def rows_out(j, par, first=False):
                dve.wait_ge(sem(f"y{f}"), j + 1)
                if not first:
                    dve.wait_ge(sem(f"y_out{f}_{par}"), first_stores(j, par))
                dve.tensor_copy(ysb[:, par, :], ps[:, PS_Y + par, :]).then_inc(sem(f"y_sb{f}"), 1)

            def first_stores(j, par):
                return 8 * (j - par)

            gated(0, 0)
            gated(1, 1)
            rows_out(0, 0, first=True)
            gated(2, 0)
            rows_out(1, 1, first=True)
            dve.wait_ge(sem(f"jex{f}"), 1)
            pairs = dve.value_load(jm[:], min_val=JOBS_LEAST // 2, max_val=JOBS // 2)
            with dve.Fori(0, pairs - 1) as i:
                gated(2 * i + 3, 1)
                rows_out(2 * i + 2, 0)
                gated(2 * i + 4, 0)
                rows_out(2 * i + 3, 1)
            rows_out(2 * pairs, 0)
            biases_x(0)
            biases_x(1)
            dve.wait_ge(sem(f"y_out{f}_1"), 16 * pairs)
            dve.tensor_copy(mark[:, 1:2], neghalf[:, 0:1]).then_inc(sem(f"y_all{f}"), 1)
            dve.wait_ge(sem(f"y_out{f}_0"), 16 * pairs + 16)
            dve.tensor_copy(mark[:, 0:1], neghalf[:, 0:1]).then_inc(sem(f"y_all{f}"), 1)
            biases_x(2)
            pairs_x(0)
            shared_h(6)
            pairs_x(1)
            biases_x(3)
            if f == 0:
                att_stats(0)
            shared_h(7)
            pairs_x(2)
            biases_x(4)
            shared_x(6)
            pairs_x(3)
            if f == 0:
                att_norm(0)
            shared_x(7)
            if f == 0:
                att_stats(1)
            for t in range(4, NT - QT if f == 0 else NT):
                pairs_x(t)
            return pairs_x


        chain_a = [0]

        def link_a(ins):
            chain_a[0] += 1
            ins.then_inc(sem("chain_a"), 1)
            nc.vector.wait_ge(sem("chain_a"), chain_a[0])

        def att_stats(b):
            dve = nc.vector
            dve.wait_ge(sem("comb0"), 2 * b + 2)
            dve.bn_stats(st[:, 2 * b, :], x[:, 2 * b, :])
            link_a(dve.bn_stats(st[:, 2 * b + 1, :], x[:, 2 * b + 1, :]))
            dve.bn_aggr(mv[:, 2 * b, :], st[:, 2 * b, :])
            link_a(dve.bn_aggr(mv[:, 2 * b + 1, :], st[:, 2 * b + 1, :]))
            dve.tensor_scalar(varE[:, 2 * b:2 * b + 2], mv[:, 2 * b:2 * b + 2, 1], EPS, None, ALU.add).then_inc(sem("a_var"), 1)

        def att_norm(b):
            dve = nc.vector
            dve.wait_ge(sem("a_rstd"), b + 1)
            if b >= 1:
                dve.wait_ge(sem("a_xt"), 4 * b)
            for q in range(QT):
                t = QT * b + q
                dve.tensor_scalar(xa[:, q, :], x[:, t, :], mv[:, t, 0:1], rstd[:, t:t + 1],
                                  ALU.subtract, ALU.mult).then_inc(sem("a_xn"), 1)

        def att_dve(pairs_x):
            dve = nc.vector
            link = link_a

            link(dve.memset(vv[:], 0.0))
            dve.memset(nm[:], 0.0)
            link(dve.memset(vv[:, :, :, HD:HD + 1], 1.0))

            def parts(b, chunks):
                for c in chunks:
                    if c is None:
                        dve.wait_ge(sem("kvT"), b + 1)
                        dve.wait_ge(sem("q_parts"), 3 * (KC * b + 2))
                        link(dve.scalar_tensor_tensor(out=kr[:], in0=kvT[0:HD, :], scalar=HD ** -0.5, in1=kp[:, 0, :],
                                                      op0=ALU.mult, op1=ALU.subtract))
                        link(dve.tensor_copy(kp[:, 1, :], kr[:]))
                        dve.tensor_tensor(kp[:, 2, :], kr[:], kp[:, 1, :], ALU.subtract).then_inc(sem("k_parts"), 3)
                        dve.wait_ge(sem("k_parts"), 3 * (b + 1))
                    else:
                        dve.wait_ge(sem("q1"), KC * b + c + 1)
                        dve.wait_ge(sem("q_parts"), 3 * (KC * b + c))
                        link(dve.tensor_tensor(qr[:], ps[:, PS_ST + c, 0:SEQ], qp[:, 0, c, :], ALU.subtract))
                        link(dve.tensor_copy(qp[:, 1, c, :], qr[:]))
                        dve.tensor_tensor(qp[:, 2, c, :], qr[:], qp[:, 1, c, :], ALU.subtract).then_inc(sem("q_parts"), 3)
                    if c == 2:
                        dve.wait_ge(sem("a_v"), b + 1)
                        dve.tensor_copy(vv[:, b % 2, :, 0:HD], ps[:, kv_bank(b) + 1, 0:QT * 2 * HD].rearrange("p (t d) -> p t d", t=QT)[:, :, HD:]).then_inc(sem("v_in"), 1)

            def head_maxima(b, h, bank):
                dve.wait_ge(sem("s_done"), HEADS * b + h + 1)
                dve.tensor_reduce(m3[:, ds(h, 1), :], ps[:, PS_S + bank, 0:3 * P].rearrange("p (n k) -> p n k", n=3),
                                  AX_X, ALU.max).then_inc(sem("s_max"), 1)

            def maxima(b, half=None):
                hs = slice(0, HEADS) if half is None else slice(half * HEADS // 2, (half + 1) * HEADS // 2)
                turned = b + 2 if half is None else half + 1
                dve.wait_ge(sem("s_max"), HEADS * b + hs.stop)
                link(dve.tensor_tensor(m3[:, hs, 1], m3[:, hs, 1], m3[:, hs, 2], ALU.max))
                dve.tensor_scalar(nm[:, 0, hs], m3[:, hs, 0], -1.0, None, ALU.mult)
                dve.tensor_scalar(nm[:, 1, hs], m3[:, hs, 1], -1.0, None, ALU.mult).then_inc(sem("m_nm"), 1)
                dve.wait_ge(sem("m_t"), turned)
                if half == 1:
                    dve.wait_ge(sem("m_out0"), 32)
                if b >= 1:
                    dve.wait_ge(sem(f"m_out{(b - 1) % 2}"), m_outs(b - 1))
                src = ps[0:QT * HEADS, PS_S if half is None else PS_A, 0:P]
                link(dve.tensor_copy(mp[:, 0, :], src))
                link(dve.tensor_tensor(mr[:], src, mp[:, 0, :], ALU.subtract))
                link(dve.tensor_copy(mp[:, 1, :], mr[:]))
                dve.tensor_tensor(mp[:, 2, :], mr[:], mp[:, 1, :], ALU.subtract).then_inc(sem("m_parts"), 3)

            def normalise(n, q):
                o = ps[:, PS_A, 0:QT * P].rearrange("p (t h d) -> p t h d", t=QT, h=4)
                dve.wait_ge(sem("ot"), n + 1)
                dve.reciprocal(rec[:], o[:, :, :, HD]).then_inc(sem("a_rec"), 1)
                dve.wait_ge(sem("a_rec"), n + 1)
                dve.tensor_tensor(attn[:, :, ds(q * 4 * HD, 4 * HD)].rearrange("p t (h d) -> p t h d", h=4), o[:, :, :, 0:HD],
                                  bc(rec[:, :, :, None], [P, QT, 4, HD]), ALU.mult).then_inc(sem("normed"), 1)

            def quad(b, q):
                if b + 1 < BATCH:
                    for h in range(4):
                        head_maxima(b + 1, 4 * q + h, h % 2)
                normalise(8 * b + q, q)

            def row_stats(b):
                for t in range(QT * b, QT * (b + 1)):
                    dve.wait_ge(sem("att_x"), t + 1)
                    dve.bn_stats(st[:, t, :], x[:, t, :]).then_inc(sem("stats"), 1)

            att_norm(1)
            parts(0, Q_ORDER[0:1])
            pairs_x(NT - 2)
            parts(0, Q_ORDER[1:3])
            pairs_x(NT - 1)
            parts(0, Q_ORDER[3:])
            parts(1, Q_ORDER[0:1])
            def first_maxima(heads):
                for h in heads:
                    head_maxima(0, h, h % 3)
            first_maxima(range(0, 10))
            parts(1, Q_ORDER[1:2])
            first_maxima(range(10, 16))
            maxima(0, 0)
            parts(1, Q_ORDER[2:3])
            first_maxima(range(16, 20))
            parts(1, Q_ORDER[3:4])
            first_maxima(range(20, 28))
            parts(1, Q_ORDER[4:5])
            first_maxima(range(28, 32))
            maxima(0, 1)
            for b in range(BATCH):
                if b >= 1:
                    dve.wait_ge(sem("a_at"), QT * b)
                if b >= 1:
                    row_stats(b - 1)
                quad(b, 0)
                if b + 2 < BATCH:
                    att_stats(b + 2)
                if b + 1 == BATCH:
                    dve.wait_ge(sem("st_done"), HEADS // 2 * b)
                    ln_stats(1, 0)
                    for q in range(1, HEADS // 4 - 1):
                        quad(b, q)
                        ln_rows(1, q - 1)
                else:
                    for q in range(1, HEADS // 4 - 1):
                        quad(b, q)
                    if b + 2 < BATCH:
                        att_norm(b + 2)
                quad(b, HEADS // 4 - 1)
                if b + 1 < BATCH:
                    maxima(b + 1)
                if b + 2 < BATCH:
                    parts(b + 2, Q_ORDER)
                for q in range(QT):
                    t = QT * b + q
                    dve.wait_ge(sem("a_wo"), t + 1)
                    dve.tensor_tensor(x[:, t, :], ps[:, WO_BANK[q], :], x[:, t, :], ALU.add).then_inc(sem("att_x"), 1)
            row_stats(BATCH - 1)

        @block.vector
        def _(dve):
            att_dve(ffn_dve(0))
            ffn_dve(1)


        def ffn_pe(f):
            pe = nc.tensor

            for t in range(NT):
                if f == 1 and t == 1:
                    pe.wait_ge(sem("att_x"), NT - 1)
                pe.wait_ge(sem(f"xn{f}"), t + 1)
                if t >= 2:
                    pe.wait_ge(sem(f"xnT{f}"), t - 1)
                for c in range(KC):
                    ins = pe.transpose(ps[:, PS_XT + t % 2, c * P:(c + 1) * P], xn[:, t, c * P:(c + 1) * P], ident)
                ins.then_inc(sem(f"xt{f}"), 1)
            pe.wait_ge(sem(f"xnT{f}"), NT)
            for c in range(KC):
                for j in range(NT // 2):
                    for t in range(2):
                        ins = pe.matmul(ps[32 * j:32 * j + 32, PS_XT, t * P:(t + 1) * P], rw[:, c, :], xnT[:, 2 * j + t, c, :],
                                        start=(c == 0 and t == 0), stop=(c == KC - 1), skip_group_check=True)
            ins.then_inc(sem(f"lt{f}"), 1)
            if f == 1:
                pe.wait_ge(sem("sw_in"), 48 + 32)
            if f == 0:
                pe.wait_ge(sem("sw_in"), 48)
                pe.wait_ge(sem("bias_out"), 32)
                pe.wait_ge(sem("cb_in"), 16)

            def logits():
                pe.wait_ge(sem(f"lgT{f}"), 1)
                for t in range(2):
                    ins = pe.transpose(ps[:, PS_MISC, t * P:(t + 1) * P], lgT[:, t * P:(t + 1) * P], ident)
                ins.then_inc(sem(f"logit{f}"), 1)

            def shared_up(t, chunks):
                o = ps[:, PS_GU + t % 2, :]
                if 0 in chunks:
                    if t >= 2:
                        pe.wait_ge(sem(f"s_h{f}"), t - 1)
                    pe.matmul(o, ones[0:3, :], b12x[:, E * 2 * INTER:], start=True, stop=False)
                for c in chunks:
                    ins = pe.matmul(o, xnT[:, t, c, :], sw12[:, c, :], start=False, stop=(c == KC - 1))
                if KC - 1 in chunks:
                    ins.then_inc(sem(f"s_gu{f}"), 1)

            def shared_turn(t):
                pe.wait_ge(sem(f"s_h{f}"), t + 1)
                if t >= 2:
                    pe.wait_ge(sem(f"s_hT{f}"), t - 1)
                for c in range(SHARED // P):
                    ins = pe.transpose(ps[:, PS_HT, (t % 2) * SHARED + c * P:(t % 2) * SHARED + (c + 1) * P],
                                       hh[:, t % 2, c * P:(c + 1) * P], ident)
                ins.then_inc(sem(f"s_ht{f}"), 1)

            def shared_down(t):
                pe.wait_ge(sem(f"s_hT{f}"), t + 1)
                if t >= 2:
                    pe.wait_ge(sem(f"s_x{f}"), t - 1)
                own = t >= BIASED
                for c in range(SHARED // P):
                    ins = pe.matmul(ps[:, PS_Y + t % 2, :], hT[:, t % 2, c * P:(c + 1) * P], sw3s[:, c, :],
                                    start=(c == 0), stop=(c == SHARED // P - 1 and not own))
                if own:
                    pe.wait_ge(sem(f"gateT{f}"), 2)
                    ins = pe.matmul(ps[:, PS_Y + t % 2, :], gateT[:, t, :], eb3x, start=False, stop=True)
                ins.then_inc(sem(f"s_z{f}"), 1)

            def ranks():
                pe.wait_ge(sem(f"taken{f}"), 1)
                pe.matmul(ps_rank, upper, taken[:], start=True, stop=True)
                for t in range(NT - 1):
                    n = NT - 1 - t
                    pe.matmul(ps_rank[:, t + 1:, :], ones, bc(taken[:, t:t + 1, :], [P, n, E]), start=False, stop=True,
                              skip_group_check=True)
                for t in range(NT):
                    ins = pe.matmul(ps_count, ones, taken[:, t, :], start=(t == 0), stop=(t == NT - 1))
                ins.then_inc(sem(f"rank{f}"), 1)

            def listing():
                pe.wait_ge(sem(f"onehot{f}"), 1)
                n = CHOICES * NT
                for k in range(n):
                    ins = pe.matmul(ps_list, onehot_p[:, k, :], onehot_j[:, k].rearrange("p a j -> p (a j)"),
                                    start=(k == 0), stop=(k == n - 1))
                ins.then_inc(sem(f"listed{f}"), 1)

            def gates():
                pe.wait_ge(sem(f"gate{f}"), 1)
                pe.wait_ge(sem(f"lgT{f}"), 1)
                for t in range(NT):
                    ins = pe.transpose(ps[0:E + 1, PS_XT + t // 4, (t % 4) * P:(t % 4 + 1) * P], gate[:, t, :], ident)
                    if t % 4 == 3:
                        ins.then_inc(sem(f"gt{f}"), 1)

            def shared(first, last):
                for t in range(first, last + 1):
                    if t < last:
                        shared_up(t, (0, 1))
                    if t == 0:
                        logits()
                    if t > first:
                        shared_turn(t - 1)
                    if t < last:
                        shared_up(t, (2, 3))
                    if f == 1 and t == 1:
                        pe.wait_ge(sem("wo_in"), 16 + 48)
                    if t > first:
                        shared_down(t - 1)
                    if t == 3 and first == 0:
                        ranks()
                        gates()
                    if t == 5 and first == 0:
                        listing()

            shared(0, FIRST)
            if f == 0:
                pe.wait_ge(sem("ew_in"), 16 * 3 * E // EG)
            pe.wait_ge(sem(f"jex{f}"), 1)
            pe.wait_ge(sem(f"gateT{f}"), 2)
            pairs = pe.value_load(jm[:], min_val=JOBS_LEAST // 2, max_val=JOBS // 2)

            def turn(j, par, n):
                pe.wait_ge(sem(f"xg{f}_{par}"), n)
                for c in range(KC):
                    ins = pe.transpose(ps[:, PS_XT + par, c * P:(c + 1) * P], xg[:, par, c * P:(c + 1) * P], ident)
                ins.then_inc(sem(f"xgt{f}"), 1)

            def expert(j):
                return pe.value_load(jex[0:1, ds(j, 1)], min_val=0, max_val=E - 1)

            def up(j, par, e, before=None):
                pe.wait_ge(sem(f"xgT{f}"), j + 1)
                if before is not None:
                    pe.wait_ge(sem(f"h{f}"), before)
                o = ps[:, PS_GU + par, 0:2 * INTER]
                pe.matmul(o, ones[0:3, :], b12x[:, ds(e * 2 * INTER, 2 * INTER)], start=True, stop=False)
                for c in range(KC):
                    ins = pe.matmul(o, xgT[:, par, c, :], w12[:, ds(e, 1), c, :], start=False, stop=(c == KC - 1))
                ins.then_inc(sem(f"gu{f}"), 1)

            def h_turn(j, par):
                pe.wait_ge(sem(f"h{f}"), j + 1)
                pe.transpose(ps[:, PS_HT, P * par:P * par + P], hh[:, par, 0:INTER], ident).then_inc(sem(f"ht{f}"), 1)

            def down(j, par, e, before=None):
                pe.wait_ge(sem(f"hT{f}"), j + 1)
                if before is not None:
                    pe.wait_ge(sem(f"y_sb{f}"), before)
                pe.matmul(ps[:, PS_Y + par, :], hT[:, par, 0:INTER], w3[:, ds(e, 1), :], start=True, stop=True).then_inc(sem(f"y{f}"), 1)

            turn(0, 0, 16)
            pe.wait_ge(sem(f"s_h{f}"), FIRST)
            up(0, 0, expert(0))
            turn(1, 1, 16)
            h_turn(0, 0)
            up(1, 1, expert(1))
            turn(2, 0, 32)
            pe.wait_ge(sem(f"s_x{f}"), FIRST)
            down(0, 0, expert(0))
            h_turn(1, 1)
            up(2, 0, expert(2), 1)
            turn(3, 1, 32)
            down(1, 1, expert(1))

            with pe.Fori(0, pairs - 1) as i:
                e0, e1 = expert(2 * i + 2), expert(2 * i + 3)
                h_turn(2 * i + 2, 0)
                up(2 * i + 3, 1, e1, 2 * i + 2)
                turn(2 * i + 4, 0, 16 * i + 48)
                down(2 * i + 2, 0, e0, 2 * i + 1)
                e2 = expert(2 * i + 4)
                h_turn(2 * i + 3, 1)
                up(2 * i + 4, 0, e2, 2 * i + 3)
                turn(2 * i + 5, 1, 16 * i + 48)
                down(2 * i + 3, 1, e1, 2 * i + 2)
            e = expert(2 * pairs)
            h_turn(2 * pairs, 0)
            down(2 * pairs, 0, e, 2 * pairs)

            def biases(tiles):
                for t in tiles:
                    if t >= 3:
                        pe.wait_ge(sem(f"biased{f}"), t - 2)
                    pe.matmul(ps[:, PS_XT + t % 3, :], gateT[:, t, :], eb3x, start=True, stop=True).then_inc(sem(f"c{f}"), 1)

            pe.wait_ge(sem(f"xgT{f}"), 2 * pairs + 2)
            biases((0, 1))
            pe.wait_ge(sem(f"h{f}"), 2 * pairs + 1)
            pe.wait_ge(sem(f"y_sb{f}"), 2 * pairs + 1)
            shared_up(6, range(KC))
            biases((2, 3))
            shared_up(7, range(KC))
            shared_turn(6)
            biases((4,))
            shared_down(6)
            shared_turn(7)
            shared_down(7)

        def att_pe():
            pe = nc.tensor
            pe.wait_ge(sem("wqkv_in"), 16)
            pe.wait_ge(sem("biased0"), BIASED)
            pe.wait_ge(sem("s_x0"), NT)

            def xa_turn(b, chunks):
                for c in chunks:
                    q, half = c // 2, c % 2
                    pe.wait_ge(sem("a_xn"), QT * b + q + 1)
                    if b == 1:
                        pe.wait_ge(sem("q_parts"), 3 * (c + 1))
                    if b >= 2 and c % 2 == 0:
                        pe.wait_ge(sem("exp"), 16 * (b - 1) - 1 + c // 2)
                    for k in range(2):
                        ins = pe.transpose(ps[:, PS_ST + c, k * P:(k + 1) * P], xa[:, q, (2 * half + k) * P:(2 * half + k + 1) * P], ident)
                    ins.then_inc(sem("a_xt"), 1)

            def q_product(b, chunks):
                pe.wait_ge(sem("a_xaT"), 4 * (b + 1))
                for c in chunks:
                    for k in range(KC):
                        ins = pe.matmul(ps[:, PS_ST + c, 0:SEQ], wqkv[:, k, c * P:(c + 1) * P], xaT[:, k, :], start=(k == 0), stop=(k == KC - 1))
                    ins.then_inc(sem("a_q"), 1)

            def kv_product(b):
                if b == 1:
                    pe.wait_ge(sem("q_parts"), 3 * (KC + 1))
                if b >= 2:
                    pe.wait_ge(sem("m_parts"), 3 * (b + 1))
                for k in range(KC):
                    ins = pe.matmul(ps[0:2 * HD, kv_bank(b), 0:SEQ], wqkv[:, k, DIM:], xaT[:, k, :], start=(k == 0), stop=(k == KC - 1))
                ins.then_inc(sem("a_k"), 1)

            def v_turn(b):
                pe.wait_ge(sem("kvT"), b + 1)
                if b == 1:
                    pe.wait_ge(sem("q_parts"), 3 * (KC + 2))
                for q in range(QT):
                    ins = pe.transpose(ps[:, kv_bank(b) + 1, q * 2 * HD:(q + 1) * 2 * HD], kvT[:, q * P:(q + 1) * P], cf[0:2 * HD, C_ID:C_ID + 2 * HD])
                ins.then_inc(sem("a_v"), 1)

            def scores(b, h, bank, banks=2):
                n = HEADS * b + h
                if not (type(n) is int and n < banks):
                    pe.wait_ge(sem("s_max"), n + 1 - banks)
                p = b % 2
                o = ps[:, PS_S + bank, :]
                pe.matmul(o.rearrange("p (n k) -> p n k", k=P)[:, 0:3:2, :], identb, mask, start=True, stop=True)
                pe.matmul(o[:, 0:P], qside[0:R_MAX, p, ds(h, 1), 0:P], kT[0:R_MAX, p, 0:P], start=False, stop=True, skip_group_check=True)
                pe.matmul(o[:, P:3 * P], qside[0:R_MAX, p, ds(h, 1), P:2 * P], kT[0:R_MAX, p, :], start=False, stop=True,
                          skip_group_check=True).then_inc(sem("s_done"), 1)

            def scores_t(b, g, pair):
                n = 16 * b + g
                if not (type(n) is int and n < 2):
                    pe.wait_ge(sem("exp"), n - 1)
                p = b % 2
                o = ps[:, PS_ST + 2 * pair:PS_ST + 2 * pair + 2, :]
                pe.matmul(o[:, 0, :].rearrange("p (h q) -> p h q", h=2)[:, :, 0:P], identb, mask_t, start=True, stop=True)
                pe.matmul(o[:, 0, :], kT[0:ROWS, p, 0:P], qside[0:ROWS, p, ds(2 * g, 2), :], start=False, stop=True,
                          skip_group_check=True)
                pe.matmul(o[:, 1, 0:2 * P], identb, mask_t, start=True, stop=True)
                pe.matmul(o[:, 1, 0:2 * P], kT[0:ROWS, p, P:2 * P], qside[0:ROWS, p, ds(2 * g, 2), P:2 * P],
                          start=False, stop=True, skip_group_check=True).then_inc(sem("st_done"), 1)

            def weigh(b, n, par):
                pe.wait_ge(sem("exp"), 2 * n + 2)
                if not (type(n) is int and n < 1):
                    pe.wait_ge(sem("oT"), n)
                for k in range(QT):
                    for h in range(4):
                        o = ps[32 * h:32 * h + 32, PS_O, k * P:SEQ]
                        w = QT * P - k * P
                        at = k * 2 * SEQ + (h % 2) * w
                        ins = pe.matmul(o, vv[:, b % 2, k, :], pr[:, par, h // 2, at:at + w], start=(k == 0), stop=True,
                                        skip_group_check=True)
                ins.then_inc(sem("pv"), 1)

            def turn_back(n):
                pe.wait_ge(sem("oT"), n + 1)
                if not (type(n) is int and n < 1):
                    pe.wait_ge(sem("normed"), n)
                for q in range(QT):
                    ins = pe.transpose(ps[:, PS_A, q * P:(q + 1) * P], oT[:, q * P:(q + 1) * P], ident)
                ins.then_inc(sem("ot"), 1)

            def max_turn(bank, n):
                pe.wait_ge(sem("m_nm"), n)
                pe.transpose(ps[0:QT * HEADS, bank, 0:P], nm[:].rearrange("p t h -> p (t h)"), ident).then_inc(sem("m_t"), 1)

            def attn_turn(b):
                pe.wait_ge(sem("normed"), 8 * (b + 1))
                for q in range(QT):
                    if q == 1 and b + 2 < BATCH:
                        pe.wait_ge(sem("q_parts"), 3 * (KC * (b + 2) + 1))
                    for c in range(KC):
                        ins = pe.transpose(ps[:, AT_BANK[q], c * P:(c + 1) * P], attn[:, q, c * P:(c + 1) * P], ident)
                    ins.then_inc(sem("a_at"), 1)

            def out_product(b):
                if b == 0:
                    pe.wait_ge(sem("wo_in"), 16)
                for q in range(QT):
                    pe.wait_ge(sem("a_aT"), QT * b + q + 1)
                    for c in range(KC):
                        ins = pe.matmul(ps[:, WO_BANK[q], :], aT[q][:, c, :], wo[:, c, :], start=(c == 0), stop=(c == KC - 1))
                    ins.then_inc(sem("a_wo"), 1)

            xa_turn(0, range(4))
            q_product(0, (0, 1))
            kv_product(0)
            q_product(0, (2,))
            v_turn(0)
            q_product(0, (3,))
            xa_turn(1, range(4))
            q_product(1, (0,))
            pe.wait_ge(sem("rows_in"), 64)
            pe.wait_ge(sem("q_in0"), Q_INS)
            def first_scores(last_head):
                for h in range(done[0], last_head):
                    scores(0, h, h % 3, 3)
                done[0] = last_head
            done = [0]
            first_scores(8)
            q_product(1, (1,))
            first_scores(12)
            kv_product(1)
            first_scores(16)
            max_turn(PS_A, 1)
            q_product(1, (2,))
            pe.wait_ge(sem("q_late0"), Q_LATE)
            first_scores(20)
            v_turn(1)
            first_scores(24)
            q_product(1, (3,))
            first_scores(32)
            pe.wait_ge(sem("m_parts"), 3)
            max_turn(PS_A, 2)
            for b in range(BATCH):
                nxt = b + 1 < BATCH
                if nxt:
                    pe.wait_ge(sem("m_parts"), 3 * (b + 2))
                    pe.wait_ge(sem("v_in"), min(b + 2, BATCH))
                pe.wait_ge(sem("q_parts"), 3 * KC * min(b + 2, BATCH))
                pe.wait_ge(sem(f"m_in{b % 2}"), m_ins(b))

                def quad(q, par, lag, h):
                    lag_s = lag and nxt
                    if lag_s:
                        scores(b + 1, h, 0)
                    scores_t(b, 2 * q, 0)
                    if lag_s:
                        scores(b + 1, h + 1, 1)
                    if lag:
                        weigh(b, 8 * b + q - 1, 1 - par)
                    if lag_s:
                        scores(b + 1, h + 2, 0)
                    scores_t(b, 2 * q + 1, 1)
                    if lag_s:
                        scores(b + 1, h + 3, 1)
                    if lag:
                        turn_back(8 * b + q - 1)
                quad(0, 0, False, 0)
                if b >= 1:
                    pe.wait_ge(sem("att_x"), QT * b)
                if nxt:
                    pe.wait_ge(sem(f"q_in{(b + 1) % 2}"), Q_INS * ((b + 1) // 2 + 1))
                quad(1, 1, True, 0)
                if b == 0:
                    pe.wait_ge(sem("m_in1"), 32)
                if nxt:
                    pe.wait_ge(sem(f"q_late{(b + 1) % 2}"), Q_LATE * ((b + 1) // 2 + 1))
                with pe.Fori(0, HEADS // 8 - 1) as i:
                    for par in range(2):
                        quad(2 * i + 2 + par, par, True, 8 * i + 4 * par + 4)
                more = b + 2 < BATCH
                if nxt:
                    for k in range(2):
                        scores(b + 1, HEADS - 4 + k, k)
                if more:
                    xa_turn(b + 2, (0, 1))
                weigh(b, 8 * b + 7, 1)
                if nxt:
                    for k in range(2):
                        scores(b + 1, HEADS - 2 + k, k)
                if more:
                    xa_turn(b + 2, (2, 3))
                turn_back(8 * b + 7)
                if more:
                    q_product(b + 2, (0,))
                if nxt:
                    max_turn(PS_S, b + 3)
                if more:
                    q_product(b + 2, (1,))
                    kv_product(b + 2)
                    q_product(b + 2, (2,))
                    v_turn(b + 2)
                    q_product(b + 2, (3,))
                attn_turn(b)
                out_product(b)

        @block.tensor
        def _(pe):
            pe.wait_ge(sem("small_in"), 96)
            ffn_pe(0)
            att_pe()
            ffn_pe(1)


_INS = ['L0_attn_hidden_states', 'L0_attn_Wqkv', 'L0_attn_Wo', 'L0_ffn_router_w', 'L0_ffn_router_b', 'L0_ffn_router_bias',
        'L0_ffn_ew1', 'L0_ffn_eb1', 'L0_ffn_ew2', 'L0_ffn_eb2', 'L0_ffn_ew3', 'L0_ffn_eb3',
        'L0_ffn_sw1', 'L0_ffn_sb1', 'L0_ffn_sw2', 'L0_ffn_sb2', 'L0_ffn_sw3', 'L0_ffn_sb3']


def kernel(**inputs):
    import numpy as _np
    import concourse.bacc as _bacc
    from concourse import mybir as _mybir
    from concourse.bass_utils import run_bass_kernel_spmd as _run

    nc = _bacc.Bacc("TRN2", target_bir_lowering=False, num_devices=1)
    arrays, args = {}, []
    named = {name: _np.ascontiguousarray(inputs[name]) for name in _INS}
    named.update(shape_constants())
    for name, a in named.items():
        if name == 'L0_attn_hidden_states':
            a = a.reshape(TOKENS, DIM)
        arrays[f"in_{name}_dram"] = a
        args.append(nc.dram_tensor(f"in_{name}_dram", a.shape, _mybir.dt.from_np(a.dtype), kind="ExternalInput").ap())
    args.append(nc.dram_tensor("out_0_dram", (TOKENS, DIM), _mybir.dt.float32, kind="ExternalOutput").ap())
    build(nc, *args)
    r = _run(nc, [arrays], core_ids=[0])
    return r.results[0]["out_0_dram"].reshape(BATCH, SEQ, DIM)
```
